# Optimizing a Trainium2 kernel written in Bass

```python
import numpy as np
import jax
import jax.numpy as jnp

def _softmax(x, axis=-1):
    return jax.nn.softmax(x, axis=axis)

def _gelu(x):
    return jax.nn.gelu(x, approximate=True)

def _silu(x):
    return jax.nn.silu(x)

def _sigmoid(x):
    return jax.nn.sigmoid(x)

def _layernorm(x, axis=-1, eps=1e-05):
    m = jnp.mean(x, axis=axis, keepdims=True)
    v = jnp.var(x, axis=axis, keepdims=True)
    return (x - m) / jnp.sqrt(v + eps)

def _scatter_add(tgt, idx, src, axis=0):
    return tgt.at[idx].add(src)

def _segment_sum(src, seg, n):
    return jax.ops.segment_sum(src, seg, n)
kernel_name = 'mk_gnn_resnorm_d4_gnn_r8_59a43f'

def setup_inputs(seed: int=0):
    np.random.seed(seed)
    _w = jnp.asarray

    def _rec_inputs():
        import jax
        import jax.numpy as jnp
        _gk = jax.random.key(seed)
        x = -0.0003713 + 1 * jax.random.normal(jax.random.fold_in(_gk, 1), (6250, 256), jnp.float32)
        src = jax.random.randint(jax.random.fold_in(_gk, 2), (100000,), 0, 6250, jnp.int32)
        dst = jnp.minimum((6250 * jax.random.uniform(jax.random.fold_in(_gk, 3), (100000,)) ** 2.0).astype(jnp.int32), 49999)
        _o = jnp.argsort(dst, stable=True)
        src = src[_o]
        dst = dst[_o]
        edge_type_32 = jax.random.randint(jax.random.fold_in(_gk, 13), (100000,), 0, 32, jnp.int32)
        edge_weight1 = jax.random.uniform(jax.random.fold_in(_gk, 14), (100000, 1), jnp.float32, 0.0, 0.999998)
        return (x, src, dst, edge_type_32, edge_weight1)
    x, src, dst, edge_type_32, edge_weight1 = _rec_inputs()

    def _L0_gnn_setup():
        import jax, jax.numpy as jnp
        import numpy as np
        N = 6250
        E = 200000
        D = 256
        H = 256
        EPS = 1e-05

        def _gnn_layer(x, row, col, W, b, g, beta):
            n = x.shape[0]
            neigh = x[col]
            agg = jax.ops.segment_sum(neigh, row, num_segments=n)
            deg = jax.ops.segment_sum(jnp.ones((row.shape[0],), x.dtype), row, num_segments=n)
            deg = jnp.maximum(deg, 1.0)[:, None]
            h = (x + agg / deg) @ W.T + b
            mu = jnp.mean(h, axis=-1, keepdims=True)
            var = jnp.mean(jnp.square(h - mu), axis=-1, keepdims=True)
            hn = (h - mu) * jax.lax.rsqrt(var + EPS) * g + beta
            return jax.nn.silu(hn)
        key = jax.random.key(seed)
        ks = jax.random.split(key, 12)
        x = jax.random.normal(ks[0], (N, D), dtype=jnp.float32)
        edge_index = jax.random.randint(ks[1], (2, E), 0, N, dtype=jnp.int32)
        s0 = 1.0 / np.sqrt(D)
        s1 = 1.0 / np.sqrt(H)
        W0 = jax.random.uniform(ks[2], (H, D), jnp.float32, -s0, s0)
        b0 = jax.random.uniform(ks[3], (H,), jnp.float32, -s0, s0)
        g0 = jnp.ones((H,), jnp.float32)
        beta0 = jnp.zeros((H,), jnp.float32)
        W1 = jax.random.uniform(ks[4], (H, H), jnp.float32, -s1, s1)
        b1 = jax.random.uniform(ks[5], (H,), jnp.float32, -s1, s1)
        g1 = jnp.ones((H,), jnp.float32)
        beta1 = jnp.zeros((H,), jnp.float32)
        return {'x': x, 'edge_index': edge_index, 'W0': W0, 'b0': b0, 'g0': g0, 'beta0': beta0, 'W1': W1, 'b1': b1, 'g1': g1, 'beta1': beta1}
    _L0_gnn_all = _L0_gnn_setup()
    _L0_gnn_in = {k: v for k, v in _L0_gnn_all.items() if k in ('W0', 'b0', 'g0', 'beta0', 'W1', 'b1', 'g1', 'beta1')}
    del _L0_gnn_all

    def _L1_gnn_setup():
        import jax, jax.numpy as jnp
        import numpy as np
        N_NODES = 6250
        key = jax.random.key(seed)
        k1, k2, k3 = jax.random.split(key, 3)
        x = jax.random.normal(k1, (N_NODES, 256), dtype=jnp.float32)
        W = jax.random.normal(k2, (256, 256), dtype=jnp.float32) * (1.0 / np.sqrt(256))
        edge_index = jax.random.randint(k3, (2, 200000), 0, N_NODES, dtype=jnp.int64)
        return {'x': x, 'W': W, 'edge_index': edge_index}
    _L1_gnn_all = _L1_gnn_setup()
    _L1_gnn_in = {k: v for k, v in _L1_gnn_all.items() if k in ('W',)}
    del _L1_gnn_all

    def _L2_gnn_setup():
        import jax, jax.numpy as jnp
        import numpy as np
        N = 12500
        E = 200000
        IN_FEATS = 256
        OUT_FEATS = 256
        MAXK = 32

        def _maxk(x, k):
            _, idx = jax.lax.top_k(x, k)
            rows = jnp.arange(x.shape[0])[:, None]
            mask = jnp.zeros_like(x).at[rows, idx].set(1.0)
            return x * mask
        key = jax.random.key(seed)
        k1, k2, k3, k4, k5 = jax.random.split(key, 5)
        feat = jax.random.normal(k1, (N, IN_FEATS), dtype=jnp.float32)
        W_self = jax.random.normal(k2, (IN_FEATS, OUT_FEATS), dtype=jnp.float32) * (1.0 / np.sqrt(IN_FEATS))
        W_neigh = jax.random.normal(k3, (IN_FEATS, OUT_FEATS), dtype=jnp.float32) * (1.0 / np.sqrt(IN_FEATS))
        src = jax.random.randint(k4, (E,), 0, N, dtype=jnp.int64)
        dst = jax.random.randint(k5, (E,), 0, N, dtype=jnp.int64)
        return {'feat': feat, 'W_self': W_self, 'W_neigh': W_neigh, 'src': src, 'dst': dst}
    _L2_gnn_all = _L2_gnn_setup()
    _L2_gnn_in = {k: v for k, v in _L2_gnn_all.items() if k in ('W_self', 'W_neigh')}
    del _L2_gnn_all

    def _L3_gnn_setup():
        import jax, jax.numpy as jnp
        import numpy as np
        N_NODES = 2500
        N_EDGES = 40000
        IN_DIM = 256
        OUT_DIM = 256
        NUM_RELS = 32
        NUM_BASES = 8
        key = jax.random.key(seed)
        k1, k2, k3, k4, k5, k6, k7 = jax.random.split(key, 7)
        h = jax.random.normal(k1, (N_NODES, IN_DIM), dtype=jnp.float32)
        src = jax.random.randint(k2, (N_EDGES,), 0, N_NODES, dtype=jnp.int32)
        dst = jax.random.randint(k3, (N_EDGES,), 0, N_NODES, dtype=jnp.int32)
        rel_type = jax.random.randint(k4, (N_EDGES,), 0, NUM_RELS, dtype=jnp.int32)
        norm = jax.random.uniform(k5, (N_EDGES, 1), dtype=jnp.float32)
        scale_w = np.sqrt(2.0) * np.sqrt(6.0 / (IN_DIM + OUT_DIM))
        bases = jax.random.uniform(k6, (NUM_BASES, IN_DIM, OUT_DIM), dtype=jnp.float32, minval=-scale_w, maxval=scale_w)
        scale_c = np.sqrt(2.0) * np.sqrt(6.0 / (NUM_RELS + NUM_BASES))
        w_comp = jax.random.uniform(k7, (NUM_RELS, NUM_BASES), dtype=jnp.float32, minval=-scale_c, maxval=scale_c)
        return {'h': h, 'src': src, 'dst': dst, 'rel_type': rel_type, 'norm': norm, 'bases': bases, 'w_comp': w_comp}
    _L3_gnn_all = _L3_gnn_setup()
    _L3_gnn_in = {k: v for k, v in _L3_gnn_all.items() if k in ('bases', 'w_comp')}
    del _L3_gnn_all
    return {'x': x, 'src': src, 'dst': dst, 'edge_type_32': edge_type_32, 'edge_weight1': edge_weight1, 'L0_gnn_W0': _L0_gnn_in['W0'], 'L0_gnn_b0': _L0_gnn_in['b0'], 'L0_gnn_g0': _L0_gnn_in['g0'], 'L0_gnn_beta0': _L0_gnn_in['beta0'], 'L0_gnn_W1': _L0_gnn_in['W1'], 'L0_gnn_b1': _L0_gnn_in['b1'], 'L0_gnn_g1': _L0_gnn_in['g1'], 'L0_gnn_beta1': _L0_gnn_in['beta1'], 'L1_gnn_W': _L1_gnn_in['W'], 'L2_gnn_W_self': _L2_gnn_in['W_self'], 'L2_gnn_W_neigh': _L2_gnn_in['W_neigh'], 'L3_gnn_bases': _L3_gnn_in['bases'], 'L3_gnn_w_comp': _L3_gnn_in['w_comp']}

def reference(x, src, dst, edge_type_32, edge_weight1, L0_gnn_W0, L0_gnn_b0, L0_gnn_g0, L0_gnn_beta0, L0_gnn_W1, L0_gnn_b1, L0_gnn_g1, L0_gnn_beta1, L1_gnn_W, L2_gnn_W_self, L2_gnn_W_neigh, L3_gnn_bases, L3_gnn_w_comp):
    import jax
    import jax.numpy as jnp

    def _L0_gnn_ref(x, edge_index, W0, b0, g0, beta0, W1, b1, g1, beta1):
        import jax, jax.numpy as jnp
        import numpy as np
        N = 6250
        E = 200000
        D = 256
        H = 256
        EPS = 1e-05

        def _gnn_layer(x, row, col, W, b, g, beta):
            n = x.shape[0]
            neigh = x[col]
            agg = jax.ops.segment_sum(neigh, row, num_segments=n)
            deg = jax.ops.segment_sum(jnp.ones((row.shape[0],), x.dtype), row, num_segments=n)
            deg = jnp.maximum(deg, 1.0)[:, None]
            h = (x + agg / deg) @ W.T + b
            mu = jnp.mean(h, axis=-1, keepdims=True)
            var = jnp.mean(jnp.square(h - mu), axis=-1, keepdims=True)
            hn = (h - mu) * jax.lax.rsqrt(var + EPS) * g + beta
            return jax.nn.silu(hn)
        row, col = (edge_index[0], edge_index[1])
        x = _gnn_layer(x, row, col, W0, b0, g0, beta0)
        x = _gnn_layer(x, row, col, W1, b1, g1, beta1)
        return x

    def _L1_gnn_ref(x, W, edge_index):
        import jax, jax.numpy as jnp
        import numpy as np
        N_NODES = 6250
        N = x.shape[0]
        src, dst = (edge_index[0], edge_index[1])
        h = x @ W
        deg = jax.ops.segment_sum(jnp.ones_like(dst, dtype=h.dtype), dst, num_segments=N)
        deg_inv_sqrt = jnp.where(deg > 0, jax.lax.rsqrt(jnp.maximum(deg, 1)), 0.0)
        norm = deg_inv_sqrt[src] * deg_inv_sqrt[dst]
        msgs = h[src] * norm[:, None]
        out = jax.ops.segment_sum(msgs, dst, num_segments=N)
        return out

    def _L2_gnn_ref(feat, W_self, W_neigh, src, dst):
        import jax, jax.numpy as jnp
        import numpy as np
        N = 12500
        E = 200000
        IN_FEATS = 256
        OUT_FEATS = 256
        MAXK = 32

        def _maxk(x, k):
            _, idx = jax.lax.top_k(x, k)
            rows = jnp.arange(x.shape[0])[:, None]
            mask = jnp.zeros_like(x).at[rows, idx].set(1.0)
            return x * mask
        n = feat.shape[0]
        h_self = feat @ W_self
        h_neigh = feat @ W_neigh
        h_sparse = _maxk(h_neigh, MAXK)
        msg = h_sparse[src]
        summed = jax.ops.segment_sum(msg, dst, num_segments=n)
        deg = jax.ops.segment_sum(jnp.ones((src.shape[0],), dtype=feat.dtype), dst, num_segments=n)
        neigh = summed / jnp.maximum(deg, 1.0)[:, None]
        return h_self + neigh

    def _L3_gnn_ref(h, src, dst, rel_type, norm, bases, w_comp):
        import jax, jax.numpy as jnp
        import numpy as np
        N_NODES = 2500
        N_EDGES = 40000
        IN_DIM = 256
        OUT_DIM = 256
        NUM_RELS = 32
        NUM_BASES = 8
        weight = jnp.einsum('rb,bio->rio', w_comp, bases)
        xw = jnp.einsum('ni,rio->nro', h, weight)
        msg = xw[src, rel_type] * norm
        out = jax.ops.segment_sum(msg, dst, num_segments=h.shape[0])
        return jax.nn.relu(out)
    edge_index = jnp.stack([src, dst])
    x = _layernorm(x + _L0_gnn_ref(x, edge_index, L0_gnn_W0, L0_gnn_b0, L0_gnn_g0, L0_gnn_beta0, L0_gnn_W1, L0_gnn_b1, L0_gnn_g1, L0_gnn_beta1), axis=-1)
    x = _layernorm(x + _L1_gnn_ref(x, L1_gnn_W, edge_index), axis=-1)
    x = _layernorm(x + _L2_gnn_ref(x, L2_gnn_W_self, L2_gnn_W_neigh, src, dst), axis=-1)
    x = _layernorm(x + _L3_gnn_ref(x, src, dst, edge_type_32, edge_weight1, L3_gnn_bases, L3_gnn_w_comp), axis=-1)
    return x

_drawn_inputs = setup_inputs


def setup_inputs(seed=0):
    import zlib

    import numpy as np

    out = dict(_drawn_inputs(seed))
    spreads = {'L0_gnn_g0': (1.0, 0.2),
     'L0_gnn_beta0': (0.0, 0.1),
     'L0_gnn_g1': (1.0, 0.2),
     'L0_gnn_beta1': (0.0, 0.1)}
    factors = {}
    for name, (base, spread) in spreads.items():
        noise = np.random.default_rng([zlib.crc32(name.encode()), seed]).standard_normal(out[name].shape)
        drawn = base * np.exp(spread * noise) if base else spread * noise
        out[name] = jnp.asarray(drawn.astype(out[name].dtype))
    for name, factor in factors.items():
        out[name] = (out[name] * factor).astype(out[name].dtype)
    return out
```

```python
from contextlib import ExitStack

import numpy as np

import concourse.bass as bass
from concourse import mybir
from concourse.alu_op_type import AluOpType as ALU

F32 = mybir.dt.float32
BF16 = mybir.dt.bfloat16
I32 = mybir.dt.int32
I16 = mybir.dt.int16
ACT = mybir.ActivationFunctionType
AX = mybir.AxisListType

P = 128
NODES, D, EDGES = 6250, 256, 100000
RELS, BASES = 32, 8
EPS = 1e-5
TILES = -(-NODES // P)
NT = TILES + 1
LAST_ROWS = NODES - (TILES - 1) * P
LANES = 16
COLS = -(-EDGES // P // LANES) * LANES
FULL = EDGES // COLS
REST = EDGES - FULL * COLS
PAD_KEY = TILES * P
ROWS = COLS
GROUP = 4
PAIRS = -(-(ROWS + TILES - 1) // 64) * 64
GROUPS = PAIRS // GROUP
PAIR_COLS = -(-PAIRS // P)
RING = 8
OH_RING = 4
CREDIT = RING


class Chain:

    def __init__(self, eng, sem):
        self.eng, self.sem, self.base, self.n = eng, sem, 0, 0

    def __call__(self, ins):
        self.n += 1
        ins.then_inc(self.sem, 1)
        self.eng.wait_ge(self.sem, self.base + self.n)

    def loop(self, base, steps_per_turn, turn):
        self.base, self.n = base + turn * steps_per_turn, 0

    def total(self, n):
        self.base, self.n = n, 0

    def settle(self, counted):
        self.eng.sem_inc(counted, 1)


def build(nc, x, src, dst, edge_type_32, edge_weight1, L0_gnn_W0, L0_gnn_b0, L0_gnn_g0, L0_gnn_beta0,
          L0_gnn_W1, L0_gnn_b1, L0_gnn_g1, L0_gnn_beta1, L1_gnn_W, L2_gnn_W_self, L2_gnn_W_neigh,
          L3_gnn_bases, L3_gnn_w_comp, out):
    ctx = ExitStack()
    ds = bass.ds
    with ctx:
        def sb(name, shape, dt=F32):
            return ctx.enter_context(nc.sbuf_tensor(name, shape, dt))

        def dram(name, shape, dt=F32):
            return nc.dram_tensor(name, shape, dt, kind="Internal").ap()

        rec_dram = {"s": dram("rec_s", [P * COLS, 2]), "d": dram("rec_d", [P * COLS, 4])}
        table = [dram(f"table{i}", [NT * P, D]) for i in range(3)]
        rel_table = dram("rel_table", [NT * P, RELS * D])
        rel_w = dram("rel_w", [RELS, D * D])

        state = sb("state", [P, NT * D])
        work = sb("work", [P, NT * D + RING * GROUP * D])
        sums = work[:, 0:NT * D]
        ring0 = NT * D
        gathered = work[:, ring0:ring0 + RING * GROUP * D].rearrange("p (s d) -> p s d", d=D)
        onehot = sb("onehot", [P, OH_RING * GROUP, P])
        ident = sb("ident", [P, P])
        ones = sb("ones", [P, P])
        before = sb("before", [P, P])
        iota_p = sb("iota_p", [P, P])
        iota_bf = sb("iota_bf", [P, P], BF16)
        npf = PAIR_COLS * P
        loc = {"s": sb("loc_s", [P, npf]), "d": sb("loc_d", [P, npf])}
        off = {"s": sb("off_s", [P, npf], I32), "d": sb("off_d", [P, npf], I32)}
        idx_s = sb("idx_s", [P, npf], I32)
        idx_d = sb("idx_d", [P, npf], I32)
        idx_rel = sb("idx_rel", [P, npf], I32)
        weight = sb("weight", [P, npf])
        idx_ring = sb("idx_ring", [P, 4 * LANES], I32)
        w_sage = [sb("w_sage0", [P, 2, D]), sb("w_sage1", [P, 2, D])]
        w_gcn = sb("w_gcn", [P, 2, D])
        w_maxk = sb("w_maxk", [P, 2, 2 * D])
        rows6 = sb("rows6", [P, 6, D])
        b_rep = [rows6[:, 0, :], rows6[:, 3, :]]
        g_rep = [rows6[:, 1, :], rows6[:, 4, :]]
        beta_rep = [rows6[:, 2, :], rows6[:, 5, :]]
        rdeg_s = sb("rdeg_s", [P, NT])
        rdeg_d = sb("rdeg_d", [P, NT])
        dis = sb("dis", [P, NT])
        moments = sb("moments", [P, NT, 2])
        rstd = sb("rstd", [P, NT])
        stats = sb("stats", [P, 2, 6])
        stats_top = sb("stats_top", [P, 8])
        operand = sb("operand", [P, 2, D])
        operandT = sb("operandT", [P, 2, D])
        psum = ctx.enter_context(nc.psum_tensor("psum", [P, 8, 512], F32))

        tot = {k: sb(f"tot_{k}", [P, NT]) for k in "sd"}
        ends = {k: sb(f"ends_{k}", [P, NT]) for k in "sd"}
        starts = {k: sb(f"starts_{k}", [P, NT]) for k in "sd"}
        moved = sb("moved", [P, 1])
        moved_i = sb("moved_i", [P, 1], I32)
        small = sb("small", [P, 8, NT])
        small_i = sb("small_i", [P, 2, NT], I32)
        iota_t = sb("iota_t", [P, NT])
        row_i = {k: sb(f"row_{k}", [P, PAIR_COLS], I32) for k in "sd"}
        row_f = sb("row_f", [P, PAIR_COLS])

        taken = {"state": 0, "work": 0}

        def carve(where, n, dt=F32):
            a = (state if where == "state" else work)[:, taken[where]:taken[where] + n]
            taken[where] += n
            assert taken[where] <= NT * D
            return a if dt == F32 else a.bitcast(dt)

        src_i, dst_i, rel_i = (carve("state", COLS, I32) for _ in range(3))
        w_in = carve("state", COLS)
        zeros = carve("state", COLS)
        rec = {"s": carve("state", 2 * COLS).rearrange("p (t f) -> p t f", f=2),
               "d": carve("state", 4 * COLS).rearrange("p (t f) -> p t f", f=4)}
        pos_i = {"s": carve("state", COLS, I32), "d": carve("state", COLS, I32)}
        tile_i, low_i = carve("work", COLS, I32), carve("work", COLS, I32)
        key_f, edge_no = carve("work", COLS), carve("work", COLS)
        tile_f = {"s": carve("work", COLS), "d": carve("work", COLS)}
        low_f = {"s": carve("work", COLS), "d": carve("work", COLS)}
        rank, pos_f = carve("work", COLS), carve("work", COLS)
        mask = carve("work", COLS // 2, I16)
        counts = carve("work", NT)
        rank0 = carve("work", NT)
        pos_ring = carve("work", LANES, I32)
        rec_ring = carve("work", LANES * 4)
        low_hot = carve("work", 2 * 4 * P // 2, BF16).rearrange("p (h c j) -> p h c j", h=2, c=4)
        tile_hot = carve("work", 2 * 4 * NT // 2, BF16).rearrange("p (h c j) -> p h c j", h=2, c=4)
        base_ring = work[:, ring0:ring0 + 4096].rearrange("p (h n) -> p h n", h=2)
        relw_ring = work[:, ring0 + 4096:ring0 + 8192].rearrange("p (h n) -> p h n", h=2)
        w_raw = onehot[:, 0:8, :].rearrange("p s j -> p (s j)").rearrange("p (w k d) -> p w k d", w=2, k=2)
        comp_t = sb("comp_t", [BASES, RELS])
        keys = {"s": src_i, "d": dst_i}
        REC = {"s": 2, "d": 4}

        cum_off, cum_tot = psum[:, 0, 0:NT], psum[:, 0, 64:64 + NT]
        deg_ps = {"d": psum[:, 1, 0:NT], "s": psum[:, 2, 0:NT]}

        passed_dve, passed_pe, passed_pool = (
            ctx.enter_context(nc.semaphore(n)) for n in ("passed_dve", "passed_pe", "passed_pool"))
        landed = [ctx.enter_context(nc.semaphore(f"landed{g}")) for g in range(RING)]
        rows_gathered = [0]

        def sort_positions(dve, o, side, counted, cum):
            o(nc.vector.tensor_copy(key_f, keys[side]))
            o(nc.vector.tensor_scalar(tile_i, keys[side], 7, None, ALU.arith_shift_right))
            o(nc.vector.tensor_scalar(low_i, keys[side], P - 1, None, ALU.bitwise_and))
            o(nc.vector.tensor_copy(tile_f[side], tile_i))
            o(nc.vector.tensor_copy(low_f[side], low_i))
            done = o.n + o.base
            with dve.Fori(0, NT) as b:
                o.loop(done, 1, b)
                o(nc.vector.tensor_scalar(mask, tile_f[side], iota_t[:, ds(b, 1)], 0.0, ALU.is_equal, ALU.add,
                                          accum_out=counts[:, ds(b, 1)]))
            o.total(done + NT)
            dve.sem_inc(counted, 1)
            dve.wait_ge(cum, 1)
            o(nc.vector.tensor_copy(tot[side][:, :], cum_tot))
            o(nc.vector.tensor_tensor_scan(ends[side][:, :], tot[side][:, :], zeros[:, 0:NT], 0.0, ALU.add, ALU.add))
            o(nc.vector.tensor_tensor(starts[side][:, :], ends[side][:, :], tot[side][:, :], ALU.subtract))
            o(nc.vector.scalar_tensor_tensor(rank0, cum_off, -1.0, starts[side][:, :], ALU.add, ALU.add))
            done = o.n + o.base
            with dve.Fori(0, NT) as b:
                o.loop(done, 3, b)
                o(nc.vector.tensor_scalar(mask, tile_f[side], iota_t[:, ds(b, 1)], None, ALU.is_equal))
                o(nc.vector.tensor_tensor_scan(rank, mask, zeros, rank0[:, ds(b, 1)], ALU.add, ALU.add))
                o.settle(passed_dve)
                o(nc.vector.copy_predicated(pos_f, mask, rank))
            o.total(done + 3 * NT)
            o(nc.vector.tensor_copy(pos_i[side], pos_f))
            o(nc.vector.tensor_copy(rec[side][:, :, 0], key_f))

        def scatter(pool, side, ring_sem, done_sems):
            f = REC[side]
            half = LANES // 2
            def turn(it, first):
                for h in range(2):
                    if not first:
                        pool.wait_ge(done_sems[h], it * (16 * half))
                    nc.gpsimd.tensor_copy(pos_ring[:, h * half:(h + 1) * half],
                                          pos_i[side][:, ds(it * LANES + h * half, half)]).then_inc(ring_sem, 1)
                    nc.gpsimd.tensor_copy(rec_ring[:, h * half * f:(h + 1) * half * f],
                                          rec[side].rearrange("p t f -> p (t f)")[:, ds((it * LANES + h * half) * f, half * f)])\
                        .then_inc(ring_sem, 1)
                    pool.wait_ge(ring_sem, it * 4 + 2 * h + 2)
                    pool.sem_inc(passed_pool, 1)
                    for k in range(h * half, (h + 1) * half):
                        pool.indirect_dma_start(
                            rec_dram[side], bass.IndirectOffsetOnAxis(pos_ring[:, k:k + 1], 0),
                            rec_ring[:, k * f:(k + 1) * f], None).then_inc(done_sems[h], 16)

            turn(0, True)
            with pool.Fori(1, COLS // LANES) as it:
                turn(it, False)
            for h in range(2):
                pool.wait_ge(done_sems[h], 16 * half * (COLS // LANES))

        with ExitStack() as c:
            sem = nc.alloc_semaphore
            padded, edges_in, dst_in, consts, order, counted, cum, stt = (
                sem(n) for n in ("padded", "edges_in", "dst_in", "consts", "order", "counted", "cum", "affine"))
            w_in_sem, wt_done, wt_copied = sem("weights_in"), sem("w_transposed"), sem("w_copied")
            block = c.enter_context(nc.Block())

            @block.sync
            def _(sp):
                sp.wait_ge(padded, 4)
                def load(dst_ap, flat, s):
                    sp.dma_start(dst_ap[0:FULL, :], flat[0:FULL * COLS].rearrange("(p t) -> p t", t=COLS)).then_inc(s, 16)
                    sp.dma_start(dst_ap[FULL:FULL + 1, 0:REST], flat[FULL * COLS:EDGES].rearrange("(p t) -> p t", p=1)).then_inc(s, 16)
                load(src_i, src, edges_in)
                load(dst_i, dst, edges_in)
                load(rel_i, edge_type_32, dst_in)
                load(w_in, edge_weight1.rearrange("e o -> (e o)"), dst_in)

            @block.scalar
            def _(act):
                for i, w in enumerate((L0_gnn_W0, L0_gnn_W1)):
                    act.dma_start(w_raw[:, i, :, :], w.rearrange("(k p) d -> p k d", p=P)).then_inc(w_in_sem, 16)
                for w, to in ((L1_gnn_W, w_gcn[:, :, :]), (L2_gnn_W_self, w_maxk[:, :, 0:D]), (L2_gnn_W_neigh, w_maxk[:, :, D:2 * D])):
                    act.dma_start(to, w.rearrange("(k p) d -> p k d", p=P)).then_inc(w_in_sem, 16)
                for i, row in enumerate((L0_gnn_b0, L0_gnn_g0, L0_gnn_beta0, L0_gnn_b1, L0_gnn_g1, L0_gnn_beta1)):
                    act.dma_start(rows6[:, i, :], row.rearrange("(o d) -> o d", o=1).to_broadcast([P, D])).then_inc(w_in_sem, 16)
                with nc.allow_non_contiguous_dma(reason="a table of 1 KB, once"):
                    act.dma_start(comp_t[:, :], L3_gnn_w_comp.rearrange("r b -> b r")).then_inc(w_in_sem, 16)
                act.wait_ge(w_in_sem, 16 * 12)
                for i in range(2):
                    act.wait_ge(wt_done, i + 1)
                    nc.scalar.copy(w_sage[i][:, :, :].rearrange("p k d -> p (k d)"), psum[:, 4 + i, :]).then_inc(wt_copied, 1)

            @block.gpsimd
            def _(pool):
                nc.gpsimd.memset(src_i, PAD_KEY).then_inc(padded, 1)
                nc.gpsimd.memset(dst_i, PAD_KEY).then_inc(padded, 1)
                nc.gpsimd.memset(rel_i, 0).then_inc(padded, 1)
                nc.gpsimd.memset(w_in, 0.0).then_inc(padded, 1)
                nc.gpsimd.iota(iota_t[:, :], [[1, NT]], base=0, channel_multiplier=0,
                               allow_small_or_imprecise_dtypes=True).then_inc(consts, 1)
                nc.gpsimd.iota(iota_p[:, :], [[1, P]], base=0, channel_multiplier=0,
                               allow_small_or_imprecise_dtypes=True).then_inc(consts, 1)
                nc.gpsimd.iota(iota_bf[:, :], [[1, P]], base=0, channel_multiplier=0,
                               allow_small_or_imprecise_dtypes=True).then_inc(consts, 1)
                nc.gpsimd.iota(edge_no, [[1, COLS]], base=0, channel_multiplier=COLS,
                               allow_small_or_imprecise_dtypes=True).then_inc(consts, 1)
                nc.gpsimd.memset(zeros, 0.0).then_inc(consts, 1)
                nc.gpsimd.memset(ones[:, :], 1.0).then_inc(consts, 1)
                nc.gpsimd.memset(ident[:, :], 0.0).then_inc(stt, 1)
                nc.gpsimd.memset(before[:, :], 1.0).then_inc(stt, 1)
                pool.wait_ge(stt, 2)
                nc.gpsimd.affine_select(out=ident[:, :], in_=ident[:, :], compare_op=ALU.not_equal, fill=1.0, base=0,
                                        pattern=[[-1, P]], channel_multiplier=1).then_inc(consts, 1)
                nc.gpsimd.affine_select(out=before[:, :], in_=before[:, :], compare_op=ALU.is_gt, fill=0.0, base=0,
                                        pattern=[[1, P]], channel_multiplier=-1).then_inc(consts, 1)

            @block.tensor
            def _(pe):
                pe.wait_ge(consts, 8)
                pe.wait_ge(w_in_sem, 16 * 12)
                for i in range(2):
                    for ki in range(2):
                        for ko in range(2):
                            ins = nc.tensor.transpose(psum[:, 4 + i, ki * D + ko * P:ki * D + (ko + 1) * P],
                                                      w_raw[:, i, ko, ki * P:(ki + 1) * P], ident[:, :])
                    ins.then_inc(wt_done, 1)
                pe.wait_ge(counted, 1)
                nc.tensor.matmul(cum_off, before[:, :], counts, start=True, stop=True)
                nc.tensor.matmul(cum_tot, ones[:, :], counts, start=True, stop=True).then_inc(cum, 1)

            @block.vector
            def _(dve):
                o = Chain(dve, order)
                dve.wait_ge(consts, 8)
                dve.wait_ge(edges_in, 64)
                sort_positions(dve, o, "s", counted, cum)
                o(nc.vector.tensor_copy(rec["s"][:, :, 1], dst_i))
                dve.wait_ge(dst_in, 64)
                dve.wait_ge(wt_copied, 2)

        with ExitStack() as c:
            sem = nc.alloc_semaphore
            order, counted, cum, hot, deg_done, rec_ready, rec_out = (
                sem(n) for n in ("order2", "counted2", "cum2", "hot", "deg_done", "rec_ready", "rec_out"))
            ring_sem = sem("ring_filled")
            scattered = [sem("scattered0"), sem("scattered1")]
            base_in = [sem("base_in0"), sem("base_in1")]
            relw_out = [sem("relw_out0"), sem("relw_out1")]
            relw_mm, relw_cp, rooted, degs = sem("relw_mm"), sem("relw_cp"), sem("rooted"), sem("degrees")
            block = c.enter_context(nc.Block())
            CH = 2048
            N_CH = D * D // CH
            HALVES = COLS // 4
            bases_flat = L3_gnn_bases.rearrange("b i o -> b (i o)")

            @block.gpsimd
            def _(pool):
                scatter(pool, "s", ring_sem, scattered)

            @block.sync
            def _(sp):
                with sp.Fori(0, N_CH // 2) as it:
                    for h in range(2):
                        sp.wait_ge(relw_mm, (it * 2 + h) * 4 + 4)
                        sp.dma_start(base_ring[0:BASES, h, :], bases_flat[:, ds((it * 2 + h) * CH, CH)]).then_inc(base_in[h], 16)
                sp.wait_ge(rec_ready, 1)
                sp.dma_start(rec_dram["d"].rearrange("(p t) f -> p (t f)", p=P), rec["d"].rearrange("p t f -> p (t f)")).then_inc(rec_out, 16)
                sp.wait_ge(rec_out, 16)

            @block.scalar
            def _(act):
                act.sem_inc(relw_cp, 4)
                for h in range(2):
                    act.sem_inc(relw_out[h], 16)
                with act.Fori(0, N_CH // 2) as it:
                    for h in range(2):
                        act.wait_ge(relw_out[h], it * 16 + 16)
                        for q in range(4):
                            act.wait_ge(relw_mm, (it * 2 + h) * 4 + q + 9)
                            nc.scalar.copy(relw_ring[0:RELS, h, q * 512:(q + 1) * 512], psum[0:RELS, 4 + q, :]).then_inc(relw_cp, 1)
                        act.wait_ge(relw_cp, (it * 2 + h) * 4 + 8)
                        act.dma_start(rel_w[:, ds((it * 2 + h) * CH, CH)], relw_ring[0:RELS, h, :]).then_inc(relw_out[h], 16)
                for h in range(2):
                    act.wait_ge(relw_out[h], 16 * (N_CH // 2) + 16)
                act.wait_ge(degs, 1)
                nc.scalar.activation(dis[:, :], small[:, 0, :], ACT.Sqrt).then_inc(rooted, 1)

            @block.tensor
            def _(pe):
                pe.sem_inc(relw_mm, 8)
                pe.wait_ge(counted, 1)
                nc.tensor.matmul(cum_off, before[:, :], counts, start=True, stop=True)
                nc.tensor.matmul(cum_tot, ones[:, :], counts, start=True, stop=True).then_inc(cum, 1)
                with pe.Fori(0, N_CH // 2) as it:
                    for h in range(2):
                        pe.wait_ge(base_in[h], it * 16 + 16)
                        for q in range(4):
                            pe.wait_ge(relw_cp, (it * 2 + h) * 4 + q + 1)
                            pe.sem_inc(passed_pe, 1)
                            nc.tensor.matmul(psum[0:RELS, 4 + q, :], comp_t[:, :], base_ring[0:BASES, h, q * 512:(q + 1) * 512],
                                             start=True, stop=True).then_inc(relw_mm, 1)
                pe.sem_inc(deg_done, 2)

                def count_half(side, n, h, first, last, base):
                    pe.wait_ge(hot, 2 * (base + n + 1))
                    for col in range(4):
                        ins = nc.tensor.matmul(deg_ps[side], low_hot[:, h, col, :], tile_hot[:, h, col, :],
                                               start=first and col == 0, stop=last and col == 3)
                    ins.then_inc(deg_done, 1)

                for s, side in enumerate("ds"):
                    for h in range(2):
                        count_half(side, h, h, h == 0, False, s * HALVES)
                    with pe.Fori(1, HALVES // 2 - 1) as it:
                        for h in range(2):
                            count_half(side, it * 2 + h, h, False, False, s * HALVES)
                    for h in range(2):
                        count_half(side, HALVES - 2 + h, h, False, h == 1, s * HALVES)

            @block.vector
            def _(dve):
                o = Chain(dve, order)
                sort_positions(dve, o, "d", counted, cum)
                o(nc.vector.tensor_copy(rec["d"][:, :, 1], src_i))
                o(nc.vector.scalar_tensor_tensor(rec["d"][:, :, 2], rec["d"][:, :, 1], float(RELS), rel_i, ALU.mult, ALU.add))
                o(nc.vector.tensor_copy(rec["d"][:, :, 3], w_in))
                o(nc.vector.tensor_tensor(rank, pos_f, edge_no, ALU.not_equal))
                o(nc.vector.tensor_reduce(moved[:, :], rank, AX.X, ALU.add))
                dve.sem_inc(rec_ready, 1)
                for s, side in enumerate("ds"):
                    with dve.Fori(0, HALVES // 2) as it:
                        for h in range(2):
                            col = it * 8 + h * 4
                            dve.wait_ge(deg_done, it * 2 + (s * HALVES + h + 1))
                            nc.vector.tensor_tensor(
                                low_hot[:, h, :, :], low_f[side][:, ds(col, 4)].unsqueeze(2).to_broadcast([P, 4, P]),
                                iota_bf[:, :].unsqueeze(1).to_broadcast([P, 4, P]), ALU.is_equal).then_inc(hot, 1)
                            nc.vector.tensor_tensor(
                                tile_hot[:, h, :, :], tile_f[side][:, ds(col, 4)].unsqueeze(2).to_broadcast([P, 4, NT]),
                                iota_t[:, :].unsqueeze(1).to_broadcast([P, 4, NT]), ALU.is_equal).then_inc(hot, 1)
                dve.wait_ge(deg_done, 2 * HALVES + 2)
                done = o.base + o.n
                o.total(done)
                o(nc.vector.tensor_scalar(small[:, 0, :], deg_ps["d"], 1.0, None, ALU.max))
                dve.sem_inc(degs, 1)
                o(nc.vector.tensor_scalar(small[:, 1, :], deg_ps["d"], 0.0, None, ALU.is_gt))
                o(nc.vector.tensor_scalar(small[:, 2, :], deg_ps["s"], 1.0, None, ALU.max))
                o(nc.vector.reciprocal(rdeg_d[:, :], small[:, 0, :]))
                o(nc.vector.reciprocal(rdeg_s[:, :], small[:, 2, :]))
                dve.wait_ge(rooted, 1)
                o(nc.vector.reciprocal(small[:, 3, :], dis[:, :]))
                o(nc.vector.tensor_tensor(dis[:, :], small[:, 3, :], small[:, 1, :], ALU.mult))

        with ExitStack() as c:
            sem = nc.alloc_semaphore
            order, flag_mm, flag_ready, rows_ready, tiles_ready, ordered = (
                sem(n) for n in ("order3", "flag_mm", "flag_ready", "rows_ready", "tiles_ready", "ordered"))
            ring_sem = sem("ring_filled3")
            scattered = [sem("scattered30"), sem("scattered31")]
            rows_in = [sem("rows_in0"), sem("rows_in1")]
            tp, cp, pcon = sem("fields_transposed"), sem("fields_copied"), sem("pair_iota")
            x_in = sem("x_in")
            block = c.enter_context(nc.Block())
            PC = PAIR_COLS
            pair_no = small[:, 7, 0:PC]
            pair_tile = {"s": small[:, 5, 0:PC], "d": small[:, 6, 0:PC]}
            rows_buf = work[:, ring0:ring0 + 2 * 512].rearrange("p (h n) -> p h n", h=2)
            tile_wide = work[:, ring0 + 1024:ring0 + 1024 + 2 * PC * P].rearrange("p (c j) -> p c j", j=P)
            tile_row = work[:, ring0 + 1024 + 2 * PC * P:ring0 + 1024 + 3 * PC * P]
            units = [(side, col) for side in "ds" for col in range(PC)]

            @block.gpsimd
            def _(pool):
                nc.gpsimd.iota(pair_no, [[P, PC]], base=0, channel_multiplier=1,
                               allow_small_or_imprecise_dtypes=True).then_inc(pcon, 1)
                pool.wait_ge(flag_ready, 1)
                n_moved = pool.value_load(moved_i[0:1, 0:1], min_val=0, max_val=P * COLS)
                with pool.If(n_moved > 0):
                    scatter(pool, "d", ring_sem, scattered)
                pool.sem_inc(ordered, 1)
                for u, (side, col) in enumerate(units):
                    f = REC[side]
                    pool.wait_ge(rows_ready, 1 if side == "d" else 2)
                    if u >= 2:
                        pool.wait_ge(tp, u - 1)
                    pool.indirect_dma_start(rows_buf[:, u % 2, 0:P * f], None,
                                            rec_dram[side].rearrange("(r j) f -> r (j f)", j=P),
                                            bass.IndirectOffsetOnAxis(row_i[side][:, col:col + 1], 0)).then_inc(rows_in[u % 2], 16)

            @block.tensor
            def _(pe):
                nc.tensor.matmul(psum[:, 0, 0:1], ones[:, :], moved[:, :], start=True, stop=True).then_inc(flag_mm, 1)
                for u, (side, col) in enumerate(units):
                    f = REC[side]
                    pe.wait_ge(rows_in[u % 2], 16 * (u // 2 + 1))
                    pe.wait_ge(tiles_ready, u + 1)
                    if u >= 2:
                        pe.wait_ge(cp, u - 1)
                    rows = rows_buf[:, u % 2, 0:P * f].rearrange("p (j f) -> p j f", f=f)
                    for k in range(f):
                        nc.tensor.transpose(psum[:, 2 + 2 * (u % 2), k * P:(k + 1) * P], rows[:, :, k], ident[:, :])
                    nc.tensor.matmul(psum[:, 3 + 2 * (u % 2), 0:P], tile_wide[:, u, :], ident[:, :],
                                     start=True, stop=True).then_inc(tp, 1)

            @block.vector
            def _(dve):
                o = Chain(dve, order)
                dve.wait_ge(flag_mm, 1)
                o(nc.vector.tensor_copy(moved_i[:, :], psum[:, 0, 0:1]))
                dve.sem_inc(flag_ready, 1)
                dve.wait_ge(pcon, 1)
                n_b = TILES
                for side in "ds":
                    first_row, last_row, pair_end, shift, step = (small[:, k, 0:n_b] for k in range(5))
                    o(nc.vector.tensor_copy(small_i[:, 0, 0:n_b], starts[side][:, 0:n_b]))
                    o(nc.vector.tensor_scalar(small_i[:, 0, 0:n_b], small_i[:, 0, 0:n_b], 7, None, ALU.arith_shift_right))
                    o(nc.vector.tensor_copy(first_row, small_i[:, 0, 0:n_b]))
                    o(nc.vector.tensor_scalar(last_row, ends[side][:, 0:n_b], -1.0, None, ALU.add))
                    o(nc.vector.tensor_copy(small_i[:, 0, 0:n_b], last_row))
                    o(nc.vector.tensor_scalar(small_i[:, 0, 0:n_b], small_i[:, 0, 0:n_b], 7, None, ALU.arith_shift_right))
                    o(nc.vector.tensor_copy(last_row, small_i[:, 0, 0:n_b]))
                    o(nc.vector.tensor_tensor(last_row, last_row, first_row, ALU.subtract))
                    o(nc.vector.tensor_scalar(step, tot[side][:, 0:n_b], 0.0, None, ALU.is_gt))
                    o(nc.vector.scalar_tensor_tensor(last_row, last_row, 1.0, step, ALU.add, ALU.mult))
                    o(nc.vector.tensor_tensor_scan(pair_end, last_row, zeros[:, 0:n_b], 0.0, ALU.add, ALU.add))
                    o(nc.vector.tensor_tensor(shift, first_row, pair_end, ALU.subtract))
                    o(nc.vector.tensor_tensor(shift, shift, last_row, ALU.add))
                    o(nc.vector.tensor_tensor(step[:, 0:n_b - 1], shift[:, 1:n_b], shift[:, 0:n_b - 1], ALU.subtract))
                    o(nc.vector.tensor_scalar(step[:, n_b - 1:n_b], shift[:, n_b - 1:n_b], -1.0, None, ALU.mult))
                    for col in range(PC):
                        o(nc.vector.tensor_scalar(first_row, pair_end, pair_no[:, col:col + 1], 0.0, ALU.is_le, ALU.add,
                                                  accum_out=pair_tile[side][:, col:col + 1]))
                        o(nc.vector.tensor_tensor(last_row, first_row, step, ALU.mult))
                        o(nc.vector.tensor_reduce(row_f[:, col:col + 1], last_row, AX.X, ALU.add))
                    o(nc.vector.tensor_scalar(row_f[:, :], row_f[:, :], shift[:, 0:1], None, ALU.add))
                    o(nc.vector.tensor_tensor(row_f[:, :], row_f[:, :], pair_no, ALU.add))
                    o(nc.vector.tensor_scalar(row_f[:, :], row_f[:, :], float(ROWS - 1), 0.0, ALU.min, ALU.max))
                    o(nc.vector.tensor_copy(row_i[side][:, :], row_f[:, :]))
                    dve.sem_inc(rows_ready, 1)
                for u, (side, col) in enumerate(units):
                    o(nc.vector.tensor_copy(tile_wide[:, u, :], pair_tile[side][:, col:col + 1].to_broadcast([P, P])))
                    dve.sem_inc(tiles_ready, 1)
                for u, (side, col) in enumerate(units):
                    here = slice(col * P, (col + 1) * P)
                    tile_ps = psum[:, 3 + 2 * (u % 2), 0:P]
                    field = lambda k: psum[:, 2 + 2 * (u % 2), k * P:(k + 1) * P]
                    dve.wait_ge(tp, u + 1)
                    o(nc.vector.tensor_copy(tile_row[:, here], tile_ps))
                    o(nc.vector.scalar_tensor_tensor(loc[side][:, here], tile_row[:, here], -float(P), field(0), ALU.mult, ALU.add))
                    o(nc.vector.tensor_scalar(off[side][:, here], tile_row[:, here], float(D), None, ALU.mult))
                    if side == "s":
                        o(nc.vector.tensor_scalar(idx_s[:, here], field(1), float(NODES - 1), None, ALU.min))
                    else:
                        o(nc.vector.tensor_scalar(idx_d[:, here], field(1), float(NODES - 1), None, ALU.min))
                        o(nc.vector.tensor_copy(idx_rel[:, here], field(2)))
                        o(nc.vector.tensor_copy(weight[:, here], field(3)))
                    dve.sem_inc(cp, 1)
                o(nc.vector.memset(state[:, (TILES - 1) * D:], 0.0))
                dve.sem_inc(cp, 1)

            @block.sync
            def _(sp):
                sp.wait_ge(cp, len(units) + 1)
                sp.dma_start(state[:, 0:(TILES - 1) * D].rearrange("p (t d) -> p t d", d=D),
                             x[0:(TILES - 1) * P, :].rearrange("(t p) d -> p t d", p=P)).then_inc(x_in, 16)
                sp.dma_start(state[0:LAST_ROWS, (TILES - 1) * D:TILES * D], x[(TILES - 1) * P:NODES, :]).then_inc(x_in, 16)
                sp.wait_ge(x_in, 32)

        def tile_of(buf, i, n=1):
            return buf[:, ds(i * D, n * D)]

        def aggregate(name, rows_dram, side, idx, w=None):
            with ExitStack() as c:
                sem = lambda n: nc.alloc_semaphore(f"{n}_{name}")
                idx_filled, hot_ready, multiplied, added, zeroed = (
                    sem(n) for n in ("idx_filled", "hot_ready", "multiplied", "added", "zeroed"))
                landed_before = rows_gathered[0]
                rows_gathered[0] += 16 * GROUP * (GROUPS // RING)
                block = c.enter_context(nc.Block())
                products = psum[:, :, :].rearrange("p b (s d) -> p (b s) d", d=D)

                @block.gpsimd
                def _(pool):
                    with pool.Fori(0, PAIRS // (4 * LANES)) as it:
                        for h in range(4):
                            nc.gpsimd.tensor_copy(idx_ring[:, h * LANES:(h + 1) * LANES],
                                                  idx[:, ds(it * (4 * LANES) + h * LANES, LANES)]).then_inc(idx_filled, 1)
                            pool.wait_ge(idx_filled, it * 4 + h + 1)
                            for g in range(h * LANES // GROUP, (h + 1) * LANES // GROUP):
                                pool.wait_ge(multiplied, it * (4 * LANES // GROUP) + g + 1)
                                pool.sem_inc(passed_pool, 1)
                                for k in range(GROUP):
                                    slot = g % RING * GROUP + k
                                    lane = g * GROUP + k
                                    pool.indirect_dma_start(gathered[:, slot, :], None, rows_dram,
                                                            bass.IndirectOffsetOnAxis(idx_ring[:, lane:lane + 1], 0))\
                                        .then_inc(landed[g % RING], 16)

                @block.tensor
                def _(pe):
                    pe.sem_inc(multiplied, CREDIT)
                    with pe.Fori(0, GROUPS // RING) as it:
                        for g in range(RING):
                            pe.wait_ge(landed[g], it * (16 * GROUP) + (landed_before + 16 * GROUP))
                            pe.wait_ge(hot_ready, it * RING + g + 1)
                            pe.wait_ge(added, (it * RING + g + 1) * GROUP)
                            for k in range(GROUP):
                                slot = g % OH_RING * GROUP + k
                                ins = nc.tensor.matmul(products[:, slot, :], onehot[:, slot, :],
                                                       gathered[:, g * GROUP + k, :], start=True, stop=True)
                            ins.then_inc(multiplied, 1)

                @block.vector
                def _(dve):
                    nc.vector.memset(sums, 0.0).then_inc(zeroed, 1)
                    dve.wait_ge(zeroed, 1)
                    dve.sem_inc(added, OH_RING * GROUP)

                    def make_onehot(q, g):
                        hot = onehot[:, g * GROUP:(g + 1) * GROUP, :]
                        dve.wait_ge(multiplied, q + 1 + CREDIT - OH_RING)
                        made = nc.vector.tensor_tensor(
                            hot, loc[side][:, ds(q * GROUP, GROUP)].unsqueeze(2).to_broadcast([P, GROUP, P]),
                            iota_p[:, :].unsqueeze(1).to_broadcast([P, GROUP, P]), ALU.is_equal)
                        if w is None:
                            made.then_inc(hot_ready, 1)
                            return
                        made.then_inc(zeroed, 1)
                        dve.wait_ge(zeroed, q + 2)
                        nc.vector.tensor_tensor(
                            hot, hot, w[:, ds(q * GROUP, GROUP)].unsqueeze(2).to_broadcast([P, GROUP, P]),
                            ALU.mult).then_inc(hot_ready, 1)

                    def add_products(q, g):
                        at = [dve.value_load(off[side][0:1, ds(q * GROUP + k, 1)], min_val=0, max_val=(NT - 1) * D)
                              for k in range(GROUP)]
                        dve.wait_ge(multiplied, q + 1 + CREDIT)
                        for k in range(GROUP):
                            dve.wait_ge(added, q * GROUP + k + OH_RING * GROUP)
                            tile = sums[:, ds(at[k], D)]
                            nc.vector.tensor_tensor(tile, tile, products[:, g * GROUP + k, :], ALU.add).then_inc(added, 1)

                    make_onehot(0, 0)
                    with dve.Fori(0, GROUPS // OH_RING - 1) as it:
                        for g in range(OH_RING):
                            make_onehot(it * OH_RING + g + 1, (g + 1) % OH_RING)
                            add_products(it * OH_RING + g, g)
                    for g in range(OH_RING):
                        if g < OH_RING - 1:
                            make_onehot(GROUPS - OH_RING + g + 1, g + 1)
                        add_products(GROUPS - OH_RING + g, g)
                    dve.wait_ge(added, PAIRS + OH_RING * GROUP)

        def row_moments(o, rows, i):
            o.settle(passed_dve)
            o(nc.vector.bn_stats(stats[:, 0, :], rows))
            o.settle(passed_dve)
            o(nc.vector.bn_aggr(stats[:, 1, 0:2], stats[:, 0, :]))
            o(nc.vector.tensor_copy(moments[:, ds(i, 1), :].rearrange("p t m -> p (t m)"), stats[:, 1, 0:2]))

        def pipelined(eng, first, second):
            first(0, 0, None, 0)
            with eng.Fori(0, NT // 2 - 1) as it:
                first(it * 2 + 1, 1, it, 0)
                second(it * 2, 0, it, 0)
                first(it * 2 + 2, 0, it, 1)
                second(it * 2 + 1, 1, it, 1)
            first(NT - 1, 1, None, 1)
            second(NT - 2, 0, NT // 2 - 1, 0)
            second(NT - 1, 1, NT // 2 - 1, 1)

        def transform(name, kind, weights, bias=None, rdeg=None):
            with ExitStack() as c:
                sem = lambda n: nc.alloc_semaphore(f"{n}_{name}")
                made, transposed, copied, multiplied, used, order = (
                    sem(n) for n in ("made", "transposed", "copied", "multiplied", "used", "order"))
                if kind == "maxk":
                    stored = [sem("stored0"), sem("stored1")]
                    sparse_ready = sem("sparse_ready")
                block = c.enter_context(nc.Block())
                n_out = weights.shape[2]
                tp = psum[:, 0:2, 0:D]
                steps = {"sage": 4, "gcn": 4, "maxk": 12}[kind]
                dense = gathered[:, 0, :]
                left = gathered[:, 1, :]
                sparse = gathered[:, 2:4, :]
                top8 = stats_top

                @block.vector
                def _(dve):
                    o = Chain(dve, order)
                    dve.sem_inc(used, 2)

                    def make(i, b, it, n):
                        dve.wait_ge(transposed, i + 1)
                        if kind == "sage":
                            ins = nc.vector.tensor_scalar(operand[:, b, :], tile_of(sums, i), rdeg[:, ds(i, 1)], None, ALU.mult)
                            ins.then_inc(made, 1)
                            dve.wait_ge(made, i * 2 + 1)
                            ins = nc.vector.tensor_tensor(operand[:, b, :], operand[:, b, :], tile_of(state, i), ALU.add)
                        elif kind == "gcn":
                            ins = nc.vector.tensor_scalar(operand[:, b, :], tile_of(sums, i), dis[:, ds(i, 1)], None, ALU.mult)
                        else:
                            ins = nc.vector.tensor_copy(operand[:, b, :], tile_of(state, i))
                        ins.then_inc(made, 1)

                    def use(i, b, it, n):
                        o.total(i * steps)
                        product = psum[:, 2 + b, 0:n_out]
                        dve.wait_ge(multiplied, i + 3)
                        if kind == "maxk":
                            dve.wait_ge(stored[b], it * 16 + 16)
                            o(nc.vector.tensor_copy(dense, product[:, D:2 * D]))
                            o(nc.vector.tensor_tensor(tile_of(state, i), product[:, 0:D], tile_of(state, i), ALU.add))
                            dve.sem_inc(used, 1)
                            for r in range(4):
                                o.settle(passed_dve)
                                o(nc.vector.max(top8[:, :], dense if r == 0 else left))
                                o.settle(passed_dve)
                                o(nc.vector.match_replace(left, top8[:, :], dense if r == 0 else left, -3.4e38))
                            o(nc.vector.tensor_tensor(left, left, dense, ALU.not_equal))
                            o(nc.vector.tensor_tensor(sparse[:, b, :], left, dense, ALU.mult))
                            dve.sem_inc(sparse_ready, 1)
                            return
                        to = tile_of(sums if kind == "sage" else state, i)
                        o(nc.vector.tensor_tensor(to, product, bias if kind == "sage" else to, ALU.add))
                        dve.sem_inc(used, 1)
                        row_moments(o, to, i)

                    pipelined(dve, make, use)

                @block.scalar
                def _(act):
                    act.sem_inc(copied, 2)
                    with act.Fori(0, NT // 2) as it:
                        for b in range(2):
                            act.wait_ge(transposed, it * 2 + b + 3)
                            act.wait_ge(multiplied, it * 2 + b + 1)
                            nc.scalar.copy(operandT[:, b, :], tp[:, b, :]).then_inc(copied, 1)

                @block.tensor
                def _(pe):
                    pe.sem_inc(transposed, 2)
                    pe.sem_inc(multiplied, 2)

                    def turn(i, b, it, n):
                        pe.wait_ge(made, i * 2 + 2 if kind == "sage" else i + 1)
                        pe.wait_ge(copied, i + 1)
                        for k in range(2):
                            ins = nc.tensor.transpose(tp[:, b, k * P:(k + 1) * P], operand[:, b, k * P:(k + 1) * P], ident[:, :])
                        ins.then_inc(transposed, 1)

                    def multiply(i, b, it, n):
                        pe.wait_ge(copied, i + 3)
                        pe.wait_ge(used, i + 1)
                        for k in range(2):
                            ins = nc.tensor.matmul(psum[:, 2 + b, 0:n_out], operandT[:, b, k * P:(k + 1) * P],
                                                   weights[:, k, :], start=k == 0, stop=k == 1)
                        ins.then_inc(multiplied, 1)

                    pipelined(pe, turn, multiply)

                if kind == "maxk":
                    @block.sync
                    def _(sp):
                        for b in range(2):
                            sp.sem_inc(stored[b], 16)
                        with sp.Fori(0, NT // 2) as it:
                            for b in range(2):
                                sp.wait_ge(sparse_ready, it * 2 + b + 1)
                                sp.dma_start(table[2][ds((it * 2 + b) * P, P), :], sparse[:, b, :]).then_inc(stored[b], 16)
                        for b in range(2):
                            sp.wait_ge(stored[b], 16 * (NT // 2) + 16)

        CHUNK = 5
        N_CHUNKS = NT // CHUNK

        def chunk_of(buf, c, n=CHUNK):
            return buf[:, ds(c * CHUNK * D, n * D)]

        def rows_of(buf):
            return buf.rearrange("p (t d) -> p t d", d=D)

        def table_chunk(t, c):
            return t[ds(c * (CHUNK * P), CHUNK * P), :].rearrange("(t p) d -> p t d", p=P)

        def root_of_variances(dve, act_turn, o):
            to_root, rooted, base = act_turn
            o(nc.vector.tensor_scalar(rstd[:, :], moments[:, :, 1], EPS, None, ALU.add))
            dve.sem_inc(to_root, 1)
            dve.wait_ge(rooted, base)
            o(nc.vector.reciprocal(rstd[:, :], rstd[:, :]))

        def normalise_sage(name, g, beta, last):
            with ExitStack() as c:
                sem = lambda n: nc.alloc_semaphore(f"{n}_{name}")
                order, to_root, rooted, normed, lit, stored = (
                    sem(n) for n in ("order", "to_root", "rooted", "normed", "lit", "stored"))
                if last:
                    scaled, x_in, x_used = sem("scaled"), [sem("x_in0"), sem("x_in1")], sem("x_used")
                block = c.enter_context(nc.Block())
                x_buf = work[:, ring0:ring0 + 2 * CHUNK * D].rearrange("p (b n) -> p b n", b=2)
                wide = [P, CHUNK, D]

                @block.scalar
                def _(act):
                    act.wait_ge(to_root, 1)
                    nc.scalar.activation(rstd[:, :], rstd[:, :], ACT.Sqrt).then_inc(rooted, 1)
                    with act.Fori(0, N_CHUNKS) as it:
                        act.wait_ge(normed, it + 1)
                        nc.scalar.activation(chunk_of(sums if last else state, it), chunk_of(sums, it), ACT.Silu).then_inc(lit, 1)
                    if last:
                        act.wait_ge(to_root, 2)
                        nc.scalar.activation(rstd[:, :], rstd[:, :], ACT.Sqrt).then_inc(rooted, 1)

                @block.vector
                def _(dve):
                    o = Chain(dve, order)
                    root_of_variances(dve, (to_root, rooted, 1), o)
                    with dve.Fori(0, N_CHUNKS) as it:
                        o.loop(2, CHUNK + 1, it)
                        for k in range(CHUNK):
                            i = it * CHUNK + k
                            o(nc.vector.tensor_scalar(tile_of(sums, i), tile_of(sums, i), moments[:, ds(i, 1), 0],
                                                      rstd[:, ds(i, 1)], ALU.subtract, ALU.mult))
                        part = rows_of(chunk_of(sums, it))
                        o(nc.vector.tensor_tensor(part, part, g.unsqueeze(1).to_broadcast(wide), ALU.mult))
                        nc.vector.tensor_tensor(part, part, beta.unsqueeze(1).to_broadcast(wide), ALU.add).then_inc(normed, 1)
                    if not last:
                        return
                    done = 2 + N_CHUNKS * (CHUNK + 1)

                    def with_x(ch, b, it):
                        dve.wait_ge(lit, ch + 1)
                        o(nc.vector.tensor_tensor(chunk_of(state, ch), chunk_of(sums, ch), x_buf[:, b, :], ALU.add))
                        dve.sem_inc(x_used, 1)
                        for k in range(CHUNK):
                            i = ch * CHUNK + k
                            row_moments(o, tile_of(state, i), i)

                    per = 3 * CHUNK + 1
                    with dve.Fori(0, N_CHUNKS // 2 - 1) as it:
                        for b in range(2):
                            o.total(it * (2 * per) + (done + b * per))
                            dve.wait_ge(x_in[b], it * 16 + 16)
                            with_x(it * 2 + b, b, it)
                    o.total(done + (N_CHUNKS - 2) * per)
                    dve.wait_ge(x_in[0], 16 * (N_CHUNKS // 2))
                    with_x(N_CHUNKS - 2, 0, None)
                    dve.wait_ge(x_in[1], 16 * (N_CHUNKS // 2 + 1))
                    with_x(N_CHUNKS - 1, 1, None)
                    root_of_variances(dve, (to_root, rooted, 2), o)
                    done += N_CHUNKS * per + 2
                    with dve.Fori(0, NT) as i:
                        o.loop(done, 1, i)
                        o(nc.vector.tensor_scalar(tile_of(state, i), tile_of(state, i), moments[:, ds(i, 1), 0],
                                                  rstd[:, ds(i, 1)], ALU.subtract, ALU.mult))
                        nc.vector.tensor_scalar(tile_of(sums, i), tile_of(state, i), dis[:, ds(i, 1)], None, ALU.mult)\
                            .then_inc(scaled, 1)

                @block.sync
                def _(sp):
                    if last:
                        with sp.Fori(0, N_CHUNKS // 2 - 1) as it:
                            for b in range(2):
                                sp.wait_ge(x_used, it * 2 + b + 1)
                                sp.dma_start(rows_of(x_buf[:, b, :]), table_chunk(x, it * 2 + b)).then_inc(x_in[b], 16)
                        sp.wait_ge(x_used, N_CHUNKS - 1)
                        sp.dma_start(rows_of(x_buf[:, 0, :]), table_chunk(x, N_CHUNKS - 2)).then_inc(x_in[0], 16)
                        sp.wait_ge(x_used, N_CHUNKS)
                        at = (N_CHUNKS - 1) * CHUNK
                        sp.dma_start(rows_of(x_buf[:, 1, 0:(TILES - 1 - at) * D]),
                                     x[at * P:(TILES - 1) * P, :].rearrange("(t p) d -> p t d", p=P)).then_inc(x_in[1], 16)
                        sp.dma_start(x_buf[0:LAST_ROWS, 1, (TILES - 1 - at) * D:(TILES - at) * D],
                                     x[(TILES - 1) * P:NODES, :]).then_inc(x_in[1], 16)
                    with sp.Fori(0, N_CHUNKS) as it:
                        if last:
                            sp.wait_ge(scaled, it * CHUNK + CHUNK)
                        else:
                            sp.wait_ge(lit, it + 1)
                        sp.dma_start(table_chunk(table[1 if last else 0], it),
                                     rows_of(chunk_of(sums if last else state, it))).then_inc(stored, 16)
                    sp.wait_ge(stored, 16 * N_CHUNKS)

                if last:
                    @block.gpsimd
                    def _(pool):
                        pool.sem_inc(x_used, 2)

        def normalise(name, before_norm=None, to_out=False):
            with ExitStack() as c:
                sem = lambda n: nc.alloc_semaphore(f"{n}_{name}")
                order, to_root, rooted, normed = (sem(n) for n in ("order", "to_root", "rooted", "normed"))
                if to_out:
                    stored = sem("stored")
                block = c.enter_context(nc.Block())

                @block.scalar
                def _(act):
                    act.wait_ge(to_root, 1)
                    nc.scalar.activation(rstd[:, :], rstd[:, :], ACT.Sqrt).then_inc(rooted, 1)

                @block.vector
                def _(dve):
                    o = Chain(dve, order)
                    done = 0
                    if before_norm:
                        with dve.Fori(0, NT) as i:
                            o.loop(0, 4, i)
                            if before_norm == "mean":
                                o(nc.vector.scalar_tensor_tensor(tile_of(state, i), tile_of(sums, i), rdeg_d[:, ds(i, 1)],
                                                                 tile_of(state, i), ALU.mult, ALU.add))
                            else:
                                o(nc.vector.scalar_tensor_tensor(tile_of(state, i), tile_of(sums, i), 0.0,
                                                                 tile_of(state, i), ALU.max, ALU.add))
                            row_moments(o, tile_of(state, i), i)
                        done = 4 * NT
                    o.total(done)
                    root_of_variances(dve, (to_root, rooted, 1), o)
                    with dve.Fori(0, NT) as i:
                        nc.vector.tensor_scalar(tile_of(state, i), tile_of(state, i), moments[:, ds(i, 1), 0],
                                                rstd[:, ds(i, 1)], ALU.subtract, ALU.mult).then_inc(normed, 1)
                    dve.wait_ge(normed, NT)

                if to_out:
                    @block.sync
                    def _(sp):
                        n = (TILES - 1) // 4
                        with sp.Fori(0, n) as it:
                            sp.wait_ge(normed, it * 4 + 4)
                            sp.dma_start(out[ds(it * (4 * P), 4 * P), :].rearrange("(t p) d -> p t d", p=P),
                                         rows_of(state[:, ds(it * (4 * D), 4 * D)])).then_inc(stored, 16)
                        sp.wait_ge(normed, TILES)
                        sp.dma_start(out[4 * n * P:NODES, :], state[0:LAST_ROWS, 4 * n * D:(4 * n + 1) * D]).then_inc(stored, 16)
                        sp.wait_ge(stored, 16 * (n + 1))

        def relation_table():
            with ExitStack() as c:
                sem = lambda n: nc.alloc_semaphore(f"{n}_rel")
                w_in, made, transposed, copied, tile_done, multiplied = (
                    sem(n) for n in ("w_in", "made", "transposed", "copied", "tile_done", "multiplied"))
                taken_by = {"dve": sem("taken_dve"), "act": sem("taken_act")}
                stored = [sem(f"stored{k}") for k in range(4)]
                block = c.enter_context(nc.Block())
                w_all = work[:, 0:2 * RELS * D].rearrange("p (k n) -> p k n", k=2)
                st0 = 2 * RELS * D
                stage = work[:, st0:st0 + 4 * 1024].rearrange("p (s n) -> p s n", s=4)
                tp = psum[:, 0:2, 0:D]
                PARTS = RELS * D // 512
                SLOTS = 4

                @block.sync
                def _(sp):
                    for k in range(4):
                        sp.sem_inc(stored[k], 16)
                    for k in range(2):
                        sp.dma_start(w_all[:, k, :].rearrange("p (r o) -> p r o", o=D),
                                     rel_w[:, k * P * D:(k + 1) * P * D].rearrange("r (i o) -> i r o", o=D)).then_inc(w_in, 16)
                    with sp.Fori(0, NT) as i:
                        for m in range(PARTS // 2):
                            sp.wait_ge(taken_by["dve" if m % 2 == 0 else "act"], i * (PARTS // 2) + (m // 2 * 2 + 2) + 2)
                            sp.dma_start(rel_table[ds(i * P, P), m * 1024:(m + 1) * 1024], stage[:, m % 4, :])\
                                .then_inc(stored[m % 4], 16)
                    for k in range(4):
                        sp.wait_ge(stored[k], 16 * NT * (PARTS // 8) + 16)

                def take(eng, copy, who, i, m):
                    eng.wait_ge(stored[m % 4], i * (16 * PARTS // 8) + (16 * (m // 4) + 16))
                    for s in range(2):
                        part = 2 * m + s
                        eng.wait_ge(multiplied, i * PARTS + part + 1)
                        copy(stage[:, m % 4, s * 512:(s + 1) * 512], psum[:, 4 + part % SLOTS, :]).then_inc(taken_by[who], 1)

                @block.vector
                def _(dve):
                    dve.sem_inc(taken_by["dve"], 2)

                    def make(i, b, it, n):
                        dve.wait_ge(transposed, i + 1)
                        nc.vector.tensor_copy(operand[:, b, :], tile_of(state, i)).then_inc(made, 1)

                    def use(i, b, it, n):
                        for m in range(0, PARTS // 2, 2):
                            take(dve, nc.vector.tensor_copy, "dve", i, m)

                    pipelined(dve, make, use)

                @block.scalar
                def _(act):
                    act.sem_inc(taken_by["act"], 2)
                    act.sem_inc(copied, 2)

                    def copy_turned(i, b, it, n):
                        act.wait_ge(transposed, i + 3)
                        act.wait_ge(tile_done, i + 1)
                        nc.scalar.copy(operandT[:, b, :], tp[:, b, :]).then_inc(copied, 1)

                    def use(i, b, it, n):
                        for m in range(1, PARTS // 2, 2):
                            take(act, nc.scalar.copy, "act", i, m)

                    pipelined(act, copy_turned, use)

                @block.tensor
                def _(pe):
                    pe.sem_inc(transposed, 2)
                    pe.sem_inc(tile_done, 2)
                    pe.wait_ge(w_in, 32)

                    def turn(i, b, it, n):
                        pe.wait_ge(made, i + 1)
                        pe.wait_ge(copied, i + 1)
                        for k in range(2):
                            ins = nc.tensor.transpose(tp[:, b, k * P:(k + 1) * P], operand[:, b, k * P:(k + 1) * P], ident[:, :])
                        ins.then_inc(transposed, 1)

                    def multiply(i, b, it, n):
                        pe.wait_ge(copied, i + 3)
                        for part in range(PARTS):
                            slot = part % SLOTS
                            who = "dve" if slot < 2 else "act"
                            pe.wait_ge(taken_by[who], i * (PARTS // 2) + (part // 4 * 2 + slot % 2 + 1))
                            for k in range(2):
                                ins = nc.tensor.matmul(psum[:, 4 + slot, :], operandT[:, b, k * P:(k + 1) * P],
                                                       w_all[:, k, part * 512:(part + 1) * 512], start=k == 0, stop=k == 1)
                            ins.then_inc(multiplied, 1)
                        pe.wait_ge(multiplied, i * PARTS + PARTS)
                        pe.sem_inc(tile_done, 1)

                    pipelined(pe, turn, multiply)

        aggregate("sum_sage0", x, "s", idx_s)
        transform("sage0", "sage", w_sage[0][:, :, :], b_rep[0], rdeg_s)
        normalise_sage("nsage0", g_rep[0], beta_rep[0], False)
        aggregate("sum_sage1", table[0], "s", idx_s)
        transform("sage1", "sage", w_sage[1][:, :, :], b_rep[1], rdeg_s)
        normalise_sage("nsage1", g_rep[1], beta_rep[1], True)
        aggregate("sum_gcn", table[1], "d", idx_d)
        transform("gcn", "gcn", w_gcn[:, :, :])
        normalise("ngcn")
        transform("maxk", "maxk", w_maxk[:, :, :])
        aggregate("sum_maxk", table[2], "d", idx_d)
        normalise("nmaxk", "mean")
        relation_table()
        aggregate("sum_rel", rel_table.rearrange("n (r d) -> (n r) d", d=D), "d", idx_rel, weight)
        normalise("nrel", "relu", True)


_INS = ["x", "src", "dst", "edge_type_32", "edge_weight1", "L0_gnn_W0", "L0_gnn_b0", "L0_gnn_g0", "L0_gnn_beta0",
        "L0_gnn_W1", "L0_gnn_b1", "L0_gnn_g1", "L0_gnn_beta1", "L1_gnn_W", "L2_gnn_W_self", "L2_gnn_W_neigh",
        "L3_gnn_bases", "L3_gnn_w_comp"]
_OUTS = [((NODES, D), "float32")]


def kernel(**inputs):
    import numpy as _np
    import concourse.bacc as _bacc
    from concourse import mybir as _mybir
    from concourse.bass_utils import run_bass_kernel_spmd as _run

    nc = _bacc.Bacc("TRN2", target_bir_lowering=False, num_devices=1)
    arrays, args = {}, []
    for name in _INS:
        a = _np.ascontiguousarray(inputs[name])
        arrays[f"in_{name}_dram"] = a
        args.append(nc.dram_tensor(f"in_{name}_dram", a.shape, _mybir.dt.from_np(a.dtype), kind="ExternalInput").ap())
    for i, (shape, dtype) in enumerate(_OUTS):
        dt = _mybir.dt.from_np(_np.dtype(dtype))
        args.append(nc.dram_tensor(f"out_{i}_dram", shape, dt, kind="ExternalOutput").ap())
    build(nc, *args)
    r = _run(nc, [arrays], core_ids=[0])
    got = tuple(r.results[0][f"out_{i}_dram"] for i in range(len(_OUTS)))
    return got[0]
```

```python
from contextlib import ExitStack

import numpy as np

import concourse.bass as bass
from concourse import mybir
from concourse.alu_op_type import AluOpType as ALU

F32 = mybir.dt.float32
BF16 = mybir.dt.bfloat16
I32 = mybir.dt.int32
I16 = mybir.dt.int16
ACT = mybir.ActivationFunctionType
AX = mybir.AxisListType

P = 128
NODES, D, EDGES = 6250, 256, 100000
RELS, BASES = 32, 8
EPS = 1e-5
TILES = -(-NODES // P)
NT = TILES + 1
LAST_ROWS = NODES - (TILES - 1) * P
LANES = 16
COLS = -(-EDGES // P // LANES) * LANES
FULL = EDGES // COLS
REST = EDGES - FULL * COLS
PAD_KEY = TILES * P
ROWS = COLS
GROUP = 4
PAIRS = -(-(ROWS + TILES - 1) // 64) * 64
GROUPS = PAIRS // GROUP
PAIR_COLS = -(-PAIRS // P)
RING = 8
OH_RING = 4
CREDIT = RING


class Chain:

    def __init__(self, eng, sem):
        self.eng, self.sem, self.base, self.n = eng, sem, 0, 0

    def __call__(self, ins):
        self.n += 1
        ins.then_inc(self.sem, 1)
        self.eng.wait_ge(self.sem, self.base + self.n)

    def loop(self, base, steps_per_turn, turn):
        self.base, self.n = base + turn * steps_per_turn, 0

    def total(self, n):
        self.base, self.n = n, 0

    def settle(self, counted):
        self.eng.sem_inc(counted, 1)


def build(nc, x, src, dst, edge_type_32, edge_weight1, L0_gnn_W0, L0_gnn_b0, L0_gnn_g0, L0_gnn_beta0,
          L0_gnn_W1, L0_gnn_b1, L0_gnn_g1, L0_gnn_beta1, L1_gnn_W, L2_gnn_W_self, L2_gnn_W_neigh,
          L3_gnn_bases, L3_gnn_w_comp, out):
    ctx = ExitStack()
    ds = bass.ds
    with ctx:
        def sb(name, shape, dt=F32):
            return ctx.enter_context(nc.sbuf_tensor(name, shape, dt))

        def dram(name, shape, dt=F32):
            return nc.dram_tensor(name, shape, dt, kind="Internal").ap()

        rec_dram = {"s": dram("rec_s", [P * COLS, 2]), "d": dram("rec_d", [P * COLS, 4])}
        table = [dram(f"table{i}", [NT * P, D]) for i in range(3)]
        rel_table = dram("rel_table", [NT * P, RELS * D])
        rel_w = dram("rel_w", [RELS, D * D])

        state = sb("state", [P, NT * D])
        work = sb("work", [P, NT * D + RING * GROUP * D])
        sums = work[:, 0:NT * D]
        ring0 = NT * D
        gathered = work[:, ring0:ring0 + RING * GROUP * D].rearrange("p (s d) -> p s d", d=D)
        onehot = sb("onehot", [P, OH_RING * GROUP, P])
        ident = sb("ident", [P, P])
        ones = sb("ones", [P, P])
        before = sb("before", [P, P])
        iota_p = sb("iota_p", [P, P])
        iota_bf = sb("iota_bf", [P, P], BF16)
        npf = PAIR_COLS * P
        loc = {"s": sb("loc_s", [P, npf]), "d": sb("loc_d", [P, npf])}
        off = {"s": sb("off_s", [P, npf], I32), "d": sb("off_d", [P, npf], I32)}
        idx_s = sb("idx_s", [P, npf], I32)
        idx_d = sb("idx_d", [P, npf], I32)
        idx_rel = sb("idx_rel", [P, npf], I32)
        weight = sb("weight", [P, npf])
        idx_ring = sb("idx_ring", [P, 4 * LANES], I32)
        w_sage = [sb("w_sage0", [P, 2, D]), sb("w_sage1", [P, 2, D])]
        w_gcn = sb("w_gcn", [P, 2, D])
        w_maxk = sb("w_maxk", [P, 2, 2 * D])
        rows6 = sb("rows6", [P, 6, D])
        b_rep = [rows6[:, 0, :], rows6[:, 3, :]]
        g_rep = [rows6[:, 1, :], rows6[:, 4, :]]
        beta_rep = [rows6[:, 2, :], rows6[:, 5, :]]
        rdeg_s = sb("rdeg_s", [P, NT])
        rdeg_d = sb("rdeg_d", [P, NT])
        dis = sb("dis", [P, NT])
        stats = sb("stats", [P, NT, 6])
        mean = sb("mean", [P, NT])
        rstd = sb("rstd", [P, NT])
        shift = sb("shift", [P, NT])
        rstd_dis = sb("rstd_dis", [P, NT])
        shift_dis = sb("shift_dis", [P, NT])
        top8 = sb("top8", [P, 2, 8])
        first_row_of = sb("first_row_of", [P, P])
        operand = sb("operand", [P, 2, D])
        operandT = sb("operandT", [P, 2, D])
        psum = ctx.enter_context(nc.psum_tensor("psum", [P, 8, 512], F32))

        tot = {k: sb(f"tot_{k}", [P, NT]) for k in "sd"}
        ends = {k: sb(f"ends_{k}", [P, NT]) for k in "sd"}
        starts = {k: sb(f"starts_{k}", [P, NT]) for k in "sd"}
        moved = sb("moved", [P, 1])
        moved_i = sb("moved_i", [P, 1], I32)
        small = sb("small", [P, 8, NT])
        small_i = sb("small_i", [P, 2, NT], I32)
        iota_t = sb("iota_t", [P, NT])
        row_i = {k: sb(f"row_{k}", [P, PAIR_COLS], I32) for k in "sd"}
        row_f = sb("row_f", [P, PAIR_COLS])

        taken = {"state": 0, "work": 0}

        def carve(where, n, dt=F32):
            a = (state if where == "state" else work)[:, taken[where]:taken[where] + n]
            taken[where] += n
            assert taken[where] <= NT * D
            return a if dt == F32 else a.bitcast(dt)

        src_i, dst_i, rel_i = (carve("state", COLS, I32) for _ in range(3))
        w_in = carve("state", COLS)
        zeros = carve("state", COLS)
        rec = {"s": carve("state", 2 * COLS).rearrange("p (t f) -> p t f", f=2),
               "d": carve("state", 4 * COLS).rearrange("p (t f) -> p t f", f=4)}
        pos_i = {"s": carve("state", COLS, I32), "d": carve("state", COLS, I32)}
        tile_i, low_i = carve("work", COLS, I32), carve("work", COLS, I32)
        key_f, edge_no = carve("work", COLS), carve("work", COLS)
        tile_f = {"s": carve("work", COLS), "d": carve("work", COLS)}
        low_f = {"s": carve("work", COLS), "d": carve("work", COLS)}
        rank, pos_f = carve("work", COLS), carve("work", COLS)
        mask = carve("work", COLS // 2, I16)
        counts = carve("work", NT)
        rank0 = carve("work", NT)
        pos_ring = carve("work", LANES, I32)
        rec_ring = carve("work", LANES * 4)
        low_hot = carve("work", 2 * 4 * P // 2, BF16).rearrange("p (h c j) -> p h c j", h=2, c=4)
        tile_hot = carve("work", 2 * 4 * NT // 2, BF16).rearrange("p (h c j) -> p h c j", h=2, c=4)
        base_ring = work[:, ring0:ring0 + 4096].rearrange("p (h n) -> p h n", h=2)
        relw_ring = work[:, ring0 + 4096:ring0 + 8192].rearrange("p (h n) -> p h n", h=2)
        w_raw = onehot[:, 0:8, :].rearrange("p s j -> p (s j)").rearrange("p (w k d) -> p w k d", w=2, k=2)
        comp_t = sb("comp_t", [BASES, RELS])
        keys = {"s": src_i, "d": dst_i}
        REC = {"s": 2, "d": 4}

        cum_off, cum_tot = psum[:, 0, 0:NT], psum[:, 0, 64:64 + NT]
        deg_ps = {"d": psum[:, 1, 0:NT], "s": psum[:, 2, 0:NT]}

        passed_dve, passed_pe, passed_pool = (
            ctx.enter_context(nc.semaphore(n)) for n in ("passed_dve", "passed_pe", "passed_pool"))
        landed = [ctx.enter_context(nc.semaphore(f"landed{g}")) for g in range(RING)]
        idx_filled, hot_ready, multiplied_sums, added_sums, zeroed = (
            ctx.enter_context(nc.semaphore(n)) for n in ("idx_filled", "hot_ready", "multiplied_sums", "added_sums", "zeroed"))

        def sort_positions(dve, o, side, counted, cum):
            o(nc.vector.tensor_copy(key_f, keys[side]))
            o(nc.vector.tensor_scalar(tile_i, keys[side], 7, None, ALU.arith_shift_right))
            o(nc.vector.tensor_scalar(low_i, keys[side], P - 1, None, ALU.bitwise_and))
            o(nc.vector.tensor_copy(tile_f[side], tile_i))
            o(nc.vector.tensor_copy(low_f[side], low_i))
            done = o.n + o.base
            with dve.Fori(0, NT) as b:
                o.loop(done, 1, b)
                o(nc.vector.tensor_scalar(mask, tile_f[side], iota_t[:, ds(b, 1)], 0.0, ALU.is_equal, ALU.add,
                                          accum_out=counts[:, ds(b, 1)]))
            o.total(done + NT)
            dve.sem_inc(counted, 1)
            dve.wait_ge(cum, 1)
            o(nc.vector.tensor_copy(tot[side][:, :], cum_tot))
            o(nc.vector.tensor_tensor_scan(ends[side][:, :], tot[side][:, :], zeros[:, 0:NT], 0.0, ALU.add, ALU.add))
            o(nc.vector.tensor_tensor(starts[side][:, :], ends[side][:, :], tot[side][:, :], ALU.subtract))
            o(nc.vector.scalar_tensor_tensor(rank0, cum_off, -1.0, starts[side][:, :], ALU.add, ALU.add))
            done = o.n + o.base
            with dve.Fori(0, NT) as b:
                o.loop(done, 3, b)
                o(nc.vector.tensor_scalar(mask, tile_f[side], iota_t[:, ds(b, 1)], None, ALU.is_equal))
                o(nc.vector.tensor_tensor_scan(rank, mask, zeros, rank0[:, ds(b, 1)], ALU.add, ALU.add))
                o.settle(passed_dve)
                o(nc.vector.copy_predicated(pos_f, mask, rank))
            o.total(done + 3 * NT)
            o(nc.vector.tensor_copy(pos_i[side], pos_f))
            o(nc.vector.tensor_copy(rec[side][:, :, 0], key_f))

        def scatter(pool, side, ring_sem, done_sems):
            f = REC[side]
            half = LANES // 2
            def turn(it, first):
                for h in range(2):
                    if not first:
                        pool.wait_ge(done_sems[h], it * (16 * half))
                    nc.gpsimd.tensor_copy(pos_ring[:, h * half:(h + 1) * half],
                                          pos_i[side][:, ds(it * LANES + h * half, half)]).then_inc(ring_sem, 1)
                    nc.gpsimd.tensor_copy(rec_ring[:, h * half * f:(h + 1) * half * f],
                                          rec[side].rearrange("p t f -> p (t f)")[:, ds((it * LANES + h * half) * f, half * f)])\
                        .then_inc(ring_sem, 1)
                    pool.wait_ge(ring_sem, it * 4 + 2 * h + 2)
                    pool.sem_inc(passed_pool, 1)
                    for k in range(h * half, (h + 1) * half):
                        pool.indirect_dma_start(
                            rec_dram[side], bass.IndirectOffsetOnAxis(pos_ring[:, k:k + 1], 0),
                            rec_ring[:, k * f:(k + 1) * f], None).then_inc(done_sems[h], 16)

            turn(0, True)
            with pool.Fori(1, COLS // LANES) as it:
                turn(it, False)
            for h in range(2):
                pool.wait_ge(done_sems[h], 16 * half * (COLS // LANES))

        with ExitStack() as c:
            sem = nc.alloc_semaphore
            padded, edges_in, dst_in, consts, order, counted, cum, stt = (
                sem(n) for n in ("padded", "edges_in", "dst_in", "consts", "order", "counted", "cum", "affine"))
            w_in_sem, wt_done, wt_copied = sem("weights_in"), sem("w_transposed"), sem("w_copied")
            block = c.enter_context(nc.Block())

            @block.sync
            def _(sp):
                sp.wait_ge(padded, 4)
                def load(dst_ap, flat, s):
                    sp.dma_start(dst_ap[0:FULL, :], flat[0:FULL * COLS].rearrange("(p t) -> p t", t=COLS)).then_inc(s, 16)
                    sp.dma_start(dst_ap[FULL:FULL + 1, 0:REST], flat[FULL * COLS:EDGES].rearrange("(p t) -> p t", p=1)).then_inc(s, 16)
                load(src_i, src, edges_in)
                load(dst_i, dst, edges_in)
                load(rel_i, edge_type_32, dst_in)
                load(w_in, edge_weight1.rearrange("e o -> (e o)"), dst_in)

            @block.scalar
            def _(act):
                for i, w in enumerate((L0_gnn_W0, L0_gnn_W1)):
                    act.dma_start(w_raw[:, i, :, :], w.rearrange("(k p) d -> p k d", p=P)).then_inc(w_in_sem, 16)
                for w, to in ((L1_gnn_W, w_gcn[:, :, :]), (L2_gnn_W_self, w_maxk[:, :, 0:D]), (L2_gnn_W_neigh, w_maxk[:, :, D:2 * D])):
                    act.dma_start(to, w.rearrange("(k p) d -> p k d", p=P)).then_inc(w_in_sem, 16)
                for i, row in enumerate((L0_gnn_b0, L0_gnn_g0, L0_gnn_beta0, L0_gnn_b1, L0_gnn_g1, L0_gnn_beta1)):
                    act.dma_start(rows6[:, i, :], row.rearrange("(o d) -> o d", o=1).to_broadcast([P, D])).then_inc(w_in_sem, 16)
                with nc.allow_non_contiguous_dma(reason="a table of 1 KB, once"):
                    act.dma_start(comp_t[:, :], L3_gnn_w_comp.rearrange("r b -> b r")).then_inc(w_in_sem, 16)
                act.wait_ge(w_in_sem, 16 * 12)
                for i in range(2):
                    act.wait_ge(wt_done, i + 1)
                    nc.scalar.copy(w_sage[i][:, :, :].rearrange("p k d -> p (k d)"), psum[:, 4 + i, :]).then_inc(wt_copied, 1)

            @block.gpsimd
            def _(pool):
                nc.gpsimd.memset(src_i, PAD_KEY).then_inc(padded, 1)
                nc.gpsimd.memset(dst_i, PAD_KEY).then_inc(padded, 1)
                nc.gpsimd.memset(rel_i, 0).then_inc(padded, 1)
                nc.gpsimd.memset(w_in, 0.0).then_inc(padded, 1)
                nc.gpsimd.iota(iota_t[:, :], [[1, NT]], base=0, channel_multiplier=0,
                               allow_small_or_imprecise_dtypes=True).then_inc(consts, 1)
                nc.gpsimd.iota(iota_p[:, :], [[1, P]], base=0, channel_multiplier=0,
                               allow_small_or_imprecise_dtypes=True).then_inc(consts, 1)
                nc.gpsimd.iota(iota_bf[:, :], [[1, P]], base=0, channel_multiplier=0,
                               allow_small_or_imprecise_dtypes=True).then_inc(consts, 1)
                nc.gpsimd.iota(edge_no, [[1, COLS]], base=0, channel_multiplier=COLS,
                               allow_small_or_imprecise_dtypes=True).then_inc(consts, 1)
                nc.gpsimd.memset(zeros, 0.0).then_inc(consts, 1)
                nc.gpsimd.memset(ones[:, :], 1.0).then_inc(consts, 1)
                nc.gpsimd.memset(ident[:, :], 0.0).then_inc(stt, 1)
                nc.gpsimd.memset(first_row_of[:, :], 0.0).then_inc(stt, 1)
                nc.gpsimd.memset(before[:, :], 1.0).then_inc(stt, 1)
                pool.wait_ge(stt, 3)
                nc.gpsimd.memset(first_row_of[0:1, :], 1.0).then_inc(consts, 1)
                nc.gpsimd.affine_select(out=ident[:, :], in_=ident[:, :], compare_op=ALU.not_equal, fill=1.0, base=0,
                                        pattern=[[-1, P]], channel_multiplier=1).then_inc(consts, 1)
                nc.gpsimd.affine_select(out=before[:, :], in_=before[:, :], compare_op=ALU.is_gt, fill=0.0, base=0,
                                        pattern=[[1, P]], channel_multiplier=-1).then_inc(consts, 1)

            @block.tensor
            def _(pe):
                pe.wait_ge(consts, 9)
                pe.wait_ge(w_in_sem, 16 * 12)
                for i in range(2):
                    for ki in range(2):
                        for ko in range(2):
                            ins = nc.tensor.transpose(psum[:, 4 + i, ki * D + ko * P:ki * D + (ko + 1) * P],
                                                      w_raw[:, i, ko, ki * P:(ki + 1) * P], ident[:, :])
                    ins.then_inc(wt_done, 1)
                pe.wait_ge(counted, 1)
                nc.tensor.matmul(cum_off, before[:, :], counts, start=True, stop=True)
                nc.tensor.matmul(cum_tot, ones[:, :], counts, start=True, stop=True).then_inc(cum, 1)

            @block.vector
            def _(dve):
                o = Chain(dve, order)
                dve.wait_ge(consts, 9)
                dve.wait_ge(edges_in, 64)
                sort_positions(dve, o, "s", counted, cum)
                o(nc.vector.tensor_copy(rec["s"][:, :, 1], dst_i))
                dve.wait_ge(dst_in, 64)
                dve.wait_ge(wt_copied, 2)

        with ExitStack() as c:
            sem = nc.alloc_semaphore
            order, counted, cum, hot, deg_done, rec_ready, rec_out = (
                sem(n) for n in ("order2", "counted2", "cum2", "hot", "deg_done", "rec_ready", "rec_out"))
            ring_sem = sem("ring_filled")
            scattered = [sem("scattered0"), sem("scattered1")]
            base_in = [sem("base_in0"), sem("base_in1")]
            relw_out = [sem("relw_out0"), sem("relw_out1")]
            relw_mm, relw_cp, rooted, degs = sem("relw_mm"), sem("relw_cp"), sem("rooted"), sem("degrees")
            block = c.enter_context(nc.Block())
            CH = 2048
            N_CH = D * D // CH
            HALVES = COLS // 4
            bases_flat = L3_gnn_bases.rearrange("b i o -> b (i o)")

            @block.gpsimd
            def _(pool):
                scatter(pool, "s", ring_sem, scattered)

            @block.sync
            def _(sp):
                with sp.Fori(0, N_CH // 2) as it:
                    for h in range(2):
                        sp.wait_ge(relw_mm, (it * 2 + h) * 4 + 4)
                        sp.dma_start(base_ring[0:BASES, h, :], bases_flat[:, ds((it * 2 + h) * CH, CH)]).then_inc(base_in[h], 16)
                sp.wait_ge(rec_ready, 1)
                sp.dma_start(rec_dram["d"].rearrange("(p t) f -> p (t f)", p=P), rec["d"].rearrange("p t f -> p (t f)")).then_inc(rec_out, 16)
                sp.wait_ge(rec_out, 16)

            @block.scalar
            def _(act):
                act.sem_inc(relw_cp, 4)
                for h in range(2):
                    act.sem_inc(relw_out[h], 16)
                with act.Fori(0, N_CH // 2) as it:
                    for h in range(2):
                        act.wait_ge(relw_out[h], it * 16 + 16)
                        for q in range(4):
                            act.wait_ge(relw_mm, (it * 2 + h) * 4 + q + 9)
                            nc.scalar.copy(relw_ring[0:RELS, h, q * 512:(q + 1) * 512], psum[0:RELS, 4 + q, :]).then_inc(relw_cp, 1)
                        act.wait_ge(relw_cp, (it * 2 + h) * 4 + 8)
                        act.dma_start(rel_w[:, ds((it * 2 + h) * CH, CH)], relw_ring[0:RELS, h, :]).then_inc(relw_out[h], 16)
                for h in range(2):
                    act.wait_ge(relw_out[h], 16 * (N_CH // 2) + 16)
                act.wait_ge(degs, 1)
                nc.scalar.activation(dis[:, :], small[:, 0, :], ACT.Sqrt).then_inc(rooted, 1)

            @block.tensor
            def _(pe):
                pe.sem_inc(relw_mm, 8)
                pe.wait_ge(counted, 1)
                nc.tensor.matmul(cum_off, before[:, :], counts, start=True, stop=True)
                nc.tensor.matmul(cum_tot, ones[:, :], counts, start=True, stop=True).then_inc(cum, 1)
                with pe.Fori(0, N_CH // 2) as it:
                    for h in range(2):
                        pe.wait_ge(base_in[h], it * 16 + 16)
                        for q in range(4):
                            pe.wait_ge(relw_cp, (it * 2 + h) * 4 + q + 1)
                            pe.sem_inc(passed_pe, 1)
                            nc.tensor.matmul(psum[0:RELS, 4 + q, :], comp_t[:, :], base_ring[0:BASES, h, q * 512:(q + 1) * 512],
                                             start=True, stop=True).then_inc(relw_mm, 1)
                pe.sem_inc(deg_done, 2)

                def count_half(side, n, h, first, last, base):
                    pe.wait_ge(hot, 2 * (base + n + 1))
                    for col in range(4):
                        ins = nc.tensor.matmul(deg_ps[side], low_hot[:, h, col, :], tile_hot[:, h, col, :],
                                               start=first and col == 0, stop=last and col == 3)
                    ins.then_inc(deg_done, 1)

                for s, side in enumerate("ds"):
                    for h in range(2):
                        count_half(side, h, h, h == 0, False, s * HALVES)
                    with pe.Fori(1, HALVES // 2 - 1) as it:
                        for h in range(2):
                            count_half(side, it * 2 + h, h, False, False, s * HALVES)
                    for h in range(2):
                        count_half(side, HALVES - 2 + h, h, False, h == 1, s * HALVES)

            @block.vector
            def _(dve):
                o = Chain(dve, order)
                sort_positions(dve, o, "d", counted, cum)
                o(nc.vector.tensor_copy(rec["d"][:, :, 1], src_i))
                o(nc.vector.scalar_tensor_tensor(rec["d"][:, :, 2], rec["d"][:, :, 1], float(RELS), rel_i, ALU.mult, ALU.add))
                o(nc.vector.tensor_copy(rec["d"][:, :, 3], w_in))
                o(nc.vector.tensor_tensor(rank, pos_f, edge_no, ALU.not_equal))
                o(nc.vector.tensor_reduce(moved[:, :], rank, AX.X, ALU.add))
                dve.sem_inc(rec_ready, 1)
                for s, side in enumerate("ds"):
                    with dve.Fori(0, HALVES // 2) as it:
                        for h in range(2):
                            col = it * 8 + h * 4
                            dve.wait_ge(deg_done, it * 2 + (s * HALVES + h + 1))
                            nc.vector.tensor_tensor(
                                low_hot[:, h, :, :], low_f[side][:, ds(col, 4)].unsqueeze(2).to_broadcast([P, 4, P]),
                                iota_bf[:, :].unsqueeze(1).to_broadcast([P, 4, P]), ALU.is_equal).then_inc(hot, 1)
                            nc.vector.tensor_tensor(
                                tile_hot[:, h, :, :], tile_f[side][:, ds(col, 4)].unsqueeze(2).to_broadcast([P, 4, NT]),
                                iota_t[:, :].unsqueeze(1).to_broadcast([P, 4, NT]), ALU.is_equal).then_inc(hot, 1)
                dve.wait_ge(deg_done, 2 * HALVES + 2)
                done = o.base + o.n
                o.total(done)
                o(nc.vector.tensor_scalar(small[:, 0, :], deg_ps["d"], 1.0, None, ALU.max))
                dve.sem_inc(degs, 1)
                o(nc.vector.tensor_scalar(small[:, 1, :], deg_ps["d"], 0.0, None, ALU.is_gt))
                o(nc.vector.tensor_scalar(small[:, 2, :], deg_ps["s"], 1.0, None, ALU.max))
                o(nc.vector.reciprocal(rdeg_d[:, :], small[:, 0, :]))
                o(nc.vector.reciprocal(rdeg_s[:, :], small[:, 2, :]))
                dve.wait_ge(rooted, 1)
                o(nc.vector.reciprocal(small[:, 3, :], dis[:, :]))
                o(nc.vector.tensor_tensor(dis[:, :], small[:, 3, :], small[:, 1, :], ALU.mult))

        with ExitStack() as c:
            sem = nc.alloc_semaphore
            order, flag_mm, flag_ready, rows_ready, tiles_ready, ordered = (
                sem(n) for n in ("order3", "flag_mm", "flag_ready", "rows_ready", "tiles_ready", "ordered"))
            ring_sem = sem("ring_filled3")
            scattered = [sem("scattered30"), sem("scattered31")]
            rows_in = [sem("rows_in0"), sem("rows_in1")]
            tp, cp, pcon = sem("fields_transposed"), sem("fields_copied"), sem("pair_iota")
            x_in = sem("x_in")
            block = c.enter_context(nc.Block())
            PC = PAIR_COLS
            pair_no = small[:, 7, 0:PC]
            pair_tile = {"s": small[:, 5, 0:PC], "d": small[:, 6, 0:PC]}
            rows_buf = work[:, ring0:ring0 + 2 * 512].rearrange("p (h n) -> p h n", h=2)
            tile_wide = work[:, ring0 + 1024:ring0 + 1024 + 2 * PC * P].rearrange("p (c j) -> p c j", j=P)
            tile_row = work[:, ring0 + 1024 + 2 * PC * P:ring0 + 1024 + 3 * PC * P]
            units = [(side, col) for side in "ds" for col in range(PC)]

            @block.gpsimd
            def _(pool):
                nc.gpsimd.iota(pair_no, [[P, PC]], base=0, channel_multiplier=1,
                               allow_small_or_imprecise_dtypes=True).then_inc(pcon, 1)
                pool.wait_ge(flag_ready, 1)
                n_moved = pool.value_load(moved_i[0:1, 0:1], min_val=0, max_val=P * COLS)
                with pool.If(n_moved > 0):
                    scatter(pool, "d", ring_sem, scattered)
                pool.sem_inc(ordered, 1)
                for u, (side, col) in enumerate(units):
                    f = REC[side]
                    pool.wait_ge(rows_ready, 1 if side == "d" else 2)
                    if u >= 2:
                        pool.wait_ge(tp, u - 1)
                    pool.indirect_dma_start(rows_buf[:, u % 2, 0:P * f], None,
                                            rec_dram[side].rearrange("(r j) f -> r (j f)", j=P),
                                            bass.IndirectOffsetOnAxis(row_i[side][:, col:col + 1], 0)).then_inc(rows_in[u % 2], 16)

            @block.tensor
            def _(pe):
                nc.tensor.matmul(psum[:, 0, 0:1], ones[:, :], moved[:, :], start=True, stop=True).then_inc(flag_mm, 1)
                for u, (side, col) in enumerate(units):
                    f = REC[side]
                    pe.wait_ge(rows_in[u % 2], 16 * (u // 2 + 1))
                    pe.wait_ge(tiles_ready, u + 1)
                    if u >= 2:
                        pe.wait_ge(cp, u - 1)
                    rows = rows_buf[:, u % 2, 0:P * f].rearrange("p (j f) -> p j f", f=f)
                    for k in range(f):
                        nc.tensor.transpose(psum[:, 2 + 2 * (u % 2), k * P:(k + 1) * P], rows[:, :, k], ident[:, :])
                    nc.tensor.matmul(psum[:, 3 + 2 * (u % 2), 0:P], tile_wide[:, u, :], ident[:, :],
                                     start=True, stop=True).then_inc(tp, 1)

            @block.vector
            def _(dve):
                o = Chain(dve, order)
                dve.wait_ge(flag_mm, 1)
                o(nc.vector.tensor_copy(moved_i[:, :], psum[:, 0, 0:1]))
                dve.sem_inc(flag_ready, 1)
                dve.wait_ge(pcon, 1)
                n_b = TILES
                for side in "ds":
                    first_row, last_row, pair_end, shift, step = (small[:, k, 0:n_b] for k in range(5))
                    o(nc.vector.tensor_copy(small_i[:, 0, 0:n_b], starts[side][:, 0:n_b]))
                    o(nc.vector.tensor_scalar(small_i[:, 0, 0:n_b], small_i[:, 0, 0:n_b], 7, None, ALU.arith_shift_right))
                    o(nc.vector.tensor_copy(first_row, small_i[:, 0, 0:n_b]))
                    o(nc.vector.tensor_scalar(last_row, ends[side][:, 0:n_b], -1.0, None, ALU.add))
                    o(nc.vector.tensor_copy(small_i[:, 0, 0:n_b], last_row))
                    o(nc.vector.tensor_scalar(small_i[:, 0, 0:n_b], small_i[:, 0, 0:n_b], 7, None, ALU.arith_shift_right))
                    o(nc.vector.tensor_copy(last_row, small_i[:, 0, 0:n_b]))
                    o(nc.vector.tensor_tensor(last_row, last_row, first_row, ALU.subtract))
                    o(nc.vector.tensor_scalar(step, tot[side][:, 0:n_b], 0.0, None, ALU.is_gt))
                    o(nc.vector.scalar_tensor_tensor(last_row, last_row, 1.0, step, ALU.add, ALU.mult))
                    o(nc.vector.tensor_tensor_scan(pair_end, last_row, zeros[:, 0:n_b], 0.0, ALU.add, ALU.add))
                    o(nc.vector.tensor_tensor(shift, first_row, pair_end, ALU.subtract))
                    o(nc.vector.tensor_tensor(shift, shift, last_row, ALU.add))
                    o(nc.vector.tensor_tensor(step[:, 0:n_b - 1], shift[:, 1:n_b], shift[:, 0:n_b - 1], ALU.subtract))
                    o(nc.vector.tensor_scalar(step[:, n_b - 1:n_b], shift[:, n_b - 1:n_b], -1.0, None, ALU.mult))
                    for col in range(PC):
                        o(nc.vector.tensor_scalar(first_row, pair_end, pair_no[:, col:col + 1], 0.0, ALU.is_le, ALU.add,
                                                  accum_out=pair_tile[side][:, col:col + 1]))
                        o(nc.vector.tensor_tensor(last_row, first_row, step, ALU.mult))
                        o(nc.vector.tensor_reduce(row_f[:, col:col + 1], last_row, AX.X, ALU.add))
                    o(nc.vector.tensor_scalar(row_f[:, :], row_f[:, :], shift[:, 0:1], None, ALU.add))
                    o(nc.vector.tensor_tensor(row_f[:, :], row_f[:, :], pair_no, ALU.add))
                    o(nc.vector.tensor_scalar(row_f[:, :], row_f[:, :], float(ROWS - 1), 0.0, ALU.min, ALU.max))
                    o(nc.vector.tensor_copy(row_i[side][:, :], row_f[:, :]))
                    dve.sem_inc(rows_ready, 1)
                for u, (side, col) in enumerate(units):
                    o(nc.vector.tensor_copy(tile_wide[:, u, :], pair_tile[side][:, col:col + 1].to_broadcast([P, P])))
                    dve.sem_inc(tiles_ready, 1)
                for u, (side, col) in enumerate(units):
                    here = slice(col * P, (col + 1) * P)
                    tile_ps = psum[:, 3 + 2 * (u % 2), 0:P]
                    field = lambda k: psum[:, 2 + 2 * (u % 2), k * P:(k + 1) * P]
                    dve.wait_ge(tp, u + 1)
                    o(nc.vector.tensor_copy(tile_row[:, here], tile_ps))
                    o(nc.vector.scalar_tensor_tensor(loc[side][:, here], tile_row[:, here], -float(P), field(0), ALU.mult, ALU.add))
                    o(nc.vector.tensor_scalar(off[side][:, here], tile_row[:, here], float(D), None, ALU.mult))
                    if side == "s":
                        o(nc.vector.tensor_scalar(idx_s[:, here], field(1), float(NODES - 1), None, ALU.min))
                    else:
                        o(nc.vector.tensor_scalar(idx_d[:, here], field(1), float(NODES - 1), None, ALU.min))
                        o(nc.vector.tensor_copy(idx_rel[:, here], field(2)))
                        o(nc.vector.tensor_copy(weight[:, here], field(3)))
                    dve.sem_inc(cp, 1)
                o(nc.vector.memset(state[:, (TILES - 1) * D:], 0.0))
                dve.sem_inc(cp, 1)

            @block.sync
            def _(sp):
                sp.wait_ge(cp, len(units) + 1)
                sp.dma_start(state[:, 0:(TILES - 1) * D].rearrange("p (t d) -> p t d", d=D),
                             x[0:(TILES - 1) * P, :].rearrange("(t p) d -> p t d", p=P)).then_inc(x_in, 16)
                sp.dma_start(state[0:LAST_ROWS, (TILES - 1) * D:TILES * D], x[(TILES - 1) * P:NODES, :]).then_inc(x_in, 16)
                sp.wait_ge(x_in, 32)

        def tile_of(buf, i, n=1):
            return buf[:, ds(i * D, n * D)]

        def aggregate(turn, rows_dram, side, idx, w=None):
            q0 = turn * GROUPS
            first = turn == 0
            products = psum[:, :, :].rearrange("p b (s d) -> p (b s) d", d=D)
            with nc.Block() as block:
                @block.gpsimd
                def _(pool):
                    with pool.Fori(0, PAIRS // (4 * LANES)) as it:
                        for h in range(4):
                            nc.gpsimd.tensor_copy(idx_ring[:, h * LANES:(h + 1) * LANES],
                                                  idx[:, ds(it * (4 * LANES) + h * LANES, LANES)]).then_inc(idx_filled, 1)
                            pool.wait_ge(idx_filled, it * 4 + (turn * PAIRS // LANES + h + 1))
                            for g in range(h * LANES // GROUP, (h + 1) * LANES // GROUP):
                                pool.wait_ge(multiplied_sums, it * (4 * LANES // GROUP) + (q0 + g + 1))
                                pool.sem_inc(passed_pool, 1)
                                for k in range(GROUP):
                                    slot = g % RING * GROUP + k
                                    lane = g * GROUP + k
                                    pool.indirect_dma_start(gathered[:, slot, :], None, rows_dram,
                                                            bass.IndirectOffsetOnAxis(idx_ring[:, lane:lane + 1], 0))\
                                        .then_inc(landed[g % RING], 16)

                @block.tensor
                def _(pe):
                    if first:
                        pe.sem_inc(multiplied_sums, CREDIT)
                    with pe.Fori(0, GROUPS // RING) as it:
                        for g in range(RING):
                            pe.wait_ge(landed[g], it * (16 * GROUP) + 16 * GROUP * (q0 // RING + 1))
                            pe.wait_ge(hot_ready, it * RING + (q0 + g + 1))
                            pe.wait_ge(added_sums, it * (RING * GROUP) + (q0 + g + 1) * GROUP)
                            for k in range(GROUP):
                                slot = g % OH_RING * GROUP + k
                                ins = nc.tensor.matmul(products[:, slot, :], onehot[:, slot, :],
                                                       gathered[:, g * GROUP + k, :], start=True, stop=True)
                            ins.then_inc(multiplied_sums, 1)

                @block.vector
                def _(dve):
                    nc.vector.memset(sums, 0.0).then_inc(zeroed, 1)
                    dve.wait_ge(zeroed, turn + 1)
                    if first:
                        dve.sem_inc(added_sums, OH_RING * GROUP)

                    def make_onehot(q, g):
                        hot = onehot[:, g * GROUP:(g + 1) * GROUP, :]
                        dve.wait_ge(multiplied_sums, q + (q0 + 1 + CREDIT - OH_RING))
                        if w is None:
                            nc.vector.tensor_tensor(
                                hot, loc[side][:, ds(q * GROUP, GROUP)].unsqueeze(2).to_broadcast([P, GROUP, P]),
                                iota_p[:, :].unsqueeze(1).to_broadcast([P, GROUP, P]), ALU.is_equal).then_inc(hot_ready, 1)
                            return
                        for k in range(GROUP):
                            ins = nc.vector.tensor_scalar(hot[:, k, :], iota_p[:, :], loc[side][:, ds(q * GROUP + k, 1)],
                                                          w[:, ds(q * GROUP + k, 1)], ALU.is_equal, ALU.mult)
                        ins.then_inc(hot_ready, 1)

                    def add_products(q, g):
                        _, at = nc.values_load_multi_w_load_instructions(
                            off[side][0:1, ds(q * GROUP, GROUP)], engines=[mybir.EngineType.DVE],
                            min_val=0, max_val=(NT - 1) * D)
                        dve.wait_ge(multiplied_sums, q + (q0 + 1 + CREDIT))
                        for k in range(GROUP):
                            dve.wait_ge(added_sums, q * GROUP + (q0 * GROUP + k + OH_RING * GROUP))
                            tile = sums[:, ds(at[k], D)]
                            nc.vector.tensor_tensor(tile, tile, products[:, g * GROUP + k, :], ALU.add).then_inc(added_sums, 1)

                    make_onehot(0, 0)
                    with dve.Fori(0, GROUPS // OH_RING - 1) as it:
                        for g in range(OH_RING):
                            make_onehot(it * OH_RING + g + 1, (g + 1) % OH_RING)
                            add_products(it * OH_RING + g, g)
                    for g in range(OH_RING):
                        if g < OH_RING - 1:
                            make_onehot(GROUPS - OH_RING + g + 1, g + 1)
                        add_products(GROUPS - OH_RING + g, g)
                    dve.wait_ge(added_sums, (q0 + GROUPS + OH_RING) * GROUP)

        def pipelined(eng, first, second, ahead=1):
            if ahead == 2:
                first(0, 0, None, 0)
                first(1, 1, None, 0)
                with eng.Fori(0, NT // 2 - 1) as it:
                    for b in range(2):
                        first(it * 2 + 2 + b, b, it, 0)
                        second(it * 2 + b, b, it, 0)
                for b in range(2):
                    second(NT - 2 + b, b, None, 0)
                return
            first(0, 0, None, 0)
            with eng.Fori(0, NT // 2 - 1) as it:
                first(it * 2 + 1, 1, it, 0)
                second(it * 2, 0, it, 0)
                first(it * 2 + 2, 0, it, 1)
                second(it * 2 + 1, 1, it, 1)
            first(NT - 1, 1, None, 1)
            second(NT - 2, 0, NT // 2 - 1, 0)
            second(NT - 1, 1, NT // 2 - 1, 1)

        def roots(dve, o, to_root, rooted, base, with_dis=False):
            even_mean, even_m2, odd_mean, odd_m2 = (stats[:, :, k] for k in (1, 2, 4, 5))
            apart, spread, both = small[:, 0, :], small[:, 1, :], small[:, 2, :]
            o(nc.vector.tensor_tensor(apart, even_mean, odd_mean, ALU.subtract))
            o(nc.vector.tensor_tensor(both, even_mean, odd_mean, ALU.add))
            o(nc.vector.tensor_scalar(mean[:, :], both, 0.5, None, ALU.mult))
            o(nc.vector.scalar_tensor_tensor(spread, apart, 0.25, apart, ALU.mult, ALU.mult))
            o(nc.vector.tensor_tensor(both, even_m2, odd_m2, ALU.add))
            o(nc.vector.scalar_tensor_tensor(spread, both, 1.0 / D, spread, ALU.mult, ALU.add))
            o(nc.vector.tensor_scalar(rstd[:, :], spread, EPS, None, ALU.add))
            dve.sem_inc(to_root, 1)
            dve.wait_ge(rooted, base)
            o(nc.vector.reciprocal(rstd[:, :], rstd[:, :]))
            o(nc.vector.scalar_tensor_tensor(shift[:, :], mean[:, :], -1.0, rstd[:, :], ALU.mult, ALU.mult))
            if with_dis:
                o(nc.vector.tensor_tensor(rstd_dis[:, :], rstd[:, :], dis[:, :], ALU.mult))
                o(nc.vector.tensor_tensor(shift_dis[:, :], shift[:, :], dis[:, :], ALU.mult))

        def root(act, to_root, rooted, base):
            act.wait_ge(to_root, base)
            nc.scalar.activation(rstd[:, :], rstd[:, :], ACT.Sqrt).then_inc(rooted, 1)

        def sums_to_state(dve, kind, added, counted):
            with dve.Fori(0, NT // 2) as it:
                for b in range(2):
                    i = it * 2 + b
                    if kind == "mean":
                        ins = nc.vector.scalar_tensor_tensor(tile_of(state, i), tile_of(sums, i), rdeg_d[:, ds(i, 1)],
                                                             tile_of(state, i), ALU.mult, ALU.add)
                    else:
                        ins = nc.vector.scalar_tensor_tensor(tile_of(state, i), tile_of(sums, i), 0.0,
                                                             tile_of(state, i), ALU.max, ALU.add)
                    ins.then_inc(added, 1)
                for b in range(2):
                    i = it * 2 + b
                    dve.wait_ge(added, i + 1)
                    dve.sem_inc(passed_dve, 1)
                    nc.vector.bn_stats(stats[:, ds(i, 1), :].rearrange("p t m -> p (t m)"), tile_of(state, i)).then_inc(counted, 1)
            dve.wait_ge(counted, NT)

        def transform(name, kind, weights, bias=None, rdeg=None):
            sem = lambda n: nc.alloc_semaphore(f"{n}_{name}")
            made, transposed, copied, multiplied, used, counted = (
                sem(n) for n in ("made", "transposed", "copied", "multiplied", "used", "counted"))
            tp = psum[:, 0:2, 0:D]
            result = sums if kind == "sage" else state
            with nc.Block() as block:
                @block.vector
                def _(dve):
                    if kind == "gcn":
                        dve.sem_inc(used, 2)

                    def make(i, b, it, n):
                        dve.wait_ge(transposed, i + 1)
                        if kind == "sage":
                            nc.vector.scalar_tensor_tensor(operand[:, b, :], tile_of(sums, i), rdeg[:, ds(i, 1)],
                                                           tile_of(state, i), ALU.mult, ALU.add).then_inc(made, 1)
                        else:
                            nc.vector.tensor_scalar(operand[:, b, :], tile_of(sums, i), dis[:, ds(i, 1)],
                                                    None, ALU.mult).then_inc(made, 1)

                    def use(i, b, it, n):
                        if kind == "gcn":
                            dve.wait_ge(multiplied, i + 3)
                            nc.vector.tensor_tensor(tile_of(state, i), psum[:, 2 + b, 0:D], tile_of(state, i),
                                                    ALU.add).then_inc(used, 1)
                        dve.wait_ge(used, i + 3)
                        dve.sem_inc(passed_dve, 1)
                        nc.vector.bn_stats(stats[:, ds(i, 1), :].rearrange("p t m -> p (t m)"), tile_of(result, i)).then_inc(counted, 1)

                    pipelined(dve, make, use, ahead=2)
                    dve.wait_ge(counted, NT)

                @block.scalar
                def _(act):
                    act.sem_inc(copied, 2)
                    if kind == "sage":
                        act.sem_inc(used, 2)

                    def copy_turned(i, b, it, n):
                        act.wait_ge(transposed, i + 3)
                        act.wait_ge(multiplied, i + 1)
                        nc.scalar.copy(operandT[:, b, :], tp[:, b, :]).then_inc(copied, 1)

                    def copy_result(i, b, it, n):
                        if kind == "sage":
                            act.wait_ge(multiplied, i + 3)
                            nc.scalar.copy(tile_of(sums, i), psum[:, 2 + b, 0:D]).then_inc(used, 1)

                    pipelined(act, copy_turned, copy_result)

                @block.tensor
                def _(pe):
                    pe.sem_inc(transposed, 2)
                    pe.sem_inc(multiplied, 2)

                    def turn(i, b, it, n):
                        pe.wait_ge(made, i + 1)
                        pe.wait_ge(copied, i + 1)
                        for k in range(2):
                            ins = nc.tensor.transpose(tp[:, b, k * P:(k + 1) * P], operand[:, b, k * P:(k + 1) * P], ident[:, :])
                        ins.then_inc(transposed, 1)

                    def multiply(i, b, it, n):
                        pe.wait_ge(copied, i + 3)
                        pe.wait_ge(used, i + 1)
                        for k in range(2):
                            ins = nc.tensor.matmul(psum[:, 2 + b, 0:D], operandT[:, b, k * P:(k + 1) * P],
                                                   weights[:, k, :], start=k == 0, stop=k == 1 and bias is None)
                        if bias is not None:
                            ins = nc.tensor.matmul(psum[:, 2 + b, 0:D], first_row_of[:, :], bias, start=False, stop=True)
                        ins.then_inc(multiplied, 1)

                    pipelined(pe, turn, multiply)

        def max_k():
            sem = lambda n: nc.alloc_semaphore(f"{n}_maxk")
            order, to_root, rooted, scales, made, transposed, copied, multiplied, added, dense_in, sparse_ready = (
                sem(n) for n in ("order", "to_root", "rooted", "scales", "made", "transposed", "copied", "multiplied",
                                 "added", "dense_in", "sparse_ready"))
            stored = [sem(f"stored{s}") for s in range(4)]
            tp = psum[:, 0:2, 0:D]
            normed, turned, dense, sparse, left = (gathered[:, s:s + 4, :] for s in (0, 4, 8, 12, 16))
            LOWEST = -3.4028235e38
            COUPLES = NT // 2

            def couples(eng, first, second):
                first(0, 0)
                with eng.Fori(0, COUPLES // 2) as it:
                    first(it * 2 + 1, 1)
                    second(it * 2, 0)
                    first(it * 2 + 2, 0)
                    second(it * 2 + 1, 1)
                second(COUPLES - 1, 0)

            with nc.Block() as block:
                @block.vector
                def _(dve):
                    o = Chain(dve, order)
                    roots(dve, o, to_root, rooted, 1)
                    dve.sem_inc(scales, 1)
                    dve.sem_inc(added, 4)
                    dve.sem_inc(sparse_ready, 4)
                    done = o.base + o.n
                    steps = 4 * 2 * 2

                    def largest(c, h):
                        for b in range(2):
                            i = c * 2 + b
                            dve.wait_ge(multiplied, i + 5)
                            nc.vector.tensor_tensor(tile_of(state, i), psum[:, 2 + b, 0:D], normed[:, 2 * h + b, :],
                                                    ALU.add).then_inc(added, 1)
                        at = c * steps + done
                        n = 0
                        for r in range(4):
                            for b in range(2):
                                if r == 0:
                                    dve.wait_ge(dense_in, c * 2 + (b + 3))
                                else:
                                    dve.wait_ge(order, at + (n - 1))
                                dve.sem_inc(passed_dve, 1)
                                nc.vector.max(top8[:, b, :], dense[:, 2 * h + b, :] if r == 0 else left[:, b, :]).then_inc(order, 1)
                                n += 1
                            for b in range(2):
                                dve.wait_ge(order, at + (n - 1))
                                dve.sem_inc(passed_dve, 1)
                                nc.vector.match_replace(left[:, b, :], top8[:, b, :],
                                                        dense[:, 2 * h + b, :] if r == 0 else left[:, b, :],
                                                        LOWEST).then_inc(order, 1)
                                n += 1
                        for b in range(2):
                            dve.wait_ge(stored[2 * h + b], c * 8 + (16 - 8 * h))
                            dve.wait_ge(order, at + (n - 1 + b))
                            nc.vector.scalar_tensor_tensor(sparse[:, 2 * h + b, :], left[:, b, :], LOWEST,
                                                           dense[:, 2 * h + b, :], ALU.is_equal, ALU.mult).then_inc(sparse_ready, 1)

                    with dve.Fori(0, COUPLES // 2) as it:
                        for h in range(2):
                            largest(it * 2 + h, h)
                    largest(COUPLES - 1, 0)

                @block.scalar
                def _(act):
                    root(act, to_root, rooted, 1)
                    act.sem_inc(copied, 2)
                    act.sem_inc(dense_in, 2)
                    act.wait_ge(scales, 1)

                    def norm_and_turn(c, h):
                        for b in range(2):
                            i = c * 2 + b
                            act.wait_ge(added, i + 1)
                            nc.scalar.activation(normed[:, 2 * h + b, :], tile_of(state, i), ACT.Identity,
                                                 bias=shift[:, ds(i, 1)], scale=rstd[:, ds(i, 1)]).then_inc(made, 1)
                        for b in range(2):
                            i = c * 2 + b
                            act.wait_ge(transposed, i + 1)
                            act.wait_ge(multiplied, i + 1)
                            nc.scalar.copy(turned[:, 2 * h + b, :], tp[:, b, :]).then_inc(copied, 1)

                    def dense_out(c, h):
                        for b in range(2):
                            i = c * 2 + b
                            act.wait_ge(multiplied, i + 5)
                            act.wait_ge(sparse_ready, i + 1)
                            nc.scalar.copy(dense[:, 2 * h + b, :], psum[:, 4 + b, 0:D]).then_inc(dense_in, 1)

                    couples(act, norm_and_turn, dense_out)

                @block.tensor
                def _(pe):
                    pe.sem_inc(multiplied, 4)

                    def turn(c, h):
                        for b in range(2):
                            i = c * 2 + b
                            pe.wait_ge(made, i + 1)
                            pe.wait_ge(copied, i + 1)
                            for k in range(2):
                                ins = nc.tensor.transpose(tp[:, b, k * P:(k + 1) * P], normed[:, 2 * h + b, k * P:(k + 1) * P],
                                                          ident[:, :])
                            ins.then_inc(transposed, 1)

                    def multiply(c, h):
                        for b in range(2):
                            i = c * 2 + b
                            pe.wait_ge(copied, i + 3)
                            pe.wait_ge(added, i + 3)
                            pe.wait_ge(dense_in, i + 1)
                            for half in range(2):
                                for k in range(2):
                                    ins = nc.tensor.matmul(psum[:, 2 + 2 * half + b, 0:D], turned[:, 2 * h + b, k * P:(k + 1) * P],
                                                           w_maxk[:, k, half * D:(half + 1) * D], start=k == 0, stop=k == 1)
                            ins.then_inc(multiplied, 1)

                    couples(pe, turn, multiply)

                @block.sync
                def _(sp):
                    for s in range(4):
                        sp.sem_inc(stored[s], 16)

                    def store(c, h):
                        for b in range(2):
                            i = c * 2 + b
                            sp.wait_ge(sparse_ready, i + 5)
                            sp.dma_start(table[2][ds(i * P, P), :], sparse[:, 2 * h + b, :]).then_inc(stored[2 * h + b], 16)

                    with sp.Fori(0, COUPLES // 2) as it:
                        for h in range(2):
                            store(it * 2 + h, h)
                    store(COUPLES - 1, 0)
                    for s in range(4):
                        sp.wait_ge(stored[s], 16 * (COUPLES // 2 + 1 - s // 2) + 16)

        CHUNK = 5
        N_CHUNKS = NT // CHUNK

        def chunk_of(buf, c, n=CHUNK):
            return buf[:, ds(c * CHUNK * D, n * D)]

        def rows_of(buf):
            return buf.rearrange("p (t d) -> p t d", d=D)

        def table_chunk(t, c):
            return t[ds(c * (CHUNK * P), CHUNK * P), :].rearrange("(t p) d -> p t d", p=P)

        def normalise_sage(name, g, beta, last):
            sem = lambda n: nc.alloc_semaphore(f"{n}_{name}")
            order, to_root, rooted, scales, normed, lit, stored, affine = (
                sem(n) for n in ("order", "to_root", "rooted", "scales", "normed", "lit", "stored", "affine"))
            if last:
                scaled, x_in, x_used, counted = sem("scaled"), [sem("x_in0"), sem("x_in1")], sem("x_used"), sem("counted")
            x_buf = work[:, ring0:ring0 + 2 * CHUNK * D].rearrange("p (b n) -> p b n", b=2)
            wide = [P, CHUNK, D]
            with nc.Block() as block:
                @block.scalar
                def _(act):
                    root(act, to_root, rooted, 1)
                    act.wait_ge(scales, 1)

                    def norm(c):
                        for k in range(CHUNK):
                            i = c * CHUNK + k
                            nc.scalar.activation(tile_of(sums, i), tile_of(sums, i), ACT.Identity, bias=shift[:, ds(i, 1)],
                                                 scale=rstd[:, ds(i, 1)]).then_inc(normed, 1)

                    def light(c):
                        act.wait_ge(affine, c * 2 + 2)
                        nc.scalar.activation(chunk_of(sums if last else state, c), chunk_of(sums, c), ACT.Silu).then_inc(lit, 1)

                    norm(0)
                    with act.Fori(0, N_CHUNKS - 1) as c:
                        norm(c + 1)
                        light(c)
                    light(N_CHUNKS - 1)
                    if last:
                        root(act, to_root, rooted, 2)
                        with act.Fori(0, NT) as i:
                            act.wait_ge(scaled, i + 1)
                            nc.scalar.activation(tile_of(state, i), tile_of(state, i), ACT.Identity, bias=shift[:, ds(i, 1)],
                                                 scale=rstd[:, ds(i, 1)])

                @block.vector
                def _(dve):
                    o = Chain(dve, order)
                    roots(dve, o, to_root, rooted, 1)
                    dve.sem_inc(scales, 1)
                    with dve.Fori(0, N_CHUNKS) as c:
                        part = rows_of(chunk_of(sums, c))
                        dve.wait_ge(normed, c * CHUNK + CHUNK)
                        nc.vector.tensor_tensor(part, part, g.unsqueeze(1).to_broadcast(wide), ALU.mult).then_inc(affine, 1)
                        dve.wait_ge(affine, c * 2 + 1)
                        nc.vector.tensor_tensor(part, part, beta.unsqueeze(1).to_broadcast(wide), ALU.add).then_inc(affine, 1)
                    if not last:
                        return
                    dve.sem_inc(x_used, 2)

                    def with_x(c, b):
                        dve.wait_ge(lit, c + 1)
                        nc.vector.tensor_tensor(chunk_of(state, c), chunk_of(sums, c), x_buf[:, b, :], ALU.add).then_inc(x_used, 1)
                        dve.wait_ge(x_used, c + 3)
                        for k in range(CHUNK):
                            i = c * CHUNK + k
                            dve.sem_inc(passed_dve, 1)
                            nc.vector.bn_stats(stats[:, ds(i, 1), :].rearrange("p t m -> p (t m)"), tile_of(state, i)).then_inc(counted, 1)

                    with dve.Fori(0, N_CHUNKS // 2 - 1) as it:
                        for b in range(2):
                            dve.wait_ge(x_in[b], it * 16 + 16)
                            with_x(it * 2 + b, b)
                    dve.wait_ge(x_in[0], 16 * (N_CHUNKS // 2))
                    with_x(N_CHUNKS - 2, 0)
                    dve.wait_ge(x_in[1], 16 * (N_CHUNKS // 2 + 1))
                    with_x(N_CHUNKS - 1, 1)
                    dve.wait_ge(counted, NT)
                    roots(dve, o, to_root, rooted, 2, with_dis=True)
                    with dve.Fori(0, NT) as i:
                        nc.vector.tensor_scalar(tile_of(sums, i), tile_of(state, i), rstd_dis[:, ds(i, 1)],
                                                shift_dis[:, ds(i, 1)], ALU.mult, ALU.add).then_inc(scaled, 1)

                @block.sync
                def _(sp):
                    if last:
                        with sp.Fori(0, N_CHUNKS // 2 - 1) as it:
                            for b in range(2):
                                sp.wait_ge(x_used, it * 2 + b + 1)
                                sp.dma_start(rows_of(x_buf[:, b, :]), table_chunk(x, it * 2 + b)).then_inc(x_in[b], 16)
                        sp.wait_ge(x_used, N_CHUNKS - 1)
                        sp.dma_start(rows_of(x_buf[:, 0, :]), table_chunk(x, N_CHUNKS - 2)).then_inc(x_in[0], 16)
                        sp.wait_ge(x_used, N_CHUNKS)
                        at = (N_CHUNKS - 1) * CHUNK
                        sp.dma_start(rows_of(x_buf[:, 1, 0:(TILES - 1 - at) * D]),
                                     x[at * P:(TILES - 1) * P, :].rearrange("(t p) d -> p t d", p=P)).then_inc(x_in[1], 16)
                        sp.dma_start(x_buf[0:LAST_ROWS, 1, (TILES - 1 - at) * D:(TILES - at) * D],
                                     x[(TILES - 1) * P:NODES, :]).then_inc(x_in[1], 16)
                    with sp.Fori(0, N_CHUNKS) as it:
                        if last:
                            sp.wait_ge(scaled, it * CHUNK + CHUNK)
                        else:
                            sp.wait_ge(lit, it + 1)
                        sp.dma_start(table_chunk(table[1 if last else 0], it),
                                     rows_of(chunk_of(sums if last else state, it))).then_inc(stored, 16)
                    sp.wait_ge(stored, 16 * N_CHUNKS)

        def last_norm():
            sem = lambda n: nc.alloc_semaphore(f"{n}_last")
            order, to_root, rooted, added, counted, normed, stored = (
                sem(n) for n in ("order", "to_root", "rooted", "added", "counted", "normed", "stored"))
            with nc.Block() as block:
                @block.scalar
                def _(act):
                    root(act, to_root, rooted, 1)

                @block.vector
                def _(dve):
                    sums_to_state(dve, "relu", added, counted)
                    roots(dve, Chain(dve, order), to_root, rooted, 1)
                    with dve.Fori(0, NT) as i:
                        nc.vector.tensor_scalar(tile_of(state, i), tile_of(state, i), rstd[:, ds(i, 1)],
                                                shift[:, ds(i, 1)], ALU.mult, ALU.add).then_inc(normed, 1)

                @block.sync
                def _(sp):
                    n = (TILES - 1) // 4
                    with sp.Fori(0, n) as it:
                        sp.wait_ge(normed, it * 4 + 4)
                        sp.dma_start(out[ds(it * (4 * P), 4 * P), :].rearrange("(t p) d -> p t d", p=P),
                                     rows_of(state[:, ds(it * (4 * D), 4 * D)])).then_inc(stored, 16)
                    sp.wait_ge(normed, TILES)
                    sp.dma_start(out[4 * n * P:NODES, :], state[0:LAST_ROWS, 4 * n * D:(4 * n + 1) * D]).then_inc(stored, 16)
                    sp.wait_ge(stored, 16 * (n + 1))

        def relation_table():
            sem = lambda n: nc.alloc_semaphore(f"{n}_rel")
            w_in, made, transposed, copied, tile_done, multiplied, order, to_root, rooted, scales, added, counted, normed = (
                sem(n) for n in ("w_in", "made", "transposed", "copied", "tile_done", "multiplied", "order", "to_root",
                                 "rooted", "scales", "added", "counted", "normed"))
            taken_by = {"dve": sem("taken_dve"), "act": sem("taken_act")}
            stored = [sem(f"stored{k}") for k in range(4)]
            w_all = work[:, 0:2 * RELS * D].rearrange("p (k n) -> p k n", k=2)
            st0 = 2 * RELS * D
            stage = work[:, st0:st0 + 4 * 1024].rearrange("p (s n) -> p s n", s=4)
            tp = psum[:, 0:2, 0:D]
            PARTS = RELS * D // 512
            SLOTS = 4
            with nc.Block() as block:
                @block.sync
                def _(sp):
                    for k in range(4):
                        sp.sem_inc(stored[k], 16)
                    sp.wait_ge(added, NT)
                    for k in range(2):
                        sp.dma_start(w_all[:, k, :].rearrange("p (r o) -> p r o", o=D),
                                     rel_w[:, k * P * D:(k + 1) * P * D].rearrange("r (i o) -> i r o", o=D)).then_inc(w_in, 16)
                    with sp.Fori(0, NT) as i:
                        for m in range(PARTS // 2):
                            sp.wait_ge(taken_by["dve" if m % 2 == 0 else "act"], i * (PARTS // 2) + (m // 2 * 2 + 2) + 2)
                            sp.dma_start(rel_table[ds(i * P, P), m * 1024:(m + 1) * 1024], stage[:, m % 4, :])\
                                .then_inc(stored[m % 4], 16)
                    for k in range(4):
                        sp.wait_ge(stored[k], 16 * NT * (PARTS // 8) + 16)

                def take(eng, copy, who, i, m):
                    eng.wait_ge(stored[m % 4], i * (16 * PARTS // 8) + (16 * (m // 4) + 16))
                    for s in range(2):
                        part = 2 * m + s
                        eng.wait_ge(multiplied, i * PARTS + part + 1)
                        copy(stage[:, m % 4, s * 512:(s + 1) * 512], psum[:, 4 + part % SLOTS, :]).then_inc(taken_by[who], 1)

                @block.vector
                def _(dve):
                    sums_to_state(dve, "mean", added, counted)
                    roots(dve, Chain(dve, order), to_root, rooted, 1)
                    dve.sem_inc(scales, 1)
                    dve.sem_inc(taken_by["dve"], 2)

                    def make(i, b, it, n):
                        dve.wait_ge(normed, i + 1)
                        dve.wait_ge(transposed, i + 1)
                        nc.vector.tensor_copy(operand[:, b, :], tile_of(state, i)).then_inc(made, 1)

                    def use(i, b, it, n):
                        for m in range(0, PARTS // 2, 2):
                            take(dve, nc.vector.tensor_copy, "dve", i, m)

                    pipelined(dve, make, use)

                @block.scalar
                def _(act):
                    root(act, to_root, rooted, 1)
                    act.wait_ge(scales, 1)
                    act.sem_inc(taken_by["act"], 2)
                    act.sem_inc(copied, 2)
                    with act.Fori(0, NT) as i:
                        nc.scalar.activation(tile_of(state, i), tile_of(state, i), ACT.Identity, bias=shift[:, ds(i, 1)],
                                             scale=rstd[:, ds(i, 1)]).then_inc(normed, 1)

                    def copy_turned(i, b, it, n):
                        act.wait_ge(transposed, i + 3)
                        act.wait_ge(tile_done, i + 1)
                        nc.scalar.copy(operandT[:, b, :], tp[:, b, :]).then_inc(copied, 1)

                    def use(i, b, it, n):
                        for m in range(1, PARTS // 2, 2):
                            take(act, nc.scalar.copy, "act", i, m)

                    pipelined(act, copy_turned, use)

                @block.tensor
                def _(pe):
                    pe.sem_inc(transposed, 2)
                    pe.sem_inc(tile_done, 2)
                    pe.wait_ge(w_in, 32)

                    def turn(i, b, it, n):
                        pe.wait_ge(made, i + 1)
                        pe.wait_ge(copied, i + 1)
                        for k in range(2):
                            ins = nc.tensor.transpose(tp[:, b, k * P:(k + 1) * P], operand[:, b, k * P:(k + 1) * P], ident[:, :])
                        ins.then_inc(transposed, 1)

                    def multiply(i, b, it, n):
                        pe.wait_ge(copied, i + 3)
                        for part in range(PARTS):
                            slot = part % SLOTS
                            who = "dve" if slot < 2 else "act"
                            pe.wait_ge(taken_by[who], i * (PARTS // 2) + (part // 4 * 2 + slot % 2 + 1))
                            for k in range(2):
                                ins = nc.tensor.matmul(psum[:, 4 + slot, :], operandT[:, b, k * P:(k + 1) * P],
                                                       w_all[:, k, part * 512:(part + 1) * 512], start=k == 0, stop=k == 1)
                            ins.then_inc(multiplied, 1)
                        pe.wait_ge(multiplied, i * PARTS + PARTS)
                        pe.sem_inc(tile_done, 1)

                    pipelined(pe, turn, multiply)

        aggregate(0, x, "s", idx_s)
        transform("sage0", "sage", w_sage[0][:, :, :], b_rep[0], rdeg_s)
        normalise_sage("nsage0", g_rep[0], beta_rep[0], False)
        aggregate(1, table[0], "s", idx_s)
        transform("sage1", "sage", w_sage[1][:, :, :], b_rep[1], rdeg_s)
        normalise_sage("nsage1", g_rep[1], beta_rep[1], True)
        aggregate(2, table[1], "d", idx_d)
        transform("gcn", "gcn", w_gcn[:, :, :])
        max_k()
        aggregate(3, table[2], "d", idx_d)
        relation_table()
        aggregate(4, rel_table.rearrange("n (r d) -> (n r) d", d=D), "d", idx_rel, weight)
        last_norm()


_INS = ["x", "src", "dst", "edge_type_32", "edge_weight1", "L0_gnn_W0", "L0_gnn_b0", "L0_gnn_g0", "L0_gnn_beta0",
        "L0_gnn_W1", "L0_gnn_b1", "L0_gnn_g1", "L0_gnn_beta1", "L1_gnn_W", "L2_gnn_W_self", "L2_gnn_W_neigh",
        "L3_gnn_bases", "L3_gnn_w_comp"]
_OUTS = [((NODES, D), "float32")]


def kernel(**inputs):
    import numpy as _np
    import concourse.bacc as _bacc
    from concourse import mybir as _mybir
    from concourse.bass_utils import run_bass_kernel_spmd as _run

    nc = _bacc.Bacc("TRN2", target_bir_lowering=False, num_devices=1)
    arrays, args = {}, []
    for name in _INS:
        a = _np.ascontiguousarray(inputs[name])
        arrays[f"in_{name}_dram"] = a
        args.append(nc.dram_tensor(f"in_{name}_dram", a.shape, _mybir.dt.from_np(a.dtype), kind="ExternalInput").ap())
    for i, (shape, dtype) in enumerate(_OUTS):
        dt = _mybir.dt.from_np(_np.dtype(dtype))
        args.append(nc.dram_tensor(f"out_{i}_dram", shape, dt, kind="ExternalOutput").ap())
    build(nc, *args)
    r = _run(nc, [arrays], core_ids=[0])
    got = tuple(r.results[0][f"out_{i}_dram"] for i in range(len(_OUTS)))
    return got[0]
```

```python
from contextlib import ExitStack

import concourse.bass as bass
from concourse import mybir
from concourse.alu_op_type import AluOpType as ALU

F32 = mybir.dt.float32
BF16 = mybir.dt.bfloat16
F32R = mybir.dt.float32r
I32 = mybir.dt.int32
I16 = mybir.dt.int16
ACT = mybir.ActivationFunctionType
AX = mybir.AxisListType

P = 128
NODES, D, EDGES = 6250, 256, 100000
RELS, BASES = 32, 8
EPS = 1e-5
TILES = -(-NODES // P)
NT = TILES + 1
LAST_ROWS = NODES - (TILES - 1) * P
LANES = 16
COLS = -(-EDGES // P // LANES) * LANES
FULL = EDGES // COLS
REST = EDGES - FULL * COLS
PAD_KEY = TILES * P
ROWS = COLS
GROUP = 4
PAIRS = -(-(ROWS + TILES - 1) // 64) * 64
GROUPS = PAIRS // GROUP
PAIR_COLS = -(-PAIRS // P)
RING = 8
OH_RING = 4
CREDIT = RING


class Chain:

    def __init__(self, eng, sem):
        self.eng, self.sem, self.base, self.n = eng, sem, 0, 0

    def __call__(self, ins):
        self.n += 1
        ins.then_inc(self.sem, 1)
        self.eng.wait_ge(self.sem, self.base + self.n)

    def total(self, n):
        self.base, self.n = n, 0


def build(nc, x, src, dst, edge_type_32, edge_weight1, L0_gnn_W0, L0_gnn_b0, L0_gnn_g0, L0_gnn_beta0,
          L0_gnn_W1, L0_gnn_b1, L0_gnn_g1, L0_gnn_beta1, L1_gnn_W, L2_gnn_W_self, L2_gnn_W_neigh,
          L3_gnn_bases, L3_gnn_w_comp, out):
    ctx = ExitStack()
    ds = bass.ds
    with ctx:
        def sb(name, shape, dt=F32):
            return ctx.enter_context(nc.sbuf_tensor(name, shape, dt))

        def dram(name, shape, dt=F32):
            return nc.dram_tensor(name, shape, dt, kind="Internal").ap()

        rec_dram = {"s": dram("rec_s", [P * COLS, 2]), "d": dram("rec_d", [P * COLS, 4])}
        table = [dram(f"table{i}", [NT * P, D]) for i in range(3)]
        rel_table = dram("rel_table", [NT * P, RELS * D])
        rel_w = dram("rel_w", [RELS, D * D])

        state = sb("state", [P, NT * D])
        onehot = sb("onehot", [P, OH_RING * GROUP, P])
        ident = sb("ident", [P, P])
        ones = sb("ones", [P, P])
        before = sb("before", [P, P])
        iota_p = sb("iota_p", [P, P])
        iota_bf = sb("iota_bf", [P, P], BF16)
        npf = PAIR_COLS * P
        loc = {"s": sb("loc_s", [P, npf]), "d": sb("loc_d", [P, npf])}
        off = {"s": sb("off_s", [P, npf], I32), "d": sb("off_d", [P, npf], I32)}
        idx_s = sb("idx_s", [P, npf], I32)
        idx_d = sb("idx_d", [P, npf], I32)
        idx_rel = sb("idx_rel", [P, npf], I32)
        weight = sb("weight", [P, npf])
        idx_ring = sb("idx_ring", [P, 4 * LANES], I32)
        w_space = sb("w_space", [P, 16 * D])
        raw = w_space[:, :].rearrange("p (h n) -> p h n", h=2)
        w_sage = [w_space[:, 2 * i * D:2 * (i + 1) * D].rearrange("p (k d) -> p k d", k=2) for i in range(2)]
        w_gcn = w_space[:, 4 * D:6 * D].rearrange("p (k d) -> p k d", k=2)
        w_maxk = w_space[:, 6 * D:10 * D].rearrange("p (k d) -> p k d", k=2)
        rows6 = w_space[:, 10 * D:16 * D].rearrange("p (r d) -> p r d", d=D)
        b_rep = [rows6[:, 0, :], rows6[:, 3, :]]
        g_rep = [rows6[:, 1, :], rows6[:, 4, :]]
        beta_rep = [rows6[:, 2, :], rows6[:, 5, :]]
        rdeg_s = sb("rdeg_s", [P, NT])
        rdeg_d = sb("rdeg_d", [P, NT])
        dis = sb("dis", [P, NT])
        stats = sb("stats", [P, NT, 6])
        mean = sb("mean", [P, NT])
        rstd = sb("rstd", [P, NT])
        shift = sb("shift", [P, NT])
        rstd_dis = sb("rstd_dis", [P, NT])
        shift_dis = sb("shift_dis", [P, NT])
        top8 = sb("top8", [P, 2, 8])
        operand = sb("operand", [P, 2, D])
        operandT = sb("operandT", [P, 2, D])
        psum = ctx.enter_context(nc.psum_tensor("psum", [P, 8, 512], F32))

        tot = {k: sb(f"tot_{k}", [P, NT]) for k in "sd"}
        ends = {k: sb(f"ends_{k}", [P, NT]) for k in "sd"}
        starts = {k: sb(f"starts_{k}", [P, NT]) for k in "sd"}
        moved = sb("moved", [P, 1])
        moved_i = sb("moved_i", [P, 1], I32)
        small = sb("small", [P, 8, NT])
        small_i = sb("small_i", [P, 2, NT], I32)
        iota_t = sb("iota_t", [P, NT])
        pair_no = small[:, 7, 0:PAIR_COLS]
        pair_tile = {"s": small[:, 5, 0:PAIR_COLS], "d": small[:, 6, 0:PAIR_COLS]}
        row_i = {k: sb(f"row_{k}", [P, PAIR_COLS], I32) for k in "sd"}
        row_f = sb("row_f", [P, PAIR_COLS])

        comp_t = sb("comp_t", [BASES, RELS])
        t_hi, t_lo = sb("t_hi", [P, 2, D], F32R), sb("t_lo", [P, 2, D], F32R)

        work_ctx = ctx.enter_context(ExitStack())
        ring0 = NT * D

        def place_work(name):
            work = work_ctx.enter_context(nc.sbuf_tensor(name, [P, NT * D + RING * GROUP * D], F32))
            return work, work[:, 0:NT * D], work[:, ring0:ring0 + RING * GROUP * D].rearrange("p (s d) -> p s d", d=D)

        work, sums, gathered = place_work("work")

        taken = {"state": 0, "work": 0}

        def carve(where, n, dt=F32):
            a = (state if where == "state" else work)[:, taken[where]:taken[where] + n]
            taken[where] += n
            assert taken[where] <= NT * D
            return a if dt == F32 else a.bitcast(dt)

        src_i, dst_i, rel_i = (carve("state", COLS, I32) for _ in range(3))
        w_in = carve("state", COLS)
        zeros = carve("state", COLS)
        rec = {"s": carve("state", 2 * COLS).rearrange("p (t f) -> p t f", f=2),
               "d": carve("state", 4 * COLS).rearrange("p (t f) -> p t f", f=4)}
        pos_i = {"s": carve("state", COLS, I32), "d": carve("state", COLS, I32)}
        tile_i, low_i = carve("work", COLS, I32), carve("work", COLS, I32)
        key_f, edge_no = carve("work", COLS), carve("work", COLS)
        tile_f = {"s": carve("work", COLS), "d": carve("work", COLS)}
        low_f = {"s": carve("work", COLS), "d": carve("work", COLS)}
        rank, pos_f = [carve("work", COLS), carve("work", COLS)], carve("work", COLS)
        mask = [carve("work", COLS // 2, I16), carve("work", COLS // 2, I16)]
        tile_wide = carve("state", 2 * PAIR_COLS * P).rearrange("p (c j) -> p c j", j=P)
        tile_bf = carve("work", COLS // 2, BF16)
        counts = carve("work", NT)
        rank0 = carve("work", NT)
        pos_ring = carve("work", LANES, I32)
        rec_ring = carve("work", LANES * 4)
        low_hot = carve("work", 2 * 4 * P // 2, BF16).rearrange("p (h c j) -> p h c j", h=2, c=4)
        tile_hot = carve("work", 2 * 4 * NT // 2, BF16).rearrange("p (h c j) -> p h c j", h=2, c=4)
        base_ring = work[:, ring0:ring0 + 4096].rearrange("p (h n) -> p h n", h=2)
        relw_ring = work[:, ring0 + 4096:ring0 + 8192].rearrange("p (h n) -> p h n", h=2)
        w_raw = onehot[:, 0:8, :].rearrange("p s j -> p (s j)").rearrange("p (w k d) -> p w k d", w=2, k=2)
        keys = {"s": src_i, "d": dst_i}
        REC = {"s": 2, "d": 4}

        cum_off, cum_tot = psum[:, 0, 0:NT], psum[:, 0, 64:64 + NT]
        deg_ps = {"d": psum[:, 1, 0:NT], "s": psum[:, 2, 0:NT]}

        passed_dve, passed_pe, passed_pool = (
            ctx.enter_context(nc.semaphore(n)) for n in ("passed_dve", "passed_pe", "passed_pool"))
        landed = [ctx.enter_context(nc.semaphore(f"landed{g}")) for g in range(RING)]
        idx_filled, hot_ready, multiplied_sums, added_sums, zeroed = (
            ctx.enter_context(nc.semaphore(n)) for n in ("idx_filled", "hot_ready", "multiplied_sums", "added_sums", "zeroed"))

        def sort_positions(dve, o, side, counted, cum):
            o(nc.vector.tensor_copy(key_f, keys[side]))
            o(nc.vector.tensor_scalar(tile_i, keys[side], 7, None, ALU.arith_shift_right))
            o(nc.vector.tensor_scalar(low_i, keys[side], P - 1, None, ALU.bitwise_and))
            o(nc.vector.tensor_copy(tile_f[side], tile_i))
            o(nc.vector.tensor_copy(low_f[side], low_i))
            o(nc.vector.tensor_copy(tile_bf, tile_i))
            done = o.n + o.base
            with dve.Fori(0, NT // 2) as it:
                for b in range(2):
                    dve.wait_ge(o.sem, it * 2 + (done + b - 1))
                    nc.vector.tensor_scalar(mask[b], tile_f[side], iota_t[:, ds(it * 2 + b, 1)], 0.0, ALU.is_equal, ALU.add,
                                            accum_out=counts[:, ds(it * 2 + b, 1)]).then_inc(o.sem, 1)
            o.total(done + NT)
            dve.wait_ge(o.sem, done + NT)
            dve.sem_inc(counted, 1)
            dve.wait_ge(cum, 1)
            o(nc.vector.tensor_copy(tot[side][:, :], cum_tot))
            o(nc.vector.tensor_tensor_scan(ends[side][:, :], tot[side][:, :], zeros[:, 0:NT], 0.0, ALU.add, ALU.add))
            o(nc.vector.tensor_tensor(starts[side][:, :], ends[side][:, :], tot[side][:, :], ALU.subtract))
            o(nc.vector.scalar_tensor_tensor(rank0, cum_off, -1.0, starts[side][:, :], ALU.add, ALU.add))
            done = o.n + o.base
            with dve.Fori(0, NT // 2) as it:
                at = it * 6 + done
                for b in range(2):
                    dve.wait_ge(o.sem, at + (b - 1))
                    nc.vector.tensor_scalar(mask[b], tile_bf, iota_t[:, ds(it * 2 + b, 1)], None,
                                            ALU.is_equal).then_inc(o.sem, 1)
                for b in range(2):
                    dve.wait_ge(o.sem, at + (b + 1))
                    nc.vector.tensor_tensor_scan(rank[b], mask[b], zeros, rank0[:, ds(it * 2 + b, 1)], ALU.add,
                                                 ALU.add).then_inc(o.sem, 1)
                for b in range(2):
                    dve.wait_ge(o.sem, at + (2 * b + 3))
                    dve.sem_inc(passed_dve, 1)
                    nc.vector.copy_predicated(pos_f, mask[b], rank[b]).then_inc(o.sem, 1)
            o.total(done + 3 * NT)
            dve.wait_ge(o.sem, done + 3 * NT)
            o(nc.vector.tensor_copy(pos_i[side], pos_f))
            o(nc.vector.tensor_copy(rec[side][:, :, 0], key_f))

        def pair_table(o, side):
            n_b = TILES
            first_row, last_row, pair_end, to_row, step = (small[:, k, 0:n_b] for k in range(5))
            pairs, ended, steps = last_row, first_row, last_row
            o(nc.vector.tensor_copy(small_i[:, 0, 0:n_b], starts[side][:, 0:n_b]))
            o(nc.vector.tensor_scalar(small_i[:, 0, 0:n_b], small_i[:, 0, 0:n_b], 7, None, ALU.arith_shift_right))
            o(nc.vector.tensor_copy(first_row, small_i[:, 0, 0:n_b]))
            o(nc.vector.tensor_scalar(last_row, ends[side][:, 0:n_b], -1.0, None, ALU.add))
            o(nc.vector.tensor_copy(small_i[:, 0, 0:n_b], last_row))
            o(nc.vector.tensor_scalar(small_i[:, 0, 0:n_b], small_i[:, 0, 0:n_b], 7, None, ALU.arith_shift_right))
            o(nc.vector.tensor_copy(last_row, small_i[:, 0, 0:n_b]))
            o(nc.vector.tensor_tensor(pairs, last_row, first_row, ALU.subtract))
            o(nc.vector.tensor_scalar(step, tot[side][:, 0:n_b], 0.0, None, ALU.is_gt))
            o(nc.vector.scalar_tensor_tensor(pairs, pairs, 1.0, step, ALU.add, ALU.mult))
            o(nc.vector.tensor_tensor_scan(pair_end, pairs, zeros[:, 0:n_b], 0.0, ALU.add, ALU.add))
            o(nc.vector.tensor_tensor(to_row, first_row, pair_end, ALU.subtract))
            o(nc.vector.tensor_tensor(to_row, to_row, pairs, ALU.add))
            o(nc.vector.tensor_tensor(step[:, 0:n_b - 1], to_row[:, 1:n_b], to_row[:, 0:n_b - 1], ALU.subtract))
            o(nc.vector.tensor_scalar(step[:, n_b - 1:n_b], to_row[:, n_b - 1:n_b], -1.0, None, ALU.mult))
            for col in range(PAIR_COLS):
                o(nc.vector.tensor_scalar(ended, pair_end, pair_no[:, col:col + 1], 0.0, ALU.is_le, ALU.add,
                                          accum_out=pair_tile[side][:, col:col + 1]))
                o(nc.vector.tensor_tensor(steps, ended, step, ALU.mult))
                o(nc.vector.tensor_reduce(row_f[:, col:col + 1], steps, AX.X, ALU.add))
            o(nc.vector.tensor_scalar(row_f[:, :], row_f[:, :], to_row[:, 0:1], None, ALU.add))
            o(nc.vector.tensor_tensor(row_f[:, :], row_f[:, :], pair_no, ALU.add))
            o(nc.vector.tensor_scalar(row_f[:, :], row_f[:, :], float(ROWS - 1), 0.0, ALU.min, ALU.max))
            o(nc.vector.tensor_copy(row_i[side][:, :], row_f[:, :]))
            for col in range(PAIR_COLS):
                u = col + (0 if side == "d" else PAIR_COLS)
                o(nc.vector.tensor_copy(tile_wide[:, u, :], pair_tile[side][:, col:col + 1].to_broadcast([P, P])))

        def scatter(pool, side, ring_sem, done_sems):
            f = REC[side]
            half = LANES // 2
            def turn(it, first):
                for h in range(2):
                    if not first:
                        pool.wait_ge(done_sems[h], it * (16 * half))
                    nc.gpsimd.tensor_copy(pos_ring[:, h * half:(h + 1) * half],
                                          pos_i[side][:, ds(it * LANES + h * half, half)]).then_inc(ring_sem, 1)
                    nc.gpsimd.tensor_copy(rec_ring[:, h * half * f:(h + 1) * half * f],
                                          rec[side].rearrange("p t f -> p (t f)")[:, ds((it * LANES + h * half) * f, half * f)])\
                        .then_inc(ring_sem, 1)
                    pool.wait_ge(ring_sem, it * 4 + 2 * h + 2)
                    pool.sem_inc(passed_pool, 1)
                    for k in range(h * half, (h + 1) * half):
                        pool.indirect_dma_start(
                            rec_dram[side], bass.IndirectOffsetOnAxis(pos_ring[:, k:k + 1], 0),
                            rec_ring[:, k * f:(k + 1) * f], None).then_inc(done_sems[h], 16)

            turn(0, True)
            with pool.Fori(1, COLS // LANES) as it:
                turn(it, False)
            for h in range(2):
                pool.wait_ge(done_sems[h], 16 * half * (COLS // LANES))

        with ExitStack() as c:
            sem = nc.alloc_semaphore
            padded, edges_in, dst_in, consts, order, counted, cum, stt = (
                sem(n) for n in ("padded", "edges_in", "dst_in", "consts", "order", "counted", "cum", "affine"))
            w_in_sem, wt_done, wt_copied, w_here = sem("weights_in"), sem("w_transposed"), sem("w_copied"), sem("weights_here")
            block = c.enter_context(nc.Block())

            @block.sync
            def _(sp):
                sp.wait_ge(padded, 4)
                def load(dst_ap, flat, s):
                    sp.dma_start(dst_ap[0:FULL, :], flat[0:FULL * COLS].rearrange("(p t) -> p t", t=COLS)).then_inc(s, 16)
                    sp.dma_start(dst_ap[FULL:FULL + 1, 0:REST], flat[FULL * COLS:EDGES].rearrange("(p t) -> p t", p=1)).then_inc(s, 16)
                load(src_i, src, edges_in)
                load(dst_i, dst, edges_in)
                load(rel_i, edge_type_32, dst_in)
                load(w_in, edge_weight1.rearrange("e o -> (e o)"), dst_in)

            @block.scalar
            def _(act):
                for i, w in enumerate((L0_gnn_W0, L0_gnn_W1)):
                    act.dma_start(w_raw[:, i, :, :], w.rearrange("(k p) d -> p k d", p=P)).then_inc(w_in_sem, 16)
                for w, to in ((L1_gnn_W, w_gcn[:, :, :]), (L2_gnn_W_self, w_maxk[:, :, 0:D]), (L2_gnn_W_neigh, w_maxk[:, :, D:2 * D])):
                    act.dma_start(to, w.rearrange("(k p) d -> p k d", p=P)).then_inc(w_in_sem, 16)
                for i, row in enumerate((L0_gnn_b0, L0_gnn_g0, L0_gnn_beta0, L0_gnn_b1, L0_gnn_g1, L0_gnn_beta1)):
                    act.dma_start(rows6[:, i, :], row.rearrange("(o d) -> o d", o=1).to_broadcast([P, D])).then_inc(w_in_sem, 16)
                with nc.allow_non_contiguous_dma(reason="a table of 1 KB, once"):
                    act.dma_start(comp_t[:, :], L3_gnn_w_comp.rearrange("r b -> b r")).then_inc(w_in_sem, 16)
                act.wait_ge(w_in_sem, 16 * 12)
                act.sem_inc(w_here, 1)
                for i in range(2):
                    act.wait_ge(wt_done, i + 1)
                    nc.scalar.copy(w_sage[i][:, :, :].rearrange("p k d -> p (k d)"), psum[:, 4 + i, :]).then_inc(wt_copied, 1)

            @block.gpsimd
            def _(pool):
                nc.gpsimd.memset(src_i, PAD_KEY).then_inc(padded, 1)
                nc.gpsimd.memset(dst_i, PAD_KEY).then_inc(padded, 1)
                nc.gpsimd.memset(rel_i, 0).then_inc(padded, 1)
                nc.gpsimd.memset(w_in, 0.0).then_inc(padded, 1)
                nc.gpsimd.iota(iota_t[:, :], [[1, NT]], base=0, channel_multiplier=0,
                               allow_small_or_imprecise_dtypes=True).then_inc(consts, 1)
                nc.gpsimd.iota(iota_p[:, :], [[1, P]], base=0, channel_multiplier=0,
                               allow_small_or_imprecise_dtypes=True).then_inc(consts, 1)
                nc.gpsimd.iota(iota_bf[:, :], [[1, P]], base=0, channel_multiplier=0,
                               allow_small_or_imprecise_dtypes=True).then_inc(consts, 1)
                nc.gpsimd.iota(edge_no, [[1, COLS]], base=0, channel_multiplier=COLS,
                               allow_small_or_imprecise_dtypes=True).then_inc(consts, 1)
                nc.gpsimd.iota(pair_no, [[P, PAIR_COLS]], base=0, channel_multiplier=1,
                               allow_small_or_imprecise_dtypes=True).then_inc(consts, 1)
                nc.gpsimd.memset(zeros, 0.0).then_inc(consts, 1)
                nc.gpsimd.memset(ones[:, :], 1.0).then_inc(consts, 1)
                nc.gpsimd.memset(ident[:, :], 0.0).then_inc(stt, 1)
                nc.gpsimd.memset(before[:, :], 1.0).then_inc(stt, 1)
                pool.wait_ge(stt, 2)
                nc.gpsimd.affine_select(out=ident[:, :], in_=ident[:, :], compare_op=ALU.not_equal, fill=1.0, base=0,
                                        pattern=[[-1, P]], channel_multiplier=1).then_inc(consts, 1)
                nc.gpsimd.affine_select(out=before[:, :], in_=before[:, :], compare_op=ALU.is_gt, fill=0.0, base=0,
                                        pattern=[[1, P]], channel_multiplier=-1).then_inc(consts, 1)

            @block.tensor
            def _(pe):
                pe.wait_ge(consts, 9)
                pe.wait_ge(w_in_sem, 16 * 12)
                for i in range(2):
                    for ki in range(2):
                        for ko in range(2):
                            ins = nc.tensor.transpose(psum[:, 4 + i, ki * D + ko * P:ki * D + (ko + 1) * P],
                                                      w_raw[:, i, ko, ki * P:(ki + 1) * P], ident[:, :])
                    ins.then_inc(wt_done, 1)
                pe.wait_ge(counted, 1)
                nc.tensor.matmul(cum_off, before[:, :], counts, start=True, stop=True)
                nc.tensor.matmul(cum_tot, ones[:, :], counts, start=True, stop=True).then_inc(cum, 1)

            @block.vector
            def _(dve):
                o = Chain(dve, order)
                dve.wait_ge(consts, 9)
                dve.wait_ge(edges_in, 64)
                sort_positions(dve, o, "s", counted, cum)
                o(nc.vector.tensor_copy(rec["s"][:, :, 1], dst_i))
                dve.wait_ge(w_here, 1)
                for k in range(2):
                    diagonal = w_maxk[:, k, k * P:(k + 1) * P]
                    o(nc.vector.tensor_tensor(diagonal, diagonal, ident[:, :], ALU.add))
                dve.wait_ge(dst_in, 64)
                dve.wait_ge(wt_copied, 2)

        with ExitStack() as c:
            sem = nc.alloc_semaphore
            order, counted, cum, hot, deg_done, rec_ready, rec_out = (
                sem(n) for n in ("order2", "counted2", "cum2", "hot", "deg_done", "rec_ready", "rec_out"))
            ring_sem = sem("ring_filled")
            scattered = [sem("scattered0"), sem("scattered1")]
            base_in = [sem("base_in0"), sem("base_in1")]
            relw_out = [sem("relw_out0"), sem("relw_out1")]
            relw_mm, relw_cp, rooted, degs = sem("relw_mm"), sem("relw_cp"), sem("rooted"), sem("degrees")
            flag_mm = sem("flag_mm")
            block = c.enter_context(nc.Block())
            CH = 2048
            N_CH = D * D // CH
            HALVES = COLS // 4
            bases_flat = L3_gnn_bases.rearrange("b i o -> b (i o)")

            @block.gpsimd
            def _(pool):
                scatter(pool, "s", ring_sem, scattered)

            @block.sync
            def _(sp):
                with sp.Fori(0, N_CH // 2) as it:
                    for h in range(2):
                        sp.wait_ge(relw_mm, (it * 2 + h) * 4 + 4)
                        sp.dma_start(base_ring[0:BASES, h, :], bases_flat[:, ds((it * 2 + h) * CH, CH)]).then_inc(base_in[h], 16)
                sp.wait_ge(rec_ready, 1)
                sp.dma_start(rec_dram["d"].rearrange("(p t) f -> p (t f)", p=P), rec["d"].rearrange("p t f -> p (t f)")).then_inc(rec_out, 16)
                sp.wait_ge(rec_out, 16)

            @block.scalar
            def _(act):
                act.sem_inc(relw_cp, 4)
                for h in range(2):
                    act.sem_inc(relw_out[h], 16)
                with act.Fori(0, N_CH // 2) as it:
                    for h in range(2):
                        act.wait_ge(relw_out[h], it * 16 + 16)
                        for q in range(4):
                            act.wait_ge(relw_mm, (it * 2 + h) * 4 + q + 9)
                            nc.scalar.copy(relw_ring[0:RELS, h, q * 512:(q + 1) * 512], psum[0:RELS, 4 + q, :]).then_inc(relw_cp, 1)
                        act.wait_ge(relw_cp, (it * 2 + h) * 4 + 8)
                        act.dma_start(rel_w[:, ds((it * 2 + h) * CH, CH)], relw_ring[0:RELS, h, :]).then_inc(relw_out[h], 16)
                for h in range(2):
                    act.wait_ge(relw_out[h], 16 * (N_CH // 2) + 16)
                act.wait_ge(degs, 1)
                nc.scalar.activation(dis[:, :], small[:, 0, :], ACT.Sqrt).then_inc(rooted, 1)

            @block.tensor
            def _(pe):
                pe.sem_inc(relw_mm, 8)
                pe.wait_ge(counted, 1)
                nc.tensor.matmul(cum_off, before[:, :], counts, start=True, stop=True)
                nc.tensor.matmul(cum_tot, ones[:, :], counts, start=True, stop=True).then_inc(cum, 1)
                with pe.Fori(0, N_CH // 2) as it:
                    for h in range(2):
                        pe.wait_ge(base_in[h], it * 16 + 16)
                        for q in range(4):
                            pe.wait_ge(relw_cp, (it * 2 + h) * 4 + q + 1)
                            pe.sem_inc(passed_pe, 1)
                            nc.tensor.matmul(psum[0:RELS, 4 + q, :], comp_t[:, :], base_ring[0:BASES, h, q * 512:(q + 1) * 512],
                                             start=True, stop=True).then_inc(relw_mm, 1)
                pe.sem_inc(deg_done, 2)

                def count_half(side, n, h, first, last, base):
                    pe.wait_ge(hot, 2 * (base + n + 1))
                    for col in range(4):
                        ins = nc.tensor.matmul(deg_ps[side], low_hot[:, h, col, :], tile_hot[:, h, col, :],
                                               start=first and col == 0, stop=last and col == 3)
                    ins.then_inc(deg_done, 1)

                for s, side in enumerate("ds"):
                    for h in range(2):
                        count_half(side, h, h, h == 0, False, s * HALVES)
                    with pe.Fori(1, HALVES // 2 - 1) as it:
                        for h in range(2):
                            count_half(side, it * 2 + h, h, False, False, s * HALVES)
                    for h in range(2):
                        count_half(side, HALVES - 2 + h, h, False, h == 1, s * HALVES)
                nc.tensor.matmul(psum[:, 3, 0:1], ones[:, :], moved[:, :], start=True, stop=True).then_inc(flag_mm, 1)

            @block.vector
            def _(dve):
                o = Chain(dve, order)
                sort_positions(dve, o, "d", counted, cum)
                o(nc.vector.tensor_copy(rec["d"][:, :, 1], src_i))
                o(nc.vector.scalar_tensor_tensor(rec["d"][:, :, 2], rec["d"][:, :, 1], float(RELS), rel_i, ALU.mult, ALU.add))
                o(nc.vector.tensor_copy(rec["d"][:, :, 3], w_in))
                o(nc.vector.tensor_tensor(rank[0], pos_f, edge_no, ALU.not_equal))
                o(nc.vector.tensor_reduce(moved[:, :], rank[0], AX.X, ALU.add))
                dve.sem_inc(rec_ready, 1)
                for s, side in enumerate("ds"):
                    with dve.Fori(0, HALVES // 2) as it:
                        for h in range(2):
                            col = it * 8 + h * 4
                            dve.wait_ge(deg_done, it * 2 + (s * HALVES + h + 1))
                            nc.vector.tensor_tensor(
                                low_hot[:, h, :, :], low_f[side][:, ds(col, 4)].unsqueeze(2).to_broadcast([P, 4, P]),
                                iota_bf[:, :].unsqueeze(1).to_broadcast([P, 4, P]), ALU.is_equal).then_inc(hot, 1)
                            nc.vector.tensor_tensor(
                                tile_hot[:, h, :, :], tile_f[side][:, ds(col, 4)].unsqueeze(2).to_broadcast([P, 4, NT]),
                                iota_t[:, :].unsqueeze(1).to_broadcast([P, 4, NT]), ALU.is_equal).then_inc(hot, 1)
                dve.wait_ge(deg_done, 2 * HALVES + 2)
                o(nc.vector.tensor_scalar(small[:, 0, :], deg_ps["d"], 1.0, None, ALU.max))
                dve.sem_inc(degs, 1)
                o(nc.vector.tensor_scalar(small[:, 1, :], deg_ps["d"], 0.0, None, ALU.is_gt))
                o(nc.vector.tensor_scalar(small[:, 2, :], deg_ps["s"], 1.0, None, ALU.max))
                o(nc.vector.reciprocal(rdeg_d[:, :], small[:, 0, :]))
                o(nc.vector.reciprocal(rdeg_s[:, :], small[:, 2, :]))
                dve.wait_ge(rooted, 1)
                o(nc.vector.reciprocal(small[:, 3, :], dis[:, :]))
                o(nc.vector.tensor_tensor(dis[:, :], small[:, 3, :], small[:, 1, :], ALU.mult))
                dve.wait_ge(flag_mm, 1)
                o(nc.vector.tensor_copy(moved_i[:, :], psum[:, 3, 0:1]))
                for side in "ds":
                    pair_table(o, side)

        with ExitStack() as c:
            sem = nc.alloc_semaphore
            order, ordered = sem("order3"), sem("ordered")
            ring_sem = sem("ring_filled3")
            scattered = [sem("scattered30"), sem("scattered31")]
            rows_in = [sem("rows_in0"), sem("rows_in1")]
            tp, cp = sem("fields_transposed"), sem("fields_copied")
            block = c.enter_context(nc.Block())
            PC = PAIR_COLS
            rows_buf = work[:, ring0:ring0 + 2 * 512].rearrange("p (h n) -> p h n", h=2)
            tile_row = work[:, ring0 + 1024:ring0 + 1024 + PC * P]
            units = [(side, col) for side in "ds" for col in range(PC)]

            @block.gpsimd
            def _(pool):
                n_moved = pool.value_load(moved_i[0:1, 0:1], min_val=0, max_val=P * COLS)
                with pool.If(n_moved > 0):
                    scatter(pool, "d", ring_sem, scattered)
                pool.sem_inc(ordered, 1)
                for u, (side, col) in enumerate(units):
                    f = REC[side]
                    if u >= 2:
                        pool.wait_ge(tp, u - 1)
                    pool.indirect_dma_start(rows_buf[:, u % 2, 0:P * f], None,
                                            rec_dram[side].rearrange("(r j) f -> r (j f)", j=P),
                                            bass.IndirectOffsetOnAxis(row_i[side][:, col:col + 1], 0)).then_inc(rows_in[u % 2], 16)

            @block.tensor
            def _(pe):
                for u, (side, col) in enumerate(units):
                    f = REC[side]
                    pe.wait_ge(rows_in[u % 2], 16 * (u // 2 + 1))
                    if u >= 2:
                        pe.wait_ge(cp, u - 1)
                    rows = rows_buf[:, u % 2, 0:P * f].rearrange("p (j f) -> p j f", f=f)
                    for k in range(f):
                        nc.tensor.transpose(psum[:, 2 + 2 * (u % 2), k * P:(k + 1) * P], rows[:, :, k], ident[:, :])
                    nc.tensor.matmul(psum[:, 3 + 2 * (u % 2), 0:P], tile_wide[:, u, :], ident[:, :],
                                     start=True, stop=True).then_inc(tp, 1)

            @block.vector
            def _(dve):
                o = Chain(dve, order)
                for u, (side, col) in enumerate(units):
                    here = slice(col * P, (col + 1) * P)
                    tile_ps = psum[:, 3 + 2 * (u % 2), 0:P]
                    field = lambda k: psum[:, 2 + 2 * (u % 2), k * P:(k + 1) * P]
                    dve.wait_ge(tp, u + 1)
                    o(nc.vector.tensor_copy(tile_row[:, here], tile_ps))
                    nc.vector.scalar_tensor_tensor(loc[side][:, here], tile_row[:, here], -float(P), field(0), ALU.mult, ALU.add)
                    nc.vector.tensor_scalar(off[side][:, here], tile_row[:, here], float(D), None, ALU.mult)
                    if side == "s":
                        ins = nc.vector.tensor_scalar(idx_s[:, here], field(1), float(NODES - 1), None, ALU.min)
                    else:
                        nc.vector.tensor_scalar(idx_d[:, here], field(1), float(NODES - 1), None, ALU.min)
                        nc.vector.tensor_copy(idx_rel[:, here], field(2))
                        ins = nc.vector.tensor_copy(weight[:, here], field(3))
                    ins.then_inc(cp, 1)
                o(nc.vector.memset(state[:, (TILES - 1) * D:], 0.0))

        def tile_of(buf, i, n=1):
            return buf[:, ds(i * D, n * D)]

        def rows_of(buf):
            return buf.rearrange("p (t d) -> p t d", d=D)

        x_loaded, hot_unweighted = nc.alloc_semaphore("x_loaded"), nc.alloc_semaphore("hot_unweighted")

        def aggregate(turn, rows_dram, side, idx, w=None):
            q0 = turn * GROUPS
            first = turn == 0
            products = psum[:, :, :].rearrange("p b (s d) -> p (b s) d", d=D)
            with nc.Block() as block:
                @block.sync
                def _(sp):
                    if first:
                        sp.dma_start(rows_of(state[:, 0:(TILES - 1) * D]),
                                     x[0:(TILES - 1) * P, :].rearrange("(t p) d -> p t d", p=P)).then_inc(x_loaded, 16)
                        sp.dma_start(state[0:LAST_ROWS, (TILES - 1) * D:TILES * D], x[(TILES - 1) * P:NODES, :]).then_inc(x_loaded, 16)
                        sp.wait_ge(x_loaded, 32)

                @block.scalar
                def _(act):
                    if w is None:
                        return
                    with act.Fori(0, GROUPS // OH_RING) as it:
                        for g in range(OH_RING):
                            act.wait_ge(hot_unweighted, it * OH_RING + (g + 1))
                            for k in range(GROUP):
                                hot = onehot[:, g * GROUP + k, :]
                                ins = nc.scalar.activation(hot, hot, ACT.Copy,
                                                           scale=w[:, ds(it * (OH_RING * GROUP) + (g * GROUP + k), 1)])
                            ins.then_inc(hot_ready, 1)

                @block.gpsimd
                def _(pool):
                    with pool.Fori(0, PAIRS // (4 * LANES)) as it:
                        for h in range(4):
                            nc.gpsimd.tensor_copy(idx_ring[:, h * LANES:(h + 1) * LANES],
                                                  idx[:, ds(it * (4 * LANES) + h * LANES, LANES)]).then_inc(idx_filled, 1)
                            pool.wait_ge(idx_filled, it * 4 + (turn * PAIRS // LANES + h + 1))
                            for g in range(h * LANES // GROUP, (h + 1) * LANES // GROUP):
                                pool.wait_ge(multiplied_sums, it * (4 * LANES // GROUP) + (q0 + g + 1))
                                pool.sem_inc(passed_pool, 1)
                                for k in range(GROUP):
                                    slot = g % RING * GROUP + k
                                    lane = g * GROUP + k
                                    pool.indirect_dma_start(gathered[:, slot, :], None, rows_dram,
                                                            bass.IndirectOffsetOnAxis(idx_ring[:, lane:lane + 1], 0))\
                                        .then_inc(landed[g % RING], 16)

                @block.tensor
                def _(pe):
                    if first:
                        pe.sem_inc(multiplied_sums, CREDIT)
                    with pe.Fori(0, GROUPS // RING) as it:
                        for g in range(RING):
                            pe.wait_ge(landed[g], it * (16 * GROUP) + 16 * GROUP * (q0 // RING + 1))
                            pe.wait_ge(hot_ready, it * RING + (q0 + g + 1))
                            pe.wait_ge(added_sums, it * (RING * GROUP) + (q0 + g + 1) * GROUP)
                            for k in range(GROUP):
                                slot = g % OH_RING * GROUP + k
                                ins = nc.tensor.matmul(products[:, slot, :], onehot[:, slot, :],
                                                       gathered[:, g * GROUP + k, :], start=True, stop=True)
                            ins.then_inc(multiplied_sums, 1)

                @block.vector
                def _(dve):
                    nc.vector.memset(sums, 0.0).then_inc(zeroed, 1)
                    dve.wait_ge(zeroed, turn + 1)
                    if first:
                        dve.sem_inc(added_sums, OH_RING * GROUP)

                    def make_onehot(q, g):
                        hot = onehot[:, g * GROUP:(g + 1) * GROUP, :]
                        dve.wait_ge(multiplied_sums, q + (q0 + 1 + CREDIT - OH_RING))
                        nc.vector.tensor_tensor(
                            hot, loc[side][:, ds(q * GROUP, GROUP)].unsqueeze(2).to_broadcast([P, GROUP, P]),
                            iota_p[:, :].unsqueeze(1).to_broadcast([P, GROUP, P]), ALU.is_equal)\
                            .then_inc(hot_ready if w is None else hot_unweighted, 1)

                    def add_products(q, g):
                        _, at = nc.values_load_multi_w_load_instructions(
                            off[side][0:1, ds(q * GROUP, GROUP)], engines=[mybir.EngineType.DVE],
                            min_val=0, max_val=(NT - 1) * D)
                        dve.wait_ge(multiplied_sums, q + (q0 + 1 + CREDIT))
                        for k in range(GROUP):
                            dve.wait_ge(added_sums, q * GROUP + (q0 * GROUP + k + OH_RING * GROUP))
                            tile = sums[:, ds(at[k], D)]
                            nc.vector.tensor_tensor(tile, tile, products[:, g * GROUP + k, :], ALU.add).then_inc(added_sums, 1)

                    make_onehot(0, 0)
                    with dve.Fori(0, GROUPS // OH_RING - 1) as it:
                        for g in range(OH_RING):
                            make_onehot(it * OH_RING + g + 1, (g + 1) % OH_RING)
                            add_products(it * OH_RING + g, g)
                    for g in range(OH_RING):
                        if g < OH_RING - 1:
                            make_onehot(GROUPS - OH_RING + g + 1, g + 1)
                        add_products(GROUPS - OH_RING + g, g)
                    dve.wait_ge(added_sums, (q0 + GROUPS + OH_RING) * GROUP)

        CHUNK = 5
        N_CHUNKS = NT // CHUNK

        def pipelined(eng, first, second):
            first(0, 0, None, 0)
            with eng.Fori(0, NT // 2 - 1) as it:
                first(it * 2 + 1, 1, it, 0)
                second(it * 2, 0, it, 0)
                first(it * 2 + 2, 0, it, 1)
                second(it * 2 + 1, 1, it, 1)
            first(NT - 1, 1, None, 1)
            second(NT - 2, 0, NT // 2 - 1, 0)
            second(NT - 1, 1, NT // 2 - 1, 1)

        ROOTS_STEPS = 9

        def roots(dve, o, to_root, rooted, base, with_dis=False):
            even_mean, even_m2, odd_mean, odd_m2 = (stats[:, :, k] for k in (1, 2, 4, 5))
            apart, spread, both = small[:, 0, :], small[:, 1, :], small[:, 2, :]
            o(nc.vector.tensor_tensor(apart, even_mean, odd_mean, ALU.subtract))
            o(nc.vector.tensor_tensor(both, even_mean, odd_mean, ALU.add))
            o(nc.vector.tensor_scalar(mean[:, :], both, 0.5, None, ALU.mult))
            o(nc.vector.scalar_tensor_tensor(spread, apart, 0.25, apart, ALU.mult, ALU.mult))
            o(nc.vector.tensor_tensor(both, even_m2, odd_m2, ALU.add))
            o(nc.vector.scalar_tensor_tensor(spread, both, 1.0 / D, spread, ALU.mult, ALU.add))
            o(nc.vector.tensor_scalar(rstd[:, :], spread, EPS, None, ALU.add))
            dve.sem_inc(to_root, 1)
            dve.wait_ge(rooted, base)
            o(nc.vector.reciprocal(rstd[:, :], rstd[:, :]))
            o(nc.vector.scalar_tensor_tensor(shift[:, :], mean[:, :], -1.0, rstd[:, :], ALU.mult, ALU.mult))
            if with_dis:
                o(nc.vector.tensor_tensor(rstd_dis[:, :], rstd[:, :], dis[:, :], ALU.mult))
                o(nc.vector.tensor_tensor(shift_dis[:, :], shift[:, :], dis[:, :], ALU.mult))

        def root(act, to_root, rooted, base):
            act.wait_ge(to_root, base)
            nc.scalar.activation(rstd[:, :], rstd[:, :], ACT.Sqrt).then_inc(rooted, 1)

        def sums_to_state(dve, kind, added, counted):
            with dve.Fori(0, N_CHUNKS) as it:
                for k in range(CHUNK):
                    i = it * CHUNK + k
                    if kind == "mean":
                        ins = nc.vector.scalar_tensor_tensor(tile_of(state, i), tile_of(sums, i), rdeg_d[:, ds(i, 1)],
                                                             tile_of(state, i), ALU.mult, ALU.add)
                    else:
                        ins = nc.vector.scalar_tensor_tensor(tile_of(state, i), tile_of(sums, i), 0.0,
                                                             tile_of(state, i), ALU.max, ALU.add)
                    ins.then_inc(added, 1)
                for k in range(CHUNK):
                    i = it * CHUNK + k
                    dve.wait_ge(added, i + 1)
                    dve.sem_inc(passed_dve, 1)
                    nc.vector.bn_stats(stats[:, ds(i, 1), :].rearrange("p t m -> p (t m)"), tile_of(state, i)).then_inc(counted, 1)
            dve.wait_ge(counted, NT)

        def transform(name, kind, weights, bias=None, rdeg=None):
            sem = lambda n: nc.alloc_semaphore(f"{n}_{name}")
            made, transposed, copied, multiplied, used, counted = (
                sem(n) for n in ("made", "transposed", "copied", "multiplied", "used", "counted"))
            tp = psum[:, 0:2, 0:D]
            result = sums if kind == "sage" else state
            BUFS, AHEAD = 4, 3
            operands = gathered[:, 0:BUFS, :]
            with nc.Block() as block:
                @block.vector
                def _(dve):
                    dve.sem_inc(used, 2)

                    def make(i, b):
                        dve.wait_ge(transposed, i + 1)
                        if kind == "sage":
                            nc.vector.scalar_tensor_tensor(operands[:, b, :], tile_of(sums, i), rdeg[:, ds(i, 1)],
                                                           tile_of(state, i), ALU.mult, ALU.add).then_inc(made, 1)
                        else:
                            nc.vector.tensor_scalar(operands[:, b, :], tile_of(sums, i), dis[:, ds(i, 1)],
                                                    None, ALU.mult).then_inc(made, 1)

                    def use(i, b):
                        dve.wait_ge(multiplied, i + 3)
                        nc.vector.tensor_tensor(tile_of(result, i), psum[:, 2 + b, 0:D],
                                                tile_of(state, i) if kind == "gcn" else bias, ALU.add).then_inc(used, 1)

                    def count(i):
                        dve.wait_ge(used, i + 3)
                        dve.sem_inc(passed_dve, 1)
                        nc.vector.bn_stats(stats[:, ds(i, 1), :].rearrange("p t m -> p (t m)"), tile_of(result, i)).then_inc(counted, 1)

                    for i in range(AHEAD):
                        make(i, i)
                    make(AHEAD, AHEAD)
                    use(0, 0)
                    turns = (NT - AHEAD - 1) // BUFS
                    with dve.Fori(0, turns) as it:
                        for u in range(1, BUFS + 1):
                            make(it * BUFS + (u + AHEAD), (u + AHEAD) % BUFS)
                            use(it * BUFS + u, u % 2)
                            count(it * BUFS + (u - 1))
                    for i in range(turns * BUFS + 1, NT):
                        if i + AHEAD < NT:
                            make(i + AHEAD, (i + AHEAD) % BUFS)
                        use(i, i % 2)
                        count(i - 1)
                    count(NT - 1)
                    dve.wait_ge(counted, NT)

                @block.scalar
                def _(act):
                    act.sem_inc(copied, 2)
                    with act.Fori(0, NT // 2) as it:
                        for b in range(2):
                            i = it * 2 + b
                            act.wait_ge(transposed, i + (BUFS + 1))
                            act.wait_ge(multiplied, i + 1)
                            nc.scalar.copy(operandT[:, b, :], tp[:, b, :]).then_inc(copied, 1)

                @block.tensor
                def _(pe):
                    pe.sem_inc(transposed, BUFS)
                    pe.sem_inc(multiplied, 2)

                    def turn(i, b):
                        pe.wait_ge(made, i + 1)
                        pe.wait_ge(copied, i + 1)
                        for k in range(2):
                            ins = nc.tensor.transpose(tp[:, b % 2, k * P:(k + 1) * P], operands[:, b, k * P:(k + 1) * P], ident[:, :])
                        ins.then_inc(transposed, 1)

                    def multiply(i, b):
                        pe.wait_ge(copied, i + 3)
                        pe.wait_ge(used, i + 1)
                        for k in range(2):
                            ins = nc.tensor.matmul(psum[:, 2 + b, 0:D], operandT[:, b, k * P:(k + 1) * P],
                                                   weights[:, k, :], start=k == 0, stop=k == 1)
                        ins.then_inc(multiplied, 1)

                    turn(0, 0)
                    turns = (NT - 1) // BUFS
                    with pe.Fori(0, turns) as it:
                        for u in range(BUFS):
                            turn(it * BUFS + (u + 1), (u + 1) % BUFS)
                            multiply(it * BUFS + u, u % 2)
                    for i in range(turns * BUFS, NT):
                        if i + 1 < NT:
                            turn(i + 1, (i + 1) % BUFS)
                        multiply(i, i % 2)

        def max_k():
            sem = lambda n: nc.alloc_semaphore(f"{n}_maxk")
            order, to_root, rooted, scales, made, transposed, copied, multiplied, added, dense_in, sparse_ready = (
                sem(n) for n in ("order", "to_root", "rooted", "scales", "made", "transposed", "copied", "multiplied",
                                 "added", "dense_in", "sparse_ready"))
            stored, kept_marked = [sem(f"stored{s}") for s in range(4)], sem("kept_marked")
            tp = psum[:, 0:2, 0:D]
            normed, turned, dense, sparse, left = (gathered[:, s:s + 4, :] for s in (0, 4, 8, 12, 16))
            LOWEST = -3.4028235e38
            COUPLES = NT // 2
            steps = 4 * 2 * 2

            def couples(eng, first, second):
                first(0, 0)
                with eng.Fori(0, COUPLES // 2) as it:
                    first(it * 2 + 1, 1)
                    second(it * 2, 0)
                    first(it * 2 + 2, 0)
                    second(it * 2 + 1, 1)
                second(COUPLES - 1, 0)

            with nc.Block() as block:
                @block.gpsimd
                def _(pool):
                    pool.sem_inc(sparse_ready, 4)

                    def keep_largest(c, h):
                        for b in range(2):
                            pool.wait_ge(stored[2 * h + b], c * 8 + (16 - 8 * h))
                            pool.wait_ge(order, c * steps + (ROOTS_STEPS + steps - 1 + b))
                            kept = left[:, 2 * h + b, :]
                            pool.sem_inc(passed_pool, 1)
                            nc.gpsimd.tensor_scalar(kept, kept, LOWEST, None, ALU.is_equal).then_inc(kept_marked, 1)
                            pool.wait_ge(kept_marked, c * 2 + (b + 1))
                            nc.gpsimd.tensor_tensor(sparse[:, 2 * h + b, :], kept, dense[:, 2 * h + b, :],
                                                    ALU.mult).then_inc(sparse_ready, 1)

                    with pool.Fori(0, COUPLES // 2) as it:
                        for h in range(2):
                            keep_largest(it * 2 + h, h)
                    keep_largest(COUPLES - 1, 0)

                @block.vector
                def _(dve):
                    o = Chain(dve, order)
                    roots(dve, o, to_root, rooted, 1)
                    assert o.n == ROOTS_STEPS
                    dve.sem_inc(scales, 1)
                    done = ROOTS_STEPS

                    def largest(c, h):
                        at = c * steps + done
                        n = 0
                        for r in range(4):
                            for b in range(2):
                                if r == 0:
                                    dve.wait_ge(dense_in, c * 2 + (b + 3))
                                    dve.wait_ge(order, at + (b - 1))
                                else:
                                    dve.wait_ge(order, at + (n - 1))
                                dve.sem_inc(passed_dve, 1)
                                nc.vector.max(top8[:, b, :], dense[:, 2 * h + b, :] if r == 0 else left[:, 2 * h + b, :]).then_inc(order, 1)
                                n += 1
                            for b in range(2):
                                if r == 0:
                                    dve.wait_ge(sparse_ready, c * 2 + (b + 1))
                                dve.wait_ge(order, at + (n - 1))
                                dve.sem_inc(passed_dve, 1)
                                nc.vector.match_replace(left[:, 2 * h + b, :], top8[:, b, :],
                                                        dense[:, 2 * h + b, :] if r == 0 else left[:, 2 * h + b, :],
                                                        LOWEST).then_inc(order, 1)
                                n += 1

                    with dve.Fori(0, COUPLES // 2) as it:
                        for h in range(2):
                            largest(it * 2 + h, h)
                    largest(COUPLES - 1, 0)

                @block.scalar
                def _(act):
                    root(act, to_root, rooted, 1)
                    act.sem_inc(copied, 2)
                    act.sem_inc(dense_in, 2)
                    act.sem_inc(added, 2)
                    act.wait_ge(scales, 1)

                    def norm(c, h):
                        for b in range(2):
                            i = c * 2 + b
                            act.wait_ge(transposed, i + 1)
                            nc.scalar.activation(normed[:, 2 * h + b, :], tile_of(state, i), ACT.Identity,
                                                 bias=shift[:, ds(i, 1)], scale=rstd[:, ds(i, 1)]).then_inc(made, 1)

                    def copy_turned(c, h):
                        for b in range(2):
                            i = c * 2 + b
                            act.wait_ge(transposed, i + 5)
                            act.wait_ge(multiplied, i + 1)
                            nc.scalar.copy(turned[:, 2 * h + b, :], tp[:, b, :]).then_inc(copied, 1)

                    def products_out(c, h):
                        for b in range(2):
                            i = c * 2 + b
                            act.wait_ge(multiplied, i + 5)
                            act.wait_ge(sparse_ready, i + 1)
                            nc.scalar.copy(dense[:, 2 * h + b, :], psum[:, 4 + b, 0:D]).then_inc(dense_in, 1)
                            nc.scalar.copy(tile_of(state, i), psum[:, 2 + b, 0:D]).then_inc(added, 1)

                    norm(0, 0)
                    norm(1, 1)
                    copy_turned(0, 0)
                    turns = (COUPLES - 2) // 2
                    with act.Fori(0, turns) as it:
                        for h in range(2):
                            norm(it * 2 + (h + 2), h)
                            copy_turned(it * 2 + (h + 1), 1 - h)
                            products_out(it * 2 + h, h)
                    for c in range(2 * turns, COUPLES):
                        if c + 2 < COUPLES:
                            norm(c + 2, c % 2)
                        if c + 1 < COUPLES:
                            copy_turned(c + 1, (c + 1) % 2)
                        products_out(c, c % 2)

                @block.tensor
                def _(pe):
                    pe.sem_inc(multiplied, 4)
                    pe.sem_inc(transposed, 4)

                    def turn(c, h):
                        for b in range(2):
                            i = c * 2 + b
                            pe.wait_ge(made, i + 1)
                            pe.wait_ge(copied, i + 1)
                            for k in range(2):
                                ins = nc.tensor.transpose(tp[:, b, k * P:(k + 1) * P], normed[:, 2 * h + b, k * P:(k + 1) * P],
                                                          ident[:, :])
                            ins.then_inc(transposed, 1)

                    def multiply(c, h):
                        for b in range(2):
                            i = c * 2 + b
                            pe.wait_ge(copied, i + 3)
                            pe.wait_ge(added, i + 1)
                            pe.wait_ge(dense_in, i + 1)
                            for half in range(2):
                                for k in range(2):
                                    ins = nc.tensor.matmul(psum[:, 2 + 2 * half + b, 0:D], turned[:, 2 * h + b, k * P:(k + 1) * P],
                                                           w_maxk[:, k, half * D:(half + 1) * D], start=k == 0, stop=k == 1)
                            ins.then_inc(multiplied, 1)

                    couples(pe, turn, multiply)

                @block.sync
                def _(sp):
                    for s in range(4):
                        sp.sem_inc(stored[s], 16)

                    def store(c, h):
                        for b in range(2):
                            i = c * 2 + b
                            sp.wait_ge(sparse_ready, i + 5)
                            sp.dma_start(table[2][ds(i * P, P), :], sparse[:, 2 * h + b, :]).then_inc(stored[2 * h + b], 16)

                    with sp.Fori(0, COUPLES // 2) as it:
                        for h in range(2):
                            store(it * 2 + h, h)
                    store(COUPLES - 1, 0)
                    for s in range(4):
                        sp.wait_ge(stored[s], 16 * (COUPLES // 2 + 1 - s // 2) + 16)

        def chunk_of(buf, c, n=CHUNK):
            return buf[:, ds(c * CHUNK * D, n * D)]

        def table_chunk(t, c):
            return t[ds(c * (CHUNK * P), CHUNK * P), :].rearrange("(t p) d -> p t d", p=P)

        def normalise_sage(name, g, beta, last):
            sem = lambda n: nc.alloc_semaphore(f"{n}_{name}")
            order, to_root, rooted, normed, lit, stored, affine = (
                sem(n) for n in ("order", "to_root", "rooted", "normed", "lit", "stored", "affine"))
            if last:
                scaled, x_in, x_used, counted = sem("scaled"), [sem("x_in0"), sem("x_in1")], sem("x_used"), sem("counted")
            x_buf = work[:, ring0:ring0 + 2 * CHUNK * D].rearrange("p (b n) -> p b n", b=2)
            with nc.Block() as block:
                @block.gpsimd
                def _(pool):
                    if not last:
                        return
                    pool.sem_inc(x_used, 2)

                    def add_x(c, b):
                        pool.wait_ge(lit, c + 1)
                        nc.gpsimd.tensor_tensor(chunk_of(state, c), chunk_of(sums, c), x_buf[:, b, :], ALU.add).then_inc(x_used, 1)

                    with pool.Fori(0, N_CHUNKS // 2 - 1) as it:
                        for b in range(2):
                            pool.wait_ge(x_in[b], it * 16 + 16)
                            add_x(it * 2 + b, b)
                    pool.wait_ge(x_in[0], 16 * (N_CHUNKS // 2))
                    add_x(N_CHUNKS - 2, 0)
                    pool.wait_ge(x_in[1], 16 * (N_CHUNKS // 2 + 1))
                    add_x(N_CHUNKS - 1, 1)

                @block.scalar
                def _(act):
                    root(act, to_root, rooted, 1)

                    def light(c):
                        act.wait_ge(affine, c * CHUNK + CHUNK)
                        nc.scalar.activation(chunk_of(sums if last else state, c), chunk_of(sums, c), ACT.Silu).then_inc(lit, 1)

                    with act.Fori(0, N_CHUNKS) as c:
                        light(c)
                    if last:
                        root(act, to_root, rooted, 2)
                        with act.Fori(0, N_CHUNKS) as c:
                            act.wait_ge(scaled, c * CHUNK + CHUNK)
                            for k in range(CHUNK):
                                i = c * CHUNK + k
                                nc.scalar.activation(tile_of(state, i), tile_of(state, i), ACT.Identity, bias=shift[:, ds(i, 1)],
                                                     scale=rstd[:, ds(i, 1)])

                @block.vector
                def _(dve):
                    o = Chain(dve, order)
                    roots(dve, o, to_root, rooted, 1)

                    def norm_and_affine(c):
                        for k in range(CHUNK):
                            i = c * CHUNK + k
                            nc.vector.scalar_tensor_tensor(tile_of(sums, i), tile_of(sums, i), mean[:, ds(i, 1)], g,
                                                           ALU.subtract, ALU.mult).then_inc(normed, 1)
                        for k in range(CHUNK):
                            i = c * CHUNK + k
                            dve.wait_ge(normed, i + 1)
                            nc.vector.scalar_tensor_tensor(tile_of(sums, i), tile_of(sums, i), rstd[:, ds(i, 1)], beta,
                                                           ALU.mult, ALU.add).then_inc(affine, 1)

                    if not last:
                        with dve.Fori(0, N_CHUNKS) as c:
                            norm_and_affine(c)
                        return

                    def count(c):
                        dve.wait_ge(x_used, c + 3)
                        for k in range(CHUNK):
                            i = c * CHUNK + k
                            dve.sem_inc(passed_dve, 1)
                            nc.vector.bn_stats(stats[:, ds(i, 1), :].rearrange("p t m -> p (t m)"), tile_of(state, i)).then_inc(counted, 1)

                    for c in range(2):
                        norm_and_affine(c)
                    with dve.Fori(0, N_CHUNKS - 2) as c:
                        norm_and_affine(c + 2)
                        count(c)
                    for c in range(N_CHUNKS - 2, N_CHUNKS):
                        count(c)
                    dve.wait_ge(counted, NT)
                    roots(dve, o, to_root, rooted, 2, with_dis=True)
                    with dve.Fori(0, N_CHUNKS) as c:
                        for k in range(CHUNK):
                            i = c * CHUNK + k
                            nc.vector.tensor_scalar(tile_of(sums, i), tile_of(state, i), rstd_dis[:, ds(i, 1)],
                                                    shift_dis[:, ds(i, 1)], ALU.mult, ALU.add).then_inc(scaled, 1)

                @block.sync
                def _(sp):
                    if last:
                        with sp.Fori(0, N_CHUNKS // 2 - 1) as it:
                            for b in range(2):
                                sp.wait_ge(x_used, it * 2 + b + 1)
                                sp.dma_start(rows_of(x_buf[:, b, :]), table_chunk(x, it * 2 + b)).then_inc(x_in[b], 16)
                        sp.wait_ge(x_used, N_CHUNKS - 1)
                        sp.dma_start(rows_of(x_buf[:, 0, :]), table_chunk(x, N_CHUNKS - 2)).then_inc(x_in[0], 16)
                        sp.wait_ge(x_used, N_CHUNKS)
                        at = (N_CHUNKS - 1) * CHUNK
                        sp.dma_start(rows_of(x_buf[:, 1, 0:(TILES - 1 - at) * D]),
                                     x[at * P:(TILES - 1) * P, :].rearrange("(t p) d -> p t d", p=P)).then_inc(x_in[1], 16)
                        sp.dma_start(x_buf[0:LAST_ROWS, 1, (TILES - 1 - at) * D:(TILES - at) * D],
                                     x[(TILES - 1) * P:NODES, :]).then_inc(x_in[1], 16)
                    with sp.Fori(0, N_CHUNKS) as it:
                        if last:
                            sp.wait_ge(scaled, it * CHUNK + CHUNK)
                        else:
                            sp.wait_ge(lit, it + 1)
                        sp.dma_start(table_chunk(table[1 if last else 0], it),
                                     rows_of(chunk_of(sums if last else state, it))).then_inc(stored, 16)
                    sp.wait_ge(stored, 16 * N_CHUNKS)

        def last_norm():
            sem = lambda n: nc.alloc_semaphore(f"{n}_last")
            order, to_root, rooted, added, counted, normed, stored = (
                sem(n) for n in ("order", "to_root", "rooted", "added", "counted", "normed", "stored"))
            with nc.Block() as block:
                @block.scalar
                def _(act):
                    root(act, to_root, rooted, 1)

                @block.vector
                def _(dve):
                    sums_to_state(dve, "relu", added, counted)
                    roots(dve, Chain(dve, order), to_root, rooted, 1)
                    with dve.Fori(0, N_CHUNKS) as c:
                        for k in range(CHUNK):
                            i = c * CHUNK + k
                            nc.vector.tensor_scalar(tile_of(state, i), tile_of(state, i), rstd[:, ds(i, 1)],
                                                    shift[:, ds(i, 1)], ALU.mult, ALU.add).then_inc(normed, 1)

                @block.sync
                def _(sp):
                    n = (TILES - 1) // 4
                    with sp.Fori(0, n) as it:
                        sp.wait_ge(normed, it * 4 + 4)
                        sp.dma_start(out[ds(it * (4 * P), 4 * P), :].rearrange("(t p) d -> p t d", p=P),
                                     rows_of(state[:, ds(it * (4 * D), 4 * D)])).then_inc(stored, 16)
                    sp.wait_ge(normed, TILES)
                    sp.dma_start(out[4 * n * P:NODES, :], state[0:LAST_ROWS, 4 * n * D:(4 * n + 1) * D]).then_inc(stored, 16)
                    sp.wait_ge(stored, 16 * (n + 1))

        def relation_table():
            sem = lambda n: nc.alloc_semaphore(f"{n}_rel")
            split_step, made, transposed, masked, halved, weights_split, multiplied, order, to_root, rooted, added, counted, normed = (
                sem(n) for n in ("split_step", "made", "transposed", "masked", "halved", "weights_split", "multiplied", "order",
                                 "to_root", "rooted", "added", "counted", "normed"))
            taken_by = {"dve": sem("taken_dve"), "act": sem("taken_act")}
            stored = [sem(f"stored{k}") for k in range(4)]
            ROUNDS = 2
            ROUND_RELS = RELS // ROUNDS
            COLS_R = ROUND_RELS * D
            PARTS = COLS_R // 512
            SLOTS = 4
            PIECES = 4
            PIECE = 2 * COLS_R // PIECES
            w_in = [sem(f"w_in{j}") for j in range(2)]

            def load_piece(sp, r, j):
                k, rel0 = j // (PIECES // 2), r * ROUND_RELS + j % (PIECES // 2) * (PIECE // D)
                sp.dma_start(raw[:, j % 2, :].rearrange("p (r o) -> p r o", o=D),
                             rel_w[rel0:rel0 + PIECE // D, k * P * D:(k + 1) * P * D]
                             .rearrange("r (i o) -> i r o", o=D)).then_inc(w_in[j % 2], 16)

            with nc.Block() as block:
                @block.sync
                def _(sp):
                    for j in range(2):
                        load_piece(sp, 0, j)
                        sp.wait_ge(w_in[j], 16)

                @block.vector
                def _(dve):
                    sums_to_state(dve, "mean", added, counted)
                    roots(dve, Chain(dve, order), to_root, rooted, 1)

                @block.scalar
                def _(act):
                    root(act, to_root, rooted, 1)

            work_ctx.close()
            w_hi, w_lo = (work_ctx.enter_context(nc.sbuf_tensor(n, [P, 2 * COLS_R], F32R)) for n in ("w_hi", "w_lo"))
            stage = work_ctx.enter_context(nc.sbuf_tensor("stage", [P, 4, 1024], F32))
            w_masked = onehot[:, :, :].rearrange("p s j -> p (s j)")
            tp = psum[:, 0:2, 0:D]
            t_masked = operandT
            MASK = -4096

            with nc.Block() as block:
                @block.sync
                def _(sp):
                    for k in range(4):
                        sp.sem_inc(stored[k], 16)
                    for r in range(ROUNDS):
                        for j in range(2, PIECES):
                            sp.wait_ge(weights_split, 2 * (r * PIECES + j - 1))
                            load_piece(sp, r, j)
                        if r + 1 < ROUNDS:
                            for j in range(2):
                                sp.wait_ge(weights_split, 2 * (r * PIECES + PIECES - 1 + j))
                                load_piece(sp, r + 1, j)
                        with sp.Fori(0, NT) as i:
                            for m in range(PARTS // 2):
                                sp.wait_ge(taken_by["dve" if m % 2 == 0 else "act"],
                                           i * (PARTS // 2) + (r * NT * (PARTS // 2) + m // 2 * 2 + 2 + 2))
                                sp.dma_start(rel_table[ds(i * P, P), r * COLS_R + m * 1024:r * COLS_R + (m + 1) * 1024],
                                             stage[:, m % 4, :]).then_inc(stored[m % 4], 16)
                    for k in range(4):
                        sp.wait_ge(stored[k], 16 * NT * ROUNDS * (PARTS // 8) + 16)

                def take(eng, copy, who, r, i, m):
                    eng.wait_ge(stored[m % 4], i * (16 * PARTS // 8) + (16 * PARTS // 8 * r * NT + 16 * (m // 4) + 16))
                    for s in range(2):
                        part = 2 * m + s
                        eng.wait_ge(multiplied, i * PARTS + ((r * NT + 2) * PARTS + part + 1))
                        copy(stage[:, m % 4, s * 512:(s + 1) * 512], psum[:, 4 + part % SLOTS, :]).then_inc(taken_by[who], 1)

                @block.vector
                def _(dve):
                    o = Chain(dve, split_step)
                    dve.sem_inc(taken_by["dve"], 2)
                    dve.sem_inc(halved, 2)
                    for r in range(ROUNDS):
                        for j in range(PIECES):
                            here = slice(j * PIECE, (j + 1) * PIECE)
                            n = r * PIECES + j
                            dve.wait_ge(w_in[j % 2], 16 * (r * (PIECES // 2) + j // 2 + 1))
                            if n > 0:
                                dve.wait_ge(weights_split, 2 * n)
                            if r > 0 and j == 0:
                                dve.wait_ge(multiplied, (r * NT + 2) * PARTS)
                            o(nc.vector.tensor_scalar(w_masked.bitcast(I32), raw[:, j % 2, :].bitcast(I32), MASK, None, ALU.bitwise_and))
                            nc.vector.tensor_tensor(w_lo[:, here], raw[:, j % 2, :], w_masked, ALU.subtract).then_inc(weights_split, 1)

                        def make(i, b):
                            dve.wait_ge(normed, i + 1)
                            dve.wait_ge(transposed, i + (r * NT + 1))
                            nc.vector.tensor_copy(operand[:, b, :], tile_of(state, i)).then_inc(made, 1)

                        def halve(i, b):
                            dve.wait_ge(transposed, i + (r * NT + 3))
                            dve.wait_ge(multiplied, i * PARTS + (r * NT + 1) * PARTS)

                            nc.vector.tensor_scalar(t_masked[:, b, :].bitcast(I32), tp[:, b, :].bitcast(I32), MASK, None,
                                                    ALU.bitwise_and).then_inc(masked, 1)
                            dve.wait_ge(masked, i + (r * NT + 1))
                            nc.vector.tensor_copy(t_hi[:, b, :], t_masked[:, b, :])
                            nc.vector.tensor_tensor(t_lo[:, b, :], tp[:, b, :], t_masked[:, b, :], ALU.subtract).then_inc(halved, 1)

                        def products(i, b, halve_next=True, make_next=True):
                            take(dve, nc.vector.tensor_copy, "dve", r, i, 0)
                            if halve_next:
                                halve(i + 1, 1 - b)
                            take(dve, nc.vector.tensor_copy, "dve", r, i, 2)
                            if make_next:
                                make(i + 2, b)

                        make(0, 0)
                        make(1, 1)
                        halve(0, 0)
                        with dve.Fori(0, NT // 2 - 1) as it:
                            for b in range(2):
                                products(it * 2 + b, b)
                        products(NT - 2, 0, make_next=False)
                        products(NT - 1, 1, False, False)

                @block.scalar
                def _(act):
                    act.sem_inc(taken_by["act"], 2)

                    def norm(i):
                        nc.scalar.activation(tile_of(state, i), tile_of(state, i), ACT.Identity, bias=shift[:, ds(i, 1)],
                                             scale=rstd[:, ds(i, 1)]).then_inc(normed, 1)

                    def products(r, i):
                        for m in range(1, PARTS // 2, 2):
                            take(act, nc.scalar.copy, "act", r, i, m)

                    ahead = 4
                    for i in range(ahead):
                        norm(i)
                    for r in range(ROUNDS):
                        for j in range(PIECES):
                            here = slice(j * PIECE, (j + 1) * PIECE)
                            act.wait_ge(split_step, r * PIECES + j + 1)
                            nc.scalar.copy(w_hi[:, here], w_masked).then_inc(weights_split, 1)
                        with act.Fori(0, NT - ahead) as i:
                            if r == 0:
                                norm(i + ahead)
                            products(r, i)
                        for i in range(NT - ahead, NT):
                            products(r, i)

                @block.tensor
                def _(pe):
                    pe.sem_inc(transposed, 2)
                    pe.sem_inc(multiplied, 2 * PARTS)
                    for r in range(ROUNDS):
                        def turn(i, b, it, n):
                            pe.wait_ge(made, i + (r * NT + 1))
                            pe.wait_ge(halved, i + (r * NT + 1))
                            for k in range(2):
                                ins = nc.tensor.transpose(tp[:, b, k * P:(k + 1) * P], operand[:, b, k * P:(k + 1) * P], ident[:, :])
                            ins.then_inc(transposed, 1)

                        def multiply(i, b, it, n):
                            pe.wait_ge(halved, i + (r * NT + 3))
                            for part in range(PARTS):
                                slot = part % SLOTS
                                who = "dve" if slot < 2 else "act"
                                pe.wait_ge(taken_by[who], i * (PARTS // 2) + (r * NT * (PARTS // 2) + part // 4 * 2 + slot % 2 + 1))
                                terms = [(t, w, k) for k in range(2) for t, w in ((t_hi, w_hi), (t_hi, w_lo), (t_lo, w_hi))]
                                for n, (t, w, k) in enumerate(terms):
                                    ins = nc.tensor.matmul(psum[:, 4 + slot, :], t[:, b, k * P:(k + 1) * P],
                                                           w[:, k * COLS_R + part * 512:k * COLS_R + (part + 1) * 512],
                                                           start=n == 0, stop=n == len(terms) - 1)
                                ins.then_inc(multiplied, 1)

                        pe.wait_ge(weights_split, 2 * PIECES * (r + 1))
                        pipelined(pe, turn, multiply)

        aggregate(0, x, "s", idx_s)
        transform("sage0", "sage", w_sage[0][:, :, :], b_rep[0], rdeg_s)
        normalise_sage("nsage0", g_rep[0], beta_rep[0], False)
        aggregate(1, table[0], "s", idx_s)
        transform("sage1", "sage", w_sage[1][:, :, :], b_rep[1], rdeg_s)
        normalise_sage("nsage1", g_rep[1], beta_rep[1], True)
        aggregate(2, table[1], "d", idx_d)
        transform("gcn", "gcn", w_gcn[:, :, :])
        max_k()
        aggregate(3, table[2], "d", idx_d)
        relation_table()
        work_ctx.close()
        work, sums, gathered = place_work("work_again")
        aggregate(4, rel_table.rearrange("n (r d) -> (n r) d", d=D), "d", idx_rel, weight)
        last_norm()


_INS = ["x", "src", "dst", "edge_type_32", "edge_weight1", "L0_gnn_W0", "L0_gnn_b0", "L0_gnn_g0", "L0_gnn_beta0",
        "L0_gnn_W1", "L0_gnn_b1", "L0_gnn_g1", "L0_gnn_beta1", "L1_gnn_W", "L2_gnn_W_self", "L2_gnn_W_neigh",
        "L3_gnn_bases", "L3_gnn_w_comp"]
_OUTS = [((NODES, D), "float32")]


def kernel(**inputs):
    import numpy as _np
    import concourse.bacc as _bacc
    from concourse import mybir as _mybir
    from concourse.bass_utils import run_bass_kernel_spmd as _run

    nc = _bacc.Bacc("TRN2", target_bir_lowering=False, num_devices=1)
    arrays, args = {}, []
    for name in _INS:
        a = _np.ascontiguousarray(inputs[name])
        arrays[f"in_{name}_dram"] = a
        args.append(nc.dram_tensor(f"in_{name}_dram", a.shape, _mybir.dt.from_np(a.dtype), kind="ExternalInput").ap())
    for i, (shape, dtype) in enumerate(_OUTS):
        dt = _mybir.dt.from_np(_np.dtype(dtype))
        args.append(nc.dram_tensor(f"out_{i}_dram", shape, dt, kind="ExternalOutput").ap())
    build(nc, *args)
    r = _run(nc, [arrays], core_ids=[0])
    got = tuple(r.results[0][f"out_{i}_dram"] for i in range(len(_OUTS)))
    return got[0]
```
